# Optimizing a Trainium2 kernel written in Bass

```python
import numpy as np
import jax
import jax.numpy as jnp

def _softmax(x, axis=-1):
    return jax.nn.softmax(x, axis=axis)

def _gelu(x):
    return jax.nn.gelu(x, approximate=True)

def _silu(x):
    return jax.nn.silu(x)

def _sigmoid(x):
    return jax.nn.sigmoid(x)

def _layernorm(x, axis=-1, eps=1e-05):
    m = jnp.mean(x, axis=axis, keepdims=True)
    v = jnp.var(x, axis=axis, keepdims=True)
    return (x - m) / jnp.sqrt(v + eps)

def _scatter_add(tgt, idx, src, axis=0):
    return tgt.at[idx].add(src)

def _segment_sum(src, seg, n):
    return jax.ops.segment_sum(src, seg, n)
kernel_name = 'mk_gnn_ffn_d1_gnn_r8_146809'

def setup_inputs(seed: int=0):
    np.random.seed(seed)
    _w = jnp.asarray

    def _rec_inputs():
        import jax
        import jax.numpy as jnp
        _gk = jax.random.key(seed)
        x = -0.0002117 + 1 * jax.random.normal(jax.random.fold_in(_gk, 1), (6250, 256), jnp.float32)
        _s = jax.random.randint(jax.random.fold_in(_gk, 2), (50000,), 0, 6250, jnp.int32)
        _d = jax.random.randint(jax.random.fold_in(_gk, 3), (50000,), 0, 6250, jnp.int32)
        _loop = jnp.arange(6250, dtype=jnp.int32)
        src = jnp.concatenate([_s, _d, _loop])
        dst = jnp.concatenate([_d, _s, _loop])
        _o = jnp.argsort(dst, stable=True)
        src = src[_o]
        dst = dst[_o]
        return (x, src, dst)
    x, src, dst = _rec_inputs()

    def _L0_gnn_setup():
        import jax, jax.numpy as jnp
        import numpy as np
        N_NODES = 12500
        N_EDGES = 200000
        D_IN = 256
        HEADS = 8
        D_HEAD = 32
        NEG_SLOPE = 0.2
        BN_EPS = 1e-05
        key = jax.random.key(seed)
        ks = jax.random.split(key, 8)
        x = jax.random.normal(ks[0], (N_NODES, D_IN), dtype=jnp.float32)
        edge_index = jax.random.randint(ks[1], (2, N_EDGES), 0, N_NODES, dtype=jnp.int32)
        W = jax.random.normal(ks[2], (D_IN, HEADS * D_HEAD), dtype=jnp.float32) / np.sqrt(D_IN)
        att_src = jax.random.normal(ks[3], (HEADS, D_HEAD), dtype=jnp.float32) / np.sqrt(D_HEAD)
        att_dst = jax.random.normal(ks[4], (HEADS, D_HEAD), dtype=jnp.float32) / np.sqrt(D_HEAD)
        bias = jax.random.normal(ks[5], (HEADS * D_HEAD,), dtype=jnp.float32) * 0.01
        gamma = jnp.ones((HEADS * D_HEAD,), dtype=jnp.float32)
        beta = jnp.zeros((HEADS * D_HEAD,), dtype=jnp.float32)
        return {'x': x, 'edge_index': edge_index, 'W': W, 'att_src': att_src, 'att_dst': att_dst, 'bias': bias, 'gamma': gamma, 'beta': beta}
    _L0_gnn_all = _L0_gnn_setup()
    _L0_gnn_in = {k: v for k, v in _L0_gnn_all.items() if k in ('W', 'att_src', 'att_dst', 'bias', 'gamma', 'beta')}
    del _L0_gnn_all

    def _L0_ffn_setup():
        import jax, jax.numpy as jnp
        import numpy as np
        TOP_K = 2
        LN_EPS = 1e-05
        key = jax.random.key(seed)
        ks = jax.random.split(key, 8)
        B, S, D, E, H = (16, 1024, 256, 8, 1024)
        x = jax.random.normal(ks[0], (B, S, D), dtype=jnp.float32)
        Wr = jax.random.normal(ks[1], (D, E), dtype=jnp.float32) * 0.1
        br = jnp.zeros((E,), dtype=jnp.float32)
        ln_g = jnp.ones((E, D), dtype=jnp.float32)
        ln_b = jnp.zeros((E, D), dtype=jnp.float32)
        W1 = jax.random.normal(ks[2], (E, D, H), dtype=jnp.float32) * (1.0 / np.sqrt(D))
        b1 = jnp.zeros((E, H), dtype=jnp.float32)
        W2 = jax.random.normal(ks[3], (E, H, D), dtype=jnp.float32) * (1.0 / np.sqrt(H))
        b2 = jnp.zeros((E, D), dtype=jnp.float32)
        return {'x': x, 'Wr': Wr, 'br': br, 'ln_g': ln_g, 'ln_b': ln_b, 'W1': W1, 'b1': b1, 'W2': W2, 'b2': b2}
    _L0_ffn_all = _L0_ffn_setup()
    _L0_ffn_in = {k: v for k, v in _L0_ffn_all.items() if k in ('Wr', 'br', 'ln_g', 'ln_b', 'W1', 'b1', 'W2', 'b2')}
    del _L0_ffn_all
    return {'x': x, 'src': src, 'dst': dst, 'L0_gnn_W': _L0_gnn_in['W'], 'L0_gnn_att_src': _L0_gnn_in['att_src'], 'L0_gnn_att_dst': _L0_gnn_in['att_dst'], 'L0_gnn_bias': _L0_gnn_in['bias'], 'L0_gnn_gamma': _L0_gnn_in['gamma'], 'L0_gnn_beta': _L0_gnn_in['beta'], 'L0_ffn_Wr': _L0_ffn_in['Wr'], 'L0_ffn_br': _L0_ffn_in['br'], 'L0_ffn_ln_g': _L0_ffn_in['ln_g'], 'L0_ffn_ln_b': _L0_ffn_in['ln_b'], 'L0_ffn_W1': _L0_ffn_in['W1'], 'L0_ffn_b1': _L0_ffn_in['b1'], 'L0_ffn_W2': _L0_ffn_in['W2'], 'L0_ffn_b2': _L0_ffn_in['b2']}

def reference(x, src, dst, L0_gnn_W, L0_gnn_att_src, L0_gnn_att_dst, L0_gnn_bias, L0_gnn_gamma, L0_gnn_beta, L0_ffn_Wr, L0_ffn_br, L0_ffn_ln_g, L0_ffn_ln_b, L0_ffn_W1, L0_ffn_b1, L0_ffn_W2, L0_ffn_b2):
    import jax
    import jax.numpy as jnp

    def _L0_gnn_ref(x, edge_index, W, att_src, att_dst, bias, gamma, beta):
        import jax, jax.numpy as jnp
        import numpy as np
        N_NODES = 12500
        N_EDGES = 200000
        D_IN = 256
        HEADS = 8
        D_HEAD = 32
        NEG_SLOPE = 0.2
        BN_EPS = 1e-05
        N = x.shape[0]
        H, D = att_src.shape
        xh = (x @ W).reshape(N, H, D)
        a_src = jnp.einsum('nhd,hd->nh', xh, att_src)
        a_dst = jnp.einsum('nhd,hd->nh', xh, att_dst)
        loops = jnp.arange(N, dtype=edge_index.dtype)
        src = jnp.concatenate([edge_index[0], loops])
        dst = jnp.concatenate([edge_index[1], loops])
        e = jax.nn.leaky_relu(a_src[src] + a_dst[dst], NEG_SLOPE)
        m = jax.ops.segment_max(e, dst, num_segments=N)
        e = jnp.exp(e - m[dst])
        denom = jax.ops.segment_sum(e, dst, num_segments=N)
        alpha = e / denom[dst]
        msg = xh[src] * alpha[:, :, None]
        out = jax.ops.segment_sum(msg, dst, num_segments=N).reshape(N, H * D) + bias
        mean = jnp.mean(out, axis=0)
        var = jnp.var(out, axis=0)
        out = (out - mean) * jax.lax.rsqrt(var + BN_EPS) * gamma + beta
        return out + x

    def _L0_ffn_ref(x, Wr, br, ln_g, ln_b, W1, b1, W2, b2):
        import jax, jax.numpy as jnp
        import numpy as np
        TOP_K = 2
        LN_EPS = 1e-05
        B, S, D = x.shape
        N = B * S
        xt = x.reshape(N, D)
        logits = xt @ Wr + br
        probs = jax.nn.softmax(logits, axis=-1)
        top_p, top_idx = jax.lax.top_k(probs, TOP_K)
        weights = top_p / top_p.sum(axis=-1, keepdims=True)
        mu = xt.mean(axis=-1, keepdims=True)
        var = ((xt - mu) ** 2).mean(axis=-1, keepdims=True)
        xn = (xt - mu) * jax.lax.rsqrt(var + LN_EPS)
        xe = xn[None, :, :] * ln_g[:, None, :] + ln_b[:, None, :]
        h = jax.nn.gelu(jnp.einsum('end,edh->enh', xe, W1) + b1[:, None, :], approximate=False)
        y = jnp.einsum('enh,ehd->end', h, W2) + b2[:, None, :]
        y_tok = jnp.transpose(y, (1, 0, 2))
        sel = jnp.take_along_axis(y_tok, top_idx[:, :, None], axis=1)
        out = (weights[:, :, None] * sel).sum(axis=1)
        return out.reshape(B, S, D)
    edge_index = jnp.stack([src, dst])
    x = x + _L0_gnn_ref(_layernorm(x, axis=-1), edge_index, L0_gnn_W, L0_gnn_att_src, L0_gnn_att_dst, L0_gnn_bias, L0_gnn_gamma, L0_gnn_beta)
    x = x + _L0_ffn_ref(_layernorm(x, axis=-1)[None], L0_ffn_Wr, L0_ffn_br, L0_ffn_ln_g, L0_ffn_ln_b, L0_ffn_W1, L0_ffn_b1, L0_ffn_W2, L0_ffn_b2)[0]
    return x

_drawn_inputs = setup_inputs


def setup_inputs(seed=0):
    import zlib

    import numpy as np

    out = dict(_drawn_inputs(seed))
    spreads = {'L0_gnn_gamma': (1.0, 0.2),
     'L0_gnn_beta': (0.0, 0.1),
     'L0_ffn_br': (0.0, 0.1),
     'L0_ffn_ln_g': (1.0, 0.2),
     'L0_ffn_ln_b': (0.0, 0.343),
     'L0_ffn_b1': (0.0, 0.337),
     'L0_ffn_b2': (0.0, 0.1)}
    factors = {'L0_gnn_bias': 8.0}
    for name, (base, spread) in spreads.items():
        noise = np.random.default_rng([zlib.crc32(name.encode()), seed]).standard_normal(out[name].shape)
        drawn = base * np.exp(spread * noise) if base else spread * noise
        out[name] = jnp.asarray(drawn.astype(out[name].dtype))
    for name, factor in factors.items():
        out[name] = (out[name] * factor).astype(out[name].dtype)
    return out
```

```python
from contextlib import ExitStack

import numpy as np

import concourse.bass as bass
from concourse import mybir

ALU = mybir.AluOpType
ACT = mybir.ActivationFunctionType
AX = mybir.AxisListType
F32 = mybir.dt.float32
I32 = mybir.dt.int32
P = 128
NEG_SLOPE = 0.2
EPS = 1e-5
IN_RANGE = "the value is worked out on the chip within the shapes' bounds, whatever the data"


def ceil_div(a, b):
    return -(-a // b)


class Marker:

    def __init__(self, sem):
        self.sem, self.count = sem, 0

    def mark(self):
        return (self.sem, self.count)


class Stream(Marker):

    def __init__(self, sem):
        super().__init__(sem)
        self.steps = []

    def do(self, fn, after=()):
        self.count += 1
        self.steps.append((tuple(after), fn, self.sem, 1))
        return self.mark()

    def quiet(self, fn, after=()):
        self.steps.append((tuple(after), fn, None, 0))

    def dma(self, marker, fn, after=()):
        marker.count += 16
        self.steps.append((tuple(after), fn, marker.sem, 16))
        return marker.mark()

    def play(self, engine):
        passed = {}
        for after, fn, sem, step in self.steps:
            for item in after:
                waited, value = item() if callable(item) else item
                if passed.get(id(waited), 0) < value:
                    engine.wait_ge(waited, value)
                    passed[id(waited)] = value
            made = fn(engine)
            if sem is not None:
                made.then_inc(sem, step)


def build_gnn_moe(nc, x, src, dst, W, att_src, att_dst, bias, gamma, beta,
                  Wr, br, ln_g, ln_b, W1, b1, W2, b2, out):
    N, D = x.shape
    HEADS, DH = att_src.shape
    E = src.shape[0]
    NE, _, HID = W1.shape
    KD = D // P
    KH = HID // P
    HALF = HID // 2
    NT = ceil_div(N, P)
    LAST = N - (NT - 1) * P
    ET = ceil_div(E, P)
    SLOT_GROUPS = ceil_div(ET + NT, P)
    SLOTS_UP = SLOT_GROUPS * P
    EB = 8
    SLOTS = ceil_div(ET + NT - 1, EB) * EB
    BATCHES = SLOTS // EB
    assert ET + 1 <= SLOTS_UP and SLOTS <= SLOTS_UP and SLOTS - ET <= NT
    ROW = D + HEADS
    PICK = 2 * HEADS
    TOP = 2
    FT = (N * TOP - NE) // P + NE
    XROW = D + 2

    node_table = nc.dram_tensor("node_table", (N, ROW), F32, kind="Internal").ap()
    resid_rows = nc.dram_tensor("resid_rows", (NT * P, D), F32, kind="Internal").ap()
    src_pad = nc.dram_tensor("src_pad", (SLOTS_UP, P), I32, kind="Internal").ap()
    dst_pad = nc.dram_tensor("dst_pad", (SLOTS_UP, P), I32, kind="Internal").ap()
    expert_rows = nc.dram_tensor("expert_rows", (FT * P, XROW), F32, kind="Internal").ap()

    with ExitStack() as ctx:
        def sem(name):
            return ctx.enter_context(nc.semaphore(name))

        base = nc.sbuf_base + (-nc.sbuf_base) % 32

        class Region:
            def __init__(self, start):
                self.at = start

            def take(self, name, shape, dt=F32):
                t = nc.alloc_sbuf_tensor_at(name, list(shape), dt, offset=self.at)
                self.at += ceil_div(int(np.prod(shape[1:])) * 4, 32) * 32
                assert self.at <= nc.sbuf_usable_end, name
                return t

        small = Region(base)
        ident = small.take("ident", [P, P])
        iota_free = small.take("iota_free", [P, P])
        ones = small.take("ones", [P, P])
        part = small.take("part", [P, 1])
        eps = small.take("eps", [P, 1])
        expert_of_tile = small.take("expert_of_tile", [P, FT], I32)
        XR, HR = 5, 3
        xs = small.take("xs", [P, XR, XROW])
        xe = small.take("xe", [P, 2, D])
        xeT = small.take("xeT", [P, 2, KD, P])
        hid = small.take("hid", [P, HR, HALF])
        y = small.take("y", [P, 2, D])
        token_id = small.take("token_id", [P, XR], I32)

        region_acc = Region(small.at)
        acc = region_acc.take("acc", [P, NT + 1, ROW])
        region_vec = Region(small.at)
        b1_all = region_vec.take("b1_all", [P, NE, HID])
        b2_all = region_vec.take("b2_all", [P, NE, D])
        g_all = region_vec.take("g_all", [P, NE, D])
        bn_all = region_vec.take("bn_all", [P, NE, D])
        region_w1 = Region(max(region_acc.at, region_vec.at))
        w1_all = region_w1.take("w1_all", [P, KD, NE, HID])
        region_w2 = Region(region_w1.at)
        w2_all = region_w2.take("w2_all", [P, NE, KH, D])
        w2_end = region_w2.at
        hT = region_w2.take("hT", [P, 2, KH // 2, P])

        early = Region(region_w1.at)
        src_slot = early.take("src_slot", [P, SLOTS_UP], I32)
        dst_slot = early.take("dst_slot", [P, SLOTS_UP])
        pick = early.take("pick", [P, NT + 1, PICK])
        ln_stats = early.take("ln_stats", [P, NT, 2])
        rstd = early.take("rstd", [P, NT])
        node_tile_row = early.take("node_tile_row", [P, SLOTS_UP], I32)
        GB = 4
        early_b = early.at
        gather_ring = early.take("gather_ring", [P, GB, EB, ROW])
        OHB = 3
        onehot = early.take("onehot", [P, OHB, EB, P])
        onehotT = early.take("onehotT", [P, 1, EB, P])
        zbuf = early.take("zbuf", [P, 2, EB, HEADS])
        assert early.at <= nc.sbuf_usable_end

        s1 = Region(early_b)
        iota_slot = s1.take("iota_slot", [P, SLOTS_UP])
        above = s1.take("above", [P, SLOT_GROUPS, SLOTS_UP])
        raw_idx = s1.take("raw_idx", [P, 2, P], I32)
        raw_f = s1.take("raw_f", [P, 2, P])
        x_ring = 6
        s1w = Region(max(region_acc.at, region_vec.at))
        xt = s1w.take("xt", [P, x_ring, D])
        xn = s1w.take("xn", [P, x_ring, D])
        rt = s1w.take("rt", [P, x_ring, D])
        xnT = s1w.take("xnT", [P, 2, KD, P])
        w_ext = s1w.take("w_ext", [P, KD, D + PICK])
        att_rows = s1w.take("att_rows", [P, 2, D])
        w_att = s1w.take("w_att", [P, KD, 2, D])
        st6 = s1w.take("st6", [P, x_ring, 6])
        beta_row = s1w.take("beta_row", [P, D])
        own = s1w.take("own", [P, NT, HEADS])
        own2 = s1w.take("own2", [P, NT, HEADS])
        max_src = s1w.take("max_src", [P, HEADS])
        max_all = s1w.take("max_all", [P, HEADS])
        last_dst = s1w.take("last_dst", [P, SLOT_GROUPS], I32)
        last_tile = s1w.take("last_tile", [P, SLOT_GROUPS], I32)
        key = s1w.take("key", [P, SLOT_GROUPS])
        tile_no = s1w.take("tile_no", [P, SLOT_GROUPS])
        edge_tile = s1w.take("edge_tile", [P, SLOT_GROUPS])
        edge_tile_i = s1w.take("edge_tile_i", [P, SLOT_GROUPS], I32)
        slot_base = s1w.take("slot_base", [P, SLOT_GROUPS])
        pad_src = s1w.take("pad_src", [P, P], I32)
        pad_dst = s1w.take("pad_dst", [P, P], I32)
        blank = s1w.take("blank", [P, XROW])

        s3 = Region(region_w1.at)
        NG = 7
        assert NT % NG == 0
        GROUPS = NT // NG
        square = s3.take("square", [P, 2, D])
        col = s3.take("col", [P, 6, D])
        bias_row, gamma_row, mean_row, scale_row, sd_row = (col[:, i, :] for i in range(5))
        r_ring = s3.take("r_ring", [P, 2, NG, D])
        bn6 = s3.take("bn6", [P, NG, 6])
        mv = s3.take("mv", [P, NT, 2])
        sd1 = s3.take("sd1", [P, NT])
        rs1 = s3.take("rs1", [P, NT])
        v2 = s3.take("v2", [P, NT])
        sd2 = s3.take("sd2", [P, NT])
        rs2 = s3.take("rs2", [P, NT])
        xf = s3.take("xf", [P, 2, D])
        xfT = s3.take("xfT", [P, 2, KD, P])
        wr = s3.take("wr", [P, KD, NE])
        br_row = s3.take("br_row", [P, NE])
        lg = s3.take("lg", [P, NT, NE])
        prob = s3.take("prob", [P, NT, NE])
        eq = s3.take("eq", [P, NT, NE])
        first = s3.take("first", [P, 2, NT, NE])
        iota_e = s3.take("iota_e", [P, NT, NE])
        tok = s3.take("tok", [P, NT])
        valid = s3.take("valid", [P, NT])
        top = s3.take("top", [P, 6, NT])
        chosen = s3.take("chosen", [P, NT, NE])
        below = s3.take("below", [P, P])
        totals = s3.take("totals", [P, NT, NE])
        upto = s3.take("upto", [P, NT, NE])
        place = s3.take("place", [P, NT, NE])
        ones_row = s3.take("ones_row", [P, NT])
        ex = s3.take("ex", [P, 6, NE])
        ex_i = s3.take("ex_i", [P, 2, NE], I32)
        cmp_e = s3.take("cmp_e", [P, FT, NE])
        tile_e = s3.take("tile_e", [P, FT])
        tile_iota = s3.take("tile_iota", [P, FT])
        tail = Region(w2_end)
        assert s3.at <= w2_end
        row_of = tail.take("row_of", [P, 2, NT], I32)
        weight = tail.take("weight", [P, 2, NT])

        bank = [ctx.enter_context(nc.psum_tensor(f"bank{i}", [P, 512], F32)) for i in range(8)]

        pe, dve, act, pool, sp = (Stream(sem(f"{n}_steps")) for n in ("pe", "dve", "act", "pool", "sp"))
        dmas = []

        def dma_marker(name):
            m = Marker(sem(name))
            dmas.append(m)
            return m

        c_iota = pool.do(lambda e: e.iota(iota_free[:, :], [[1, P]], base=0, channel_multiplier=0,
                                          allow_small_or_imprecise_dtypes=True))
        c_part = pool.do(lambda e: e.iota(part[:, :], [[0, 1]], base=0, channel_multiplier=1,
                                          allow_small_or_imprecise_dtypes=True))
        c_slot = pool.do(lambda e: e.iota(iota_slot[:, :], [[1, SLOTS_UP]], base=0, channel_multiplier=0,
                                          allow_small_or_imprecise_dtypes=True))
        c_tileno = pool.do(lambda e: e.iota(tile_no[:, :], [[P, SLOT_GROUPS]], base=0, channel_multiplier=1,
                                            allow_small_or_imprecise_dtypes=True))
        c_pads = pool.do(lambda e: e.memset(pad_src[:, :], 0))
        c_padd = pool.do(lambda e: e.memset(pad_dst[:, :], (NT + 1) * P))
        c_blank = pool.do(lambda e: e.memset(blank[:, :], 0.0))
        c_ones = dve.do(lambda e: e.memset(ones[:, :], 1.0))
        c_eps = dve.do(lambda e: e.memset(eps[:, :], EPS))
        c_ident = dve.do(lambda e: e.tensor_scalar(ident[:, :], iota_free[:, :], part[:, 0:1], None, ALU.is_equal),
                         [c_iota, c_part])
        m = dve.do(lambda e: e.tensor_scalar(blank[:, D + 1:D + 2], part[:, 0:1], float(N), None, ALU.add),
                   [c_part, c_blank])
        c_blank = m
        c_acc = dve.do(lambda e: e.memset(acc[:, NT, :], 0.0))
        c_pick = dve.do(lambda e: e.memset(pick[:, NT, :], 0.0))
        c_xlast = dve.do(lambda e: e.memset(xt[:, (NT - 1) % x_ring, :], 0.0))

        d_edge = dma_marker("edge_lists_padded")
        full = (ET - 1) * P
        for raw, padded, pad in ((src, src_pad, pad_src), (dst, dst_pad, pad_dst)):
            sp.dma(d_edge, lambda e, raw=raw, padded=padded: e.dma_start(
                padded[0:ET - 1, :], raw[0:full].rearrange("(t p) -> t p", p=P)))
            sp.dma(d_edge, lambda e, raw=raw, padded=padded: e.dma_start(
                padded[ET - 1:ET, 0:E - full], raw[full:E].rearrange("(t p) -> t p", t=1)))
            if E - full < P:
                sp.dma(d_edge, lambda e, padded=padded, pad=pad: e.dma_start(
                    padded[ET - 1:ET, E - full:P], pad[0:1, E - full:P]), [c_pads, c_padd])
            sp.dma(d_edge, lambda e, padded=padded, pad=pad: e.dma_start(
                padded[ET:SLOTS_UP, :], pad[0:SLOTS_UP - ET, :]), [c_pads, c_padd])
        edges_padded = d_edge.mark()

        d_w = dma_marker("stage1_weights")
        act.dma(d_w, lambda e: e.dma_start(w_ext[:, :, 0:D], W.rearrange("(k p) n -> p k n", p=P)))
        for i, a in enumerate((att_src, att_dst)):
            act.dma(d_w, lambda e, i=i, a=a: e.dma_start(
                att_rows[:, i, :], a.rearrange("h d -> (h d)").rearrange("(a n) -> a n", a=1).broadcast_to([P, D])))
        act.dma(d_w, lambda e: e.dma_start(beta_row[:, :], beta.rearrange("(a n) -> a n", a=1).broadcast_to([P, D])))
        w_loaded = d_w.mark()

        d_last = dma_marker("last_dst_loaded")
        last_loaded = sp.dma(d_last, lambda e: e.dma_start(
            last_dst[:, :].rearrange("p (c a) -> p c a", a=1),
            dst_pad.rearrange("(c p) k -> p c k", p=P)[:, :, P - 1:P], allow_slow_non_contiguous=True), [edges_padded])

        d_blank = dma_marker("expert_rows_blanked")
        BL = 15 if FT % 15 == 0 else 1
        for f in range(0, FT, BL):
            rows_blank = sp.dma(d_blank, lambda e, f=f: e.dma_start(
                expert_rows[f * P:(f + BL) * P, :].rearrange("(s p) c -> p s c", p=P),
                blank[:, :].rearrange("p (a c) -> p a c", a=1).broadcast_to([P, BL, XROW])), [c_blank])
        spare_zero = sp.dma(d_blank, lambda e: e.dma_start(out[N:N + P, :], blank[:, 0:D]), [c_blank])

        for k in range(KD):
            for i in range(2):
                m = dve.do(lambda e, k=k, i=i: e.tensor_tensor(w_att[:, k, i, :], w_ext[:, k, 0:D], att_rows[:, i, :],
                                                               ALU.mult), [w_loaded])
        w_folded = dve.do(lambda e: e.tensor_reduce(
            w_ext[:, :, D:D + PICK].rearrange("p k (i h) -> p k i h", i=2),
            w_att[:, :, :, :].rearrange("p k i (h d) -> p k i h d", d=DH), AX.X, ALU.add), [m])

        d_x = [dma_marker(f"x_loaded{i}") for i in range(x_ring)]
        d_t = dma_marker("node_table_written")
        d_r = [dma_marker(f"resid_written{i}") for i in range(x_ring)]
        xn_made, resid_made, xnT_ready, rows_done, tr_done, table_marks = {}, {}, {}, {}, {}, None
        rs_made, sd_made, stat_made, acc_copied, x_marks, resid_marks = {}, {}, {}, {}, {}, {}

        def rows_of(n):
            return LAST if n == NT - 1 else P

        def s1_load(n):
            after = [c_xlast]
            if n >= x_ring:
                after += [xn_made[n - x_ring], resid_made[n - x_ring]]
            x_marks[n] = sp.dma(d_x[n % x_ring], lambda e: e.dma_start(
                xt[0:rows_of(n), n % x_ring, :], x[n * P:n * P + rows_of(n), :]), after)

        def s1_stats(n):
            j = n % x_ring
            m = dve.do(lambda e: e.bn_stats(st6[:, j, :], xt[:, j, :]), [x_marks[n], c_xlast])
            stat_made[n] = dve.do(lambda e: e.bn_aggr(ln_stats[:, n, :], st6[:, j, :]), [m])
            sd_made[n] = act.do(lambda e: e.activation(rstd[:, n:n + 1], ln_stats[:, n, 1:2], ACT.Sqrt, bias=eps[:, :]),
                                [stat_made[n], c_eps])

        def s1_norm(n):
            j = n % x_ring
            m = dve.do(lambda e: e.reciprocal(rstd[:, n:n + 1], rstd[:, n:n + 1]), [sd_made[n]])
            after = [m, stat_made[n]]
            if n >= x_ring:
                after += [tr_done[n - x_ring], resid_made[n - x_ring]]
            xn_made[n] = dve.do(lambda e: e.tensor_scalar(xn[:, j, :], xt[:, j, :], ln_stats[:, n, 0:1],
                                                          rstd[:, n:n + 1], ALU.subtract, ALU.mult), after)
            after = [xn_made[n]] + ([resid_marks[n - x_ring]] if n >= x_ring else [])
            m = pool.do(lambda e: e.tensor_tensor(rt[:, j, :], xt[:, j, :], xn[:, j, :], ALU.add), after)
            resid_made[n] = pool.do(lambda e: e.tensor_tensor(rt[:, j, :], rt[:, j, :], beta_row[:, :], ALU.add),
                                    [m, w_loaded])

        def s1_turn(n):
            j, q = n % x_ring, n % 2
            after = [xn_made[n], c_ident] + ([xnT_ready[n - 2]] if n >= 2 else [])
            for k in range(KD):
                tr_done[n] = pe.do(lambda e, k=k: e.transpose(bank[q][:, k * P:(k + 1) * P],
                                                              xn[:, j, k * P:(k + 1) * P], ident[:, :]), after)
            after = [tr_done[n]] + ([rows_done[n - 2]] if n >= 2 else [])
            xnT_ready[n] = act.do(lambda e: e.activation(xnT[:, q, :, :].rearrange("p k m -> p (k m)"),
                                                         bank[q][:, 0:D], ACT.Copy), after)

        def s1_product(n):
            q = n % 2
            after = [xnT_ready[n], w_folded] + ([acc_copied[n - 2][0], acc_copied[n - 2][1]] if n >= 2 else [])
            for k in range(KD):
                rows_done[n] = pe.do(lambda e, k=k: e.matmul(bank[2 + q][:, 0:D + PICK], xnT[:, q, k, :], w_ext[:, k, :],
                                                             start=(k == 0), stop=(k == KD - 1)), after)

        def s1_keep(n):
            q = n % 2
            a = dve.do(lambda e: e.tensor_copy(acc[:, n, :], bank[2 + q][:, 0:ROW]), [rows_done[n]])
            b = act.do(lambda e: e.activation(pick[:, n, 0:HEADS], bank[2 + q][:, ROW:D + PICK], ACT.Copy),
                       [a])
            acc_copied[n] = (a, b)

        def s1_store(n):
            j = n % x_ring
            resid_marks[n] = act.dma(d_r[j], lambda e: e.dma_start(resid_rows[n * P:(n + 1) * P, :], rt[:, j, :]),
                                     [resid_made[n]])
            sp.dma(d_t, lambda e: e.dma_start(node_table[n * P:n * P + rows_of(n), :], acc[0:rows_of(n), n, :]),
                   [acc_copied[n][0]])

        d_raw = [dma_marker(f"slot_rows{i}") for i in range(2)]

        def slot_keys():
            m = dve.do(lambda e: e.tensor_single_scalar(last_tile[:, :], last_dst[:, :], 7, ALU.arith_shift_right),
                       [last_loaded])
            m = dve.do(lambda e: e.tensor_copy(key[:, :], last_tile[:, :]), [m])
            m = dve.do(lambda e: e.scalar_tensor_tensor(key[:, :], key[:, :], float(NT - 1), tile_no[:, :],
                                                        ALU.min, ALU.add), [m, c_tileno])
            for c in range(SLOT_GROUPS):
                above_made = dve.do(lambda e, c=c: e.tensor_scalar(above[:, c, :], iota_slot[:, :], key[:, c:c + 1], None,
                                                                   ALU.is_gt), [m, c_slot])
            for g in range(SLOT_GROUPS):
                for c in range(SLOT_GROUPS):
                    t_part = pe.do(lambda e, g=g, c=c: e.matmul(bank[4][:, g:g + 1], above[:, c, g * P:(g + 1) * P],
                                                                ones[:, 0:1], start=(c == 0), stop=(c == SLOT_GROUPS - 1)),
                                   [above_made, c_ones])
            hw = SLOTS_UP // 2
            for h in range(2):
                for c in range(SLOT_GROUPS):
                    t_row = pe.do(lambda e, h=h, c=c: e.matmul(bank[5 + h][:, 0:hw], ones[:, :],
                                                               above[:, c, h * hw:(h + 1) * hw], start=(c == 0),
                                                               stop=(c == SLOT_GROUPS - 1)), [])
            for h in range(2):
                row_made = dve.do(lambda e, h=h: e.tensor_tensor(
                    node_tile_row[:, h * hw:(h + 1) * hw], iota_slot[:, h * hw:(h + 1) * hw], bank[5 + h][:, 0:hw],
                    ALU.subtract), [t_row])
            a = dve.do(lambda e: e.tensor_copy(edge_tile_i[:, :], bank[4][:, 0:SLOT_GROUPS]), [t_part])
            b = dve.do(lambda e: e.tensor_tensor(slot_base[:, :], tile_no[:, :], bank[4][:, 0:SLOT_GROUPS],
                                                 ALU.subtract), [t_part])
            b = dve.do(lambda e: e.tensor_single_scalar(slot_base[:, :], slot_base[:, :], float(P), ALU.mult), [b])
            return row_made, a, b

        tables = {}

        def slot_table(i):
            g, which = divmod(i, 2)
            row_made, idx_made, base_made = tables["keys"]
            after = [idx_made, edges_padded] + ([tables["float", i - 2]] if i >= 2 else [])
            got = pool.dma(d_raw[which], lambda e: e.indirect_dma_start(
                out=raw_idx[:, which, :], out_offset=None, in_=(src_pad, dst_pad)[which],
                in_offset=bass.IndirectOffsetOnAxis(ap=edge_tile_i[:, g:g + 1], axis=0)), after)
            after = [got] + ([tables["turned", i - 2]] if i >= 2 else [])
            m = dve.do(lambda e: e.tensor_copy(raw_f[:, which, :], raw_idx[:, which, :]), after)
            tables["float", i] = m
            if which:
                m = dve.do(lambda e: e.tensor_scalar(raw_f[:, which, :], raw_f[:, which, :], slot_base[:, g:g + 1], None,
                                                     ALU.subtract), [m, base_made])
            tables["turned", i] = pe.do(lambda e: e.transpose(bank[7][:, which * P:(which + 1) * P], raw_f[:, which, :],
                                                              ident[:, :]),
                                        [m, c_ident] + ([tables["kept", i - 2]] if i >= 2 else []))
            to = (src_slot, dst_slot)[which]
            tables["kept", i] = dve.do(lambda e: e.tensor_copy(to[:, g * P:(g + 1) * P],
                                                               bank[7][:, which * P:(which + 1) * P]),
                                       [tables["turned", i]])

        for n in range(NT + 4):
            if n < NT:
                s1_load(n)
            if n == 12:
                tables["keys"] = slot_keys()
            if 16 <= n < 16 + 2 * SLOT_GROUPS:
                slot_table(n - 16)
            if n < NT:
                s1_stats(n)
            if 2 <= n <= NT + 1:
                s1_norm(n - 2)
                s1_turn(n - 2)
            if 3 <= n <= NT + 2:
                s1_product(n - 3)
            if 4 <= n:
                s1_keep(n - 4)
                s1_store(n - 4)
        table_written = d_t.mark()
        slots_ready = tables["kept", 2 * SLOT_GROUPS - 1]
        rows_ready = acc_copied[NT - 1]
        row_made = tables["keys"][0]

        m = dve.do(lambda e: e.tensor_reduce(max_src[:, :], acc[:, 0:NT, D:ROW].rearrange("p n h -> p h n"),
                                             AX.X, ALU.max), [rows_ready[0]])
        all_max = pool.do(lambda e: e.partition_all_reduce(max_all[:, :], max_src[:, :], P, bass.bass_isa.ReduceOp.max), [m])
        shift_ap = pick[:, 0:NT, HEADS:PICK]
        a_dst_ap = pick[:, 0:NT, 0:HEADS]
        m = dve.do(lambda e: e.tensor_tensor(own[:, :, :], a_dst_ap, max_all[:, :].rearrange("p (a h) -> p a h", a=1)
                                             .broadcast_to([P, NT, HEADS]), ALU.add), [all_max, rows_ready[1]])
        shift_made = dve.do(lambda e: e.scalar_tensor_tensor(shift_ap, own[:, :, :], NEG_SLOPE, own[:, :, :],
                                                             ALU.mult, ALU.max), [m])
        m = dve.do(lambda e: e.tensor_tensor(own2[:, :, :], a_dst_ap, acc[:, 0:NT, D:ROW], ALU.add), [rows_ready[1]])
        m = dve.do(lambda e: e.scalar_tensor_tensor(own[:, :, :], own2[:, :, :], NEG_SLOPE, own2[:, :, :],
                                                    ALU.mult, ALU.max), [m, shift_made])
        m = dve.do(lambda e: e.tensor_tensor(own[:, :, :], own[:, :, :], shift_ap, ALU.subtract), [m])
        own_weight = act.do(lambda e: e.activation(acc[:, 0:NT, D:ROW], own[:, :, :], ACT.Exp), [m, table_written])
        for g in range(GROUPS):
            acc_started = dve.do(lambda e, g=g: e.tensor_tensor(
                acc[:, g * NG:(g + 1) * NG, 0:D].rearrange("p n (h d) -> p n h d", d=DH),
                acc[:, g * NG:(g + 1) * NG, 0:D].rearrange("p n (h d) -> p n h d", d=DH),
                acc[:, g * NG:(g + 1) * NG, D:ROW].rearrange("p n (h a) -> p n h a", a=1)
                .broadcast_to([P, NG, HEADS, DH]), ALU.mult), [own_weight, table_written])

        d_w1 = dma_marker("w1_loaded")
        for ee in range(NE):
            w1_ready = sp.dma(d_w1, lambda e, ee=ee: e.dma_start(
                w1_all[:, :, ee, :], W1[ee].rearrange("(k p) h -> p k h", p=P)),
                [acc_started, own_weight, all_max, edges_padded, rows_blank, spare_zero, resid_made[NT - 1],
                 slots_ready] + [r.mark() for r in d_r])

        d_g = [[dma_marker(f"gathered{b}_{j}") for j in range(EB)] for b in range(GB)]
        OHT, AGG = (0, 1), (3, 4, 5, 6)
        PICKS = (2, 7)
        gat, oh, ohT, ohTc, pk, zz, wgt, msg, agg, added = ({} for _ in range(10))

        def e_gather(b):
            for j in range(EB):
                s = b * EB + j
                after = [slots_ready, table_written]
                if b >= GB:
                    after.append(agg[b - GB, EB - 1])
                else:
                    after.append(row_made)
                gat[b, j] = pool.dma(d_g[b % GB][j], lambda e, s=s, j=j: e.indirect_dma_start(
                    out=gather_ring[:, b % GB, j, :], out_offset=None, in_=node_table,
                    in_offset=bass.IndirectOffsetOnAxis(ap=src_slot[:, s:s + 1], axis=0)), after)

        def e_onehot(b, j):
            s = b * EB + j
            after = [slots_ready] + ([agg[b - OHB, EB - 1]] if b >= OHB else [])
            oh[b, j] = dve.do(lambda e: e.tensor_scalar(onehot[:, b % OHB, j, :], iota_free[:, :],
                                                        dst_slot[:, s:s + 1], None, ALU.is_equal), after)

        def e_turn(b):
            for h in range(2):
                after = [ohTc[b - 1, h]] if b >= 1 else list(acc_copied[NT - 1]) + [slots_ready]
                for j in range(4 * h, 4 * h + 4):
                    ohT[b, h] = pe.do(lambda e, j=j, h=h: e.transpose(
                        bank[OHT[h]][:, (j % 4) * P:(j % 4 + 1) * P], onehot[:, b % OHB, j, :], ident[:, :]),
                        after + [oh[b, j]])
                ohTc[b, h] = act.do(lambda e, h=h: e.activation(
                    onehotT[:, 0, 4 * h:4 * h + 4, :].rearrange("p j m -> p (j m)"), bank[OHT[h]][:, :], ACT.Copy),
                    [ohT[b, h]] + ([pk[b - 1]] if b >= 1 else []))

        reg = {}

        def load_tiles(stream, name, b):
            def go(e):
                _, values = nc.values_load_multi_w_load_instructions(
                    node_tile_row[0:1, b * EB:(b + 1) * EB], engines=[e.engine], min_val=0, max_val=NT,
                    skip_runtime_bounds_check_because=IN_RANGE)
                reg[name, b] = values
            stream.quiet(go, [row_made])

        def e_pick(b):
            load_tiles(pe, "pe", b)
            for j in range(EB):
                after = [ohTc[b, j // 4], shift_made] + ([zz[b - 2]] if b >= 2 else [])
                at = j * PICK
                pk[b] = pe.do(lambda e, j=j, at=at: e.matmul(
                    bank[PICKS[b % 2]][:, at:at + PICK], onehotT[:, 0, j, :],
                    pick[:, bass.ds(reg["pe", b][j], 1), :], start=True, stop=True), after)

        def picked(b, lo):
            return bank[PICKS[b % 2]][:, 0:EB * PICK].rearrange("p (j c) -> p j c", c=PICK)[:, :, lo:lo + HEADS]

        def e_z(b):
            return dve.do(lambda e: e.tensor_tensor(zbuf[:, 0, :, :], gather_ring[:, b % GB, :, D:ROW], picked(b, 0),
                                                    ALU.add), [gat[b, j] for j in range(EB)] + [pk[b]])

        def e_leaky(b, m):
            return dve.do(lambda e: e.scalar_tensor_tensor(zbuf[:, 1, :, :], zbuf[:, 0, :, :], NEG_SLOPE,
                                                           zbuf[:, 0, :, :], ALU.mult, ALU.max),
                          [m] + ([wgt[b - 1]] if b >= 1 else []))

        def e_shift(b, m):
            zz[b] = dve.do(lambda e: e.tensor_tensor(zbuf[:, 1, :, :], zbuf[:, 1, :, :], picked(b, HEADS),
                                                     ALU.subtract), [m])
            return zz[b]

        def e_bound(b, m):
            return dve.do(lambda e: e.tensor_single_scalar(zbuf[:, 1, :, :], zbuf[:, 1, :, :], 0.0, ALU.min), [m])

        def e_weight(b, m):
            wgt[b] = act.do(lambda e: e.activation(gather_ring[:, b % GB, :, D:ROW], zbuf[:, 1, :, :], ACT.Exp), [m])

        def e_message(b):
            v = lambda: gather_ring[:, b % GB, :, 0:D].rearrange("p j (h d) -> p j h d", d=DH)
            msg[b] = dve.do(lambda e: e.tensor_tensor(
                v(), v(), gather_ring[:, b % GB, :, D:ROW].rearrange("p j (h a) -> p j h a", a=1)
                .broadcast_to([P, EB, HEADS, DH]), ALU.mult), [wgt[b]])

        def e_sum(b):
            for j in range(EB):
                s = b * EB + j
                after = [msg[b], wgt[b], oh[b, j]]
                if s >= len(AGG):
                    after.append(lambda s=s: added[s - len(AGG)])
                agg[b, j] = pe.do(lambda e, s=s, j=j: e.matmul(
                    bank[AGG[s % len(AGG)]][:, 0:ROW], onehot[:, b % OHB, j, :], gather_ring[:, b % GB, j, :],
                    start=True, stop=True), after)

        def e_add(b, j):
            s = b * EB + j
            after = [agg[b, j], acc_started] + ([added[s - 1]] if s else [])

            def go(e):
                a = acc[:, bass.ds(reg["dve", b][j], 1), :]
                return e.tensor_tensor(a, a, bank[AGG[s % len(AGG)]][:, 0:ROW].rearrange("p (a c) -> p a c", a=1), ALU.add)
            added[s] = dve.do(go, after)

        for j in range(EB):
            e_onehot(0, j)
        e_turn(0)
        e_pick(0)
        for b in range(BATCHES + 1):
            now, nxt = b < BATCHES, b + 1 < BATCHES
            if b:
                load_tiles(dve, "dve", b - 1)
            if now:
                e_gather(b)
                m = e_z(b)
            for j in range(EB):
                if nxt:
                    e_onehot(b + 1, j)
                if now and j in (0, 1, 2):
                    m = (e_leaky, e_shift, e_bound)[j](b, m)
                    if j == 2:
                        e_weight(b, m)
                if b:
                    e_add(b - 1, j)
            if now:
                e_message(b)
            if nxt:
                e_turn(b + 1)
                e_pick(b + 1)
            if now:
                e_sum(b)
        edges_done = added[SLOTS - 1]

        ring_free = [edges_done, agg[BATCHES - 1, EB - 1], wgt[BATCHES - 1]]
        d_c = dma_marker("stage3_rows")
        for to, of in ((bias_row, bias), (gamma_row, gamma)):
            act.dma(d_c, lambda e, to=to, of=of: e.dma_start(to, of.rearrange("(a n) -> a n", a=1).broadcast_to([P, D])),
                    ring_free)
        act.dma(d_c, lambda e: e.dma_start(wr[:, :, :], Wr.rearrange("(k p) n -> p k n", p=P)), ring_free)
        act.dma(d_c, lambda e: e.dma_start(br_row[:, :], br.rearrange("(a n) -> a n", a=1).broadcast_to([P, NE])),
                ring_free)
        c_rows = d_c.mark()

        def tiles(g):
            return slice(g * NG, (g + 1) * NG)

        m = dve.do(lambda e: e.reciprocal(acc[:, 0:NT, D:ROW], acc[:, 0:NT, D:ROW]), [edges_done])
        summed = None
        for g in range(GROUPS):
            v = lambda g=g: acc[:, tiles(g), 0:D].rearrange("p n (h d) -> p n h d", d=DH)
            a = dve.do(lambda e, g=g, v=v: e.tensor_tensor(v(), v(), acc[:, tiles(g), D:ROW].rearrange(
                "p n (h a) -> p n h a", a=1).broadcast_to([P, NG, HEADS, DH]), ALU.mult), [m])
            a = dve.do(lambda e, g=g: e.tensor_tensor(
                acc[:, tiles(g), 0:D], acc[:, tiles(g), 0:D],
                bias_row.rearrange("p (a d) -> p a d", a=1).broadcast_to([P, NG, D]), ALU.add), [a, c_rows])
            for n in range(g * NG, (g + 1) * NG):
                r = rows_of(n)
                summed = pe.do(lambda e, n=n, r=r: e.matmul(bank[7][:, 0:D], ones[0:r, :], acc[0:r, n, 0:D],
                                                            start=(n == 0), stop=(n == NT - 1)), [a])
        mean_made = act.do(lambda e: e.activation(mean_row, bank[7][:, 0:D], ACT.Copy, scale=1.0 / N), [summed])
        sq, sq_used = {}, {}
        for g in range(GROUPS):
            a = dve.do(lambda e, g=g: e.tensor_tensor(
                acc[:, tiles(g), 0:D], acc[:, tiles(g), 0:D],
                mean_row.rearrange("p (a d) -> p a d", a=1).broadcast_to([P, NG, D]), ALU.subtract), [mean_made, summed])
            for n in range(g * NG, (g + 1) * NG):
                r = rows_of(n)
                sq[n] = act.do(lambda e, n=n: e.activation(square[:, n % 2, :], acc[:, n, 0:D], ACT.Square),
                               [a] + ([sq_used[n - 2]] if n >= 2 else ring_free))
                sq_used[n] = pe.do(lambda e, n=n, r=r: e.matmul(bank[6][:, 0:D], ones[0:r, :], square[0:r, n % 2, :],
                                                                start=(n == 0), stop=(n == NT - 1)), [sq[n]])
        centred = a
        m = act.do(lambda e: e.activation(sd_row, bank[6][:, 0:D], ACT.Sqrt, bias=eps[:, :], scale=1.0 / N),
                   [sq_used[NT - 1]])
        m = dve.do(lambda e: e.reciprocal(scale_row, sd_row), [m])
        scale_made = dve.do(lambda e: e.tensor_tensor(scale_row, scale_row, gamma_row, ALU.mult), [m, c_rows])

        d_ri = [dma_marker(f"resid_loaded{i}") for i in range(2)]
        d_o = dma_marker("out_started")
        xf_made, xf_turned, xfT_made, lg_done, row_ready, x1_used = {}, {}, {}, {}, {}, {}
        r_loaded, x1_made, rs_done = {}, {}, {}

        def resid_load(g):
            r_loaded[g] = sp.dma(d_ri[g % 2], lambda e: e.dma_start(
                r_ring[:, g % 2, :, :], resid_rows[g * NG * P:(g + 1) * NG * P, :].rearrange("(n p) d -> p n d", p=P)),
                ring_free + [r.mark() for r in d_r] + ([x1_made[g - 2]] if g >= 2 else []))

        def x1_stage(g):
            a = dve.do(lambda e: e.tensor_tensor(acc[:, tiles(g), 0:D], acc[:, tiles(g), 0:D],
                                                 scale_row.rearrange("p (a d) -> p a d", a=1).broadcast_to([P, NG, D]),
                                                 ALU.mult), [scale_made, sq[NT - 1]])
            a = x1_made[g] = dve.do(lambda e: e.tensor_tensor(acc[:, tiles(g), 0:D], acc[:, tiles(g), 0:D],
                                                              r_ring[:, g % 2, :, :], ALU.add), [a, r_loaded[g]])
            for n in range(g * NG, (g + 1) * NG):
                x1_used[n] = sp.dma(d_o, lambda e, n=n: e.dma_start(out[n * P:n * P + rows_of(n), :],
                                                                    acc[0:rows_of(n), n, 0:D]), [a])
            for i in range(NG):
                b = dve.do(lambda e, i=i: e.bn_stats(bn6[:, i, :], acc[:, g * NG + i, 0:D]), [a])
            for i in range(NG):
                b2_ = dve.do(lambda e, i=i: e.bn_aggr(mv[:, g * NG + i, :], bn6[:, i, :]), [b])
            t = tiles(g)
            var = mv[:, t, 1:2].rearrange("p n a -> p (n a)")
            m = act.do(lambda e: e.activation(sd1[:, t], var, ACT.Sqrt, bias=eps[:, :]), [b2_])
            m = r1 = dve.do(lambda e: e.reciprocal(rs1[:, t], sd1[:, t]), [m])
            m = dve.do(lambda e: e.tensor_tensor(v2[:, t], var, rs1[:, t], ALU.mult), [m])
            m = dve.do(lambda e: e.tensor_tensor(v2[:, t], v2[:, t], rs1[:, t], ALU.mult), [m])
            m = act.do(lambda e: e.activation(sd2[:, t], v2[:, t], ACT.Sqrt, bias=eps[:, :]), [m])
            rs_done[g] = dve.do(lambda e: e.reciprocal(rs2[:, t], sd2[:, t]), [m])

        def xf_stage(n):
            q, g = n % 2, n // NG
            after = [rs_done[g]] + ([xf_turned[n - 2], row_ready[n - 2]] if n >= 2 else [])
            xf_made[n] = dve.do(lambda e: e.tensor_scalar(xf[:, q, :], acc[:, n, 0:D], mv[:, n, 0:1], rs1[:, n:n + 1],
                                                          ALU.subtract, ALU.mult), after)
            row_ready[n] = act.do(lambda e: e.activation(acc[:, n, 0:D], xf[:, q, :], ACT.Copy, scale=rs2[:, n:n + 1]),
                                  [xf_made[n], d_o_all[g]])
            for k in range(KD):
                xf_turned[n] = pe.do(lambda e, k=k: e.transpose(bank[q][:, k * P:(k + 1) * P],
                                                                xf[:, q, k * P:(k + 1) * P], ident[:, :]),
                                     [xf_made[n]] + ([xfT_made[n - 2]] if n >= 2 else []))
            xfT_made[n] = act.do(lambda e: e.activation(xfT[:, q, :, :].rearrange("p k m -> p (k m)"), bank[q][:, 0:D],
                                                        ACT.Copy), [xf_turned[n]] + ([lg_done[n - 2]] if n >= 2 else []))
            for k in range(KD):
                lg_done[n] = pe.do(lambda e, k=k: e.matmul(bank[5][:, n * NE:(n + 1) * NE], xfT[:, q, k, :], wr[:, k, :],
                                                           start=(k == 0), stop=(k == KD - 1)), [xfT_made[n], c_rows])

        d_o_all = {}
        for g in range(GROUPS + 1):
            if g < GROUPS:
                resid_load(g)
                x1_stage(g)
                d_o_all[g] = d_o.mark()
            if g:
                for n in range((g - 1) * NG, g * NG):
                    xf_stage(n)

        c_e = pool.do(lambda e: e.iota(iota_e[:, :, :], [[0, NT], [1, NE]], base=0, channel_multiplier=0,
                                       allow_small_or_imprecise_dtypes=True), ring_free)
        c_tok = pool.do(lambda e: e.iota(tok[:, :], [[P, NT]], base=0, channel_multiplier=1,
                                         allow_small_or_imprecise_dtypes=True), ring_free)
        c_ti = pool.do(lambda e: e.iota(tile_iota[:, :], [[1, FT]], base=0, channel_multiplier=0,
                                        allow_small_or_imprecise_dtypes=True), ring_free)
        c_valid = dve.do(lambda e: e.tensor_single_scalar(valid[:, :], tok[:, :], float(N), ALU.is_lt), [c_tok])
        c_below = dve.do(lambda e: e.tensor_scalar(below[:, :], iota_free[:, :], part[:, 0:1], None, ALU.is_gt),
                         ring_free)
        c_or = dve.do(lambda e: e.memset(ones_row[:, :], 1.0), ring_free)

        def per_tile(ap):
            return ap.rearrange("p (n a) -> p n a", a=1).broadcast_to([P, NT, NE])

        def tt(o, a, b, op, after):
            return dve.do(lambda e: e.tensor_tensor(o, a, b, op), after)

        def reduce_e(o, a, op, after):
            return dve.do(lambda e: e.tensor_reduce(o, a, AX.X, op), after)

        L3, P3, Q3, C3 = lg[:, :, :], prob[:, :, :], eq[:, :, :], chosen[:, :, :]
        m = tt(L3, bank[5][:, 0:NT * NE].rearrange("p (n a) -> p n a", a=NE),
               br_row[:, :].rearrange("p (a h) -> p a h", a=1).broadcast_to([P, NT, NE]), ALU.add, [lg_done[NT - 1], c_rows])
        m = reduce_e(top[:, 0, :], L3, ALU.max, [m])
        m = tt(L3, L3, per_tile(top[:, 0, :]), ALU.subtract, [m])
        m = act.do(lambda e: e.activation(P3, L3, ACT.Exp), [m])
        m = reduce_e(top[:, 1, :], P3, ALU.add, [m])
        m = dve.do(lambda e: e.reciprocal(top[:, 1, :], top[:, 1, :]), [m])
        m = tt(P3, P3, per_tile(top[:, 1, :]), ALU.mult, [m])
        for c in range(TOP):
            F3 = first[:, c, :, :]
            m = reduce_e(top[:, 2 + c, :], P3, ALU.max, [m])
            m = tt(Q3, P3, per_tile(top[:, 2 + c, :]), ALU.is_equal, [m])
            m = dve.do(lambda e, F3=F3: e.scalar_tensor_tensor(F3, iota_e[:, :, :], float(NE), Q3, ALU.subtract, ALU.mult),
                       [m, c_e])
            m = reduce_e(top[:, 4, :], F3, ALU.min, [m])
            m = dve.do(lambda e: e.tensor_single_scalar(top[:, 4, :], top[:, 4, :], float(NE), ALU.add), [m])
            m = tt(F3, iota_e[:, :, :], per_tile(top[:, 4, :]), ALU.is_equal, [m])
            if c == 0:
                m = dve.do(lambda e, F3=F3: e.scalar_tensor_tensor(P3, F3, -2.0, P3, ALU.mult, ALU.add), [m])
        m = tt(top[:, 5, :], top[:, 2, :], top[:, 3, :], ALU.add, [m])
        m = dve.do(lambda e: e.reciprocal(top[:, 5, :], top[:, 5, :]), [m])
        for c in range(TOP):
            m = tt(weight[:, c, :], top[:, 2 + c, :], top[:, 5, :], ALU.mult, [m])
        m = tt(C3, first[:, 0, :, :], first[:, 1, :, :], ALU.add, [m])
        m = tt(C3, C3, per_tile(valid[:, :]), ALU.mult, [m, c_valid])
        flat = chosen[:, :, :].rearrange("p n a -> p (n a)")
        rank_done = pe.do(lambda e: e.matmul(bank[0][:, 0:NT * NE], below[:, :], flat, start=True, stop=True),
                          [m, c_below, xfT_made[NT - 1], xfT_made[NT - 2]])
        tot_done = pe.do(lambda e: e.matmul(bank[1][:, 0:NT * NE], ones[:, :], flat, start=True, stop=True), [m])
        m = dve.do(lambda e: e.tensor_copy(totals[:, :, :].rearrange("p n a -> p (n a)"), bank[1][:, 0:NT * NE]),
                   [tot_done])
        for ee in range(NE):
            mm = dve.do(lambda e, ee=ee: e.tensor_tensor_scan(
                upto[:, :, ee:ee + 1].rearrange("p n a -> p (n a)"), ones_row[:, :],
                totals[:, :, ee:ee + 1].rearrange("p n a -> p (n a)"), 0.0, ALU.mult, ALU.add), [m, c_or])
        count = upto[:, NT - 1, :]
        up = tt(place[:, :, :], upto[:, :, :], totals[:, :, :], ALU.subtract, [mm])
        up = tt(place[:, :, :], place[:, :, :], bank[0][:, 0:NT * NE].rearrange("p (n a) -> p n a", a=NE), ALU.add,
                [up, rank_done])
        m = dve.do(lambda e: e.tensor_single_scalar(ex[:, 0, :], count, float(P - 1), ALU.add), [mm])
        m = dve.do(lambda e: e.tensor_copy(ex_i[:, 0, :], ex[:, 0, :]), [m])
        m = dve.do(lambda e: e.tensor_single_scalar(ex_i[:, 1, :], ex_i[:, 0, :], 7, ALU.arith_shift_right), [m])
        m = dve.do(lambda e: e.tensor_copy(ex[:, 1, :], ex_i[:, 1, :]), [m])
        m = dve.do(lambda e: e.tensor_tensor_scan(ex[:, 2, :], ones_row[:, 0:NE], ex[:, 1, :], 0.0, ALU.mult, ALU.add),
                   [m])
        ends = m
        m = tt(ex[:, 3, :], ex[:, 2, :], ex[:, 1, :], ALU.subtract, [m])
        m = dve.do(lambda e: e.tensor_single_scalar(ex[:, 3, :], ex[:, 3, :], float(P), ALU.mult), [m])
        m = tt(place[:, :, :], place[:, :, :], ex[:, 3, :].rearrange("p (a h) -> p a h", a=1)
               .broadcast_to([P, NT, NE]), ALU.add, [m, up])
        for c in range(TOP):
            m = tt(Q3, place[:, :, :], first[:, c, :, :], ALU.mult, [m])
            m = reduce_e(top[:, c, :], Q3, ALU.add, [m])
            m = dve.do(lambda e, c=c: e.tensor_copy(row_of[:, c, :], top[:, c, :]), [m])
        placed = m
        m = tt(cmp_e[:, :, :], tile_iota[:, :].rearrange("p (s a) -> p s a", a=1).broadcast_to([P, FT, NE]),
               ex[:, 2, :].rearrange("p (a h) -> p a h", a=1).broadcast_to([P, FT, NE]), ALU.is_ge, [ends, c_ti])
        m = reduce_e(tile_e[:, :], cmp_e[:, :, :], ALU.add, [m])
        experts_known = dve.do(lambda e: e.tensor_single_scalar(expert_of_tile[:, :], tile_e[:, :], float(NE - 1),
                                                                ALU.min), [m])
        m = dve.do(lambda e: e.tensor_copy(acc[:, 0:NT, D + 1:D + 2].rearrange("p n a -> p (n a)"), tok[:, :]),
                   [placed, row_ready[NT - 1]])
        put = {}
        tails = {0: dve.do(lambda e: e.tensor_copy(acc[:, 0:NT, D:D + 1].rearrange("p n a -> p (n a)"),
                                                   weight[:, 0, :]), [m])}
        d_s = [dma_marker(f"dispatched{c}") for c in range(TOP)]
        for c in range(TOP):
            if c:
                tails[c] = dve.do(lambda e: e.tensor_copy(acc[:, 0:NT, D:D + 1].rearrange("p n a -> p (n a)"),
                                                          weight[:, 1, :]), [d_s[0].mark()])
            for n in range(NT):
                r = rows_of(n)
                pool.dma(d_s[c], lambda e, n=n, c=c, r=r: e.indirect_dma_start(
                    out=expert_rows, out_offset=bass.IndirectOffsetOnAxis(ap=row_of[0:r, c, n:n + 1], axis=0),
                    in_=acc[0:r, n, 0:XROW], in_offset=None), [tails[c], placed, rows_blank, row_ready[n]])
        dispatched = [d_s[0].mark(), d_s[1].mark()]

        d_w2 = dma_marker("w2_loaded")
        for ee in range(NE):
            w2_ready = sp.dma(d_w2, lambda e, ee=ee: e.dma_start(
                w2_all[:, ee, :, :], W2[ee].rearrange("(c p) d -> p c d", p=P)), [experts_known, placed, tails[0], rank_done])
        d_v = dma_marker("expert_vectors_loaded")
        for to, of in ((g_all, ln_g), (bn_all, ln_b), (b1_all, b1), (b2_all, b2)):
            v_ready = sp.dma(d_v, lambda e, to=to, of=of: e.dma_start(
                to[:, :, :].rearrange("p e d -> p (e d)"),
                of.rearrange("e d -> (e d)").rearrange("(a n) -> a n", a=1).broadcast_to([P, of.shape[0] * of.shape[1]])),
                dispatched)

        d_xs = [dma_marker(f"expert_rows_loaded{i}") for i in range(XR)]
        d_y = dma_marker("out_added")
        XT, HB, TB, YB = 0, (1, 2, 3, 4), (5, 6), 7
        loaded, gone, xe_made, xeT_made, turned, h_done, h_biased, h_act, hT_turned, hT_made, y_done, y_made, y_sent = (
            {} for _ in range(13))
        ereg = {}
        EL = 4

        def expert_regs(stream, name, s):
            if s % EL == 0:
                def go(e):
                    hi = min(s + EL, FT)
                    _, values = nc.values_load_multi_w_load_instructions(
                        expert_of_tile[0:1, s:hi], engines=[e.engine], min_val=0, max_val=NE - 1,
                        skip_runtime_bounds_check_because=IN_RANGE)
                    for i in range(s, hi):
                        ereg[name, i] = values[i - s]
                stream.quiet(go, [experts_known])

        def f_load(s):
            after = dispatched + ([y_made[s - XR]] if s >= XR else [])
            loaded[s] = sp.dma(d_xs[s % XR], lambda e: e.dma_start(xs[:, s % XR, :], expert_rows[s * P:(s + 1) * P, :]),
                               after)

        def f_input(s):
            q = s % 2
            expert_regs(dve, "dve", s)
            three = lambda t: t.rearrange("p (a d) -> p a d", a=1)
            m = dve.do(lambda e: e.tensor_tensor(three(xe[:, q, :]), three(xs[:, s % XR, 0:D]),
                                                 g_all[:, bass.ds(ereg["dve", s], 1), :], ALU.mult),
                       [loaded[s], v_ready] + ([turned[s - 2]] if s >= 2 else []))
            gone[s] = dve.do(lambda e: e.tensor_copy(token_id[:, s % XR:s % XR + 1], xs[:, s % XR, D + 1:D + 2]),
                             [loaded[s]] + ([y_sent[s - XR]] if s >= XR else []))
            xe_made[s] = dve.do(lambda e: e.tensor_tensor(three(xe[:, q, :]), three(xe[:, q, :]),
                                                          bn_all[:, bass.ds(ereg["dve", s], 1), :], ALU.add), [m])
            for k in range(KD):
                turned[s] = pe.do(lambda e, k=k: e.transpose(bank[XT][:, k * P:(k + 1) * P],
                                                             xe[:, q, k * P:(k + 1) * P], ident[:, :]),
                                  [xe_made[s]] + ([xeT_made[s - 1]] if s else [rank_done, placed]))
            xeT_made[s] = act.do(lambda e: e.activation(xeT[:, q, :, :].rearrange("p k m -> p (k m)"),
                                                        bank[XT][:, 0:D], ACT.Copy),
                                 [turned[s]] + ([h_done[s - 2, 1]] if s >= 2 else []))

        def f_hidden(s):
            q = s % 2
            expert_regs(pe, "pe", s)
            for h in range(2):
                i = 2 * s + h
                bk = bank[HB[i % 4]]
                for k in range(KD):
                    h_done[s, h] = pe.do(lambda e, k=k, h=h, bk=bk: e.matmul(
                        bk[:, :], xeT[:, q, k, :],
                        w1_all[:, k, bass.ds(ereg["pe", s], 1), h * HALF:(h + 1) * HALF],
                        start=(k == 0), stop=(k == KD - 1)),
                        [xeT_made[s], w1_ready] + ([h_biased[(i - 4) // 2, h]] if i >= 4 else []))
                h_biased[s, h] = dve.do(lambda e, h=h, i=i, bk=bk: e.tensor_tensor(
                    hid[:, i % HR, :].rearrange("p (a n) -> p a n", a=1), bk[:, :].rearrange("p (a n) -> p a n", a=1),
                    b1_all[:, bass.ds(ereg["dve", s], 1), h * HALF:(h + 1) * HALF], ALU.add),
                    [h_done[s, h], v_ready] + ([hT_turned[(i - HR) // 2, (i - HR) % 2]] if i >= HR else []))
                h_act[s, h] = act.do(lambda e, i=i: e.activation(hid[:, i % HR, :], hid[:, i % HR, :], ACT.Gelu),
                                     [h_biased[s, h]])

        def f_turn(s, h):
            i = 2 * s + h
            tb = bank[TB[h]]
            for c in range(4):
                hT_turned[s, h] = pe.do(lambda e, c=c: e.transpose(
                    tb[:, c * P:(c + 1) * P], hid[:, i % HR, c * P:(c + 1) * P], ident[:, :]),
                    [h_act[s, h]] + ([hT_made[s - 1, h]] if s else []))
            hT_made[s, h] = act.do(lambda e: e.activation(hT[:, h, :, :].rearrange("p c m -> p (c m)"), tb[:, :],
                                                          ACT.Copy),
                                   [hT_turned[s, h]] + ([y_done[s - 1, h]] if s else [w2_ready]))

        def f_output(s, h):
            q = s % 2
            for c in range(4):
                y_done[s, h] = pe.do(lambda e, c=c: e.matmul(
                    bank[YB][:, 0:D], hT[:, h, c, :],
                    w2_all[:, bass.ds(ereg["pe", s], 1), 4 * h + c, :],
                    start=(h == 0 and c == 0), stop=(h == 1 and c == 3)),
                    [hT_made[s, h], w2_ready] + ([y_made[s - 1]] if s else []))

        def f_finish(s):
            q = s % 2
            m = dve.do(lambda e: e.tensor_tensor(
                y[:, q, :].rearrange("p (a d) -> p a d", a=1),
                bank[YB][:, 0:D].rearrange("p (a d) -> p a d", a=1),
                b2_all[:, bass.ds(ereg["dve", s], 1), :], ALU.add), [y_done[s, 1]] + ([y_sent[s - 2]] if s >= 2 else []))
            y_made[s] = dve.do(lambda e: e.tensor_scalar(y[:, q, :], y[:, q, :], xs[:, s % XR, D:D + 1], None, ALU.mult),
                               [m])
            y_sent[s] = pool.dma(d_y, lambda e: e.indirect_dma_start(
                out=out, out_offset=bass.IndirectOffsetOnAxis(ap=token_id[:, s % XR:s % XR + 1], axis=0),
                in_=y[:, q, :], in_offset=None, compute_op=ALU.add),
                [y_made[s], gone[s], d_o.mark(), spare_zero] + ([y_sent[s - 1]] if s else []))

        AHEAD = 3
        for s in range(AHEAD):
            f_load(s)
        f_input(0)
        for s in range(FT + 1):
            if s + AHEAD < FT:
                f_load(s + AHEAD)
            if s < FT:
                if s + 1 < FT:
                    f_input(s + 1)
                f_hidden(s)
            if s:
                f_output(s - 1, 0)
                f_output(s - 1, 1)
                f_finish(s - 1)
            if s < FT:
                f_turn(s, 0)
                f_turn(s, 1)

        sp.quiet(lambda e: None, [m_.mark() for m_ in dmas if m_.count])

        block = ctx.enter_context(nc.Block())

        @block.sync
        def _(e):
            sp.play(e)

        @block.gpsimd
        def _(e):
            pool.play(e)

        @block.scalar
        def _(e):
            act.play(e)

        @block.vector
        def _(e):
            dve.play(e)

        @block.tensor
        def _(e):
            pe.play(e)


INPUTS = ["x", "src", "dst", "L0_gnn_W", "L0_gnn_att_src", "L0_gnn_att_dst", "L0_gnn_bias", "L0_gnn_gamma",
          "L0_gnn_beta", "L0_ffn_Wr", "L0_ffn_br", "L0_ffn_ln_g", "L0_ffn_ln_b", "L0_ffn_W1", "L0_ffn_b1",
          "L0_ffn_W2", "L0_ffn_b2"]


def kernel(**inputs):
    import numpy as _np
    import concourse.bacc as _bacc
    from concourse import mybir as _mybir
    from concourse.bass_utils import run_bass_kernel_spmd as _run

    nc = _bacc.Bacc("TRN2", target_bir_lowering=False, num_devices=1)
    arrays, args = {}, []
    for name in INPUTS:
        a = _np.ascontiguousarray(inputs[name])
        arrays[f"in_{name}"] = a
        args.append(nc.dram_tensor(f"in_{name}", a.shape, _mybir.dt.from_np(a.dtype), kind="ExternalInput").ap())
    n, d = inputs["x"].shape
    args.append(nc.dram_tensor("out_rows", (n + 128, d), _mybir.dt.float32, kind="ExternalOutput").ap())
    build_gnn_moe(nc, *args)
    r = _run(nc, [arrays], core_ids=[0])
    return r.results[0]["out_rows"][:n]
```

```python
from contextlib import ExitStack

import numpy as np

import concourse.bass as bass
from concourse import mybir

ALU = mybir.AluOpType
ACT = mybir.ActivationFunctionType
AX = mybir.AxisListType
F32 = mybir.dt.float32
I32 = mybir.dt.int32
P = 128
NEG_SLOPE = 0.2
EPS = 1e-5
IN_RANGE = "the value is worked out on the chip within the shapes' bounds, whatever the data"


def ceil_div(a, b):
    return -(-a // b)


class Marker:

    def __init__(self, sem):
        self.sem, self.count = sem, 0

    def mark(self):
        return (self.sem, self.count)


class Stream(Marker):

    def __init__(self, sem):
        super().__init__(sem)
        self.steps = []

    def do(self, fn, after=()):
        self.count += 1
        self.steps.append((tuple(after), fn, self.sem, 1))
        return self.mark()

    def quiet(self, fn, after=()):
        self.steps.append((tuple(after), fn, None, 0))

    def dma(self, marker, fn, after=()):
        marker.count += 16
        self.steps.append((tuple(after), fn, marker.sem, 16))
        return marker.mark()

    def play(self, engine):
        passed = {}
        for after, fn, sem, step in self.steps:
            for item in after:
                waited, value = item() if callable(item) else item
                if passed.get(id(waited), 0) < value:
                    engine.wait_ge(waited, value)
                    passed[id(waited)] = value
            made = fn(engine)
            if sem is not None:
                made.then_inc(sem, step)


def build_gnn_moe(nc, x, src, dst, W, att_src, att_dst, bias, gamma, beta,
                  Wr, br, ln_g, ln_b, W1, b1, W2, b2, out):
    N, D = x.shape
    HEADS, DH = att_src.shape
    E = src.shape[0]
    NE, _, HID = W1.shape
    KD = D // P
    KH = HID // P
    HALF = HID // 2
    NT = ceil_div(N, P)
    LAST = N - (NT - 1) * P
    ET = ceil_div(E, P)
    SLOT_GROUPS = ceil_div(ET + NT, P)
    SLOTS_UP = SLOT_GROUPS * P
    EB = 8
    SLOTS = ceil_div(ET + NT - 1, EB) * EB
    BATCHES = SLOTS // EB
    assert ET + 1 <= SLOTS_UP and SLOTS <= SLOTS_UP and SLOTS - ET <= NT
    ROW = D + HEADS
    PICK = 2 * HEADS
    TOP = 2
    FT = (N * TOP - NE) // P + NE
    XROW = D + 4
    W_COL, TOKEN_COL, FIRST_COL = D, D + 2, D + 3
    REGION = (NT + 1) * P
    SPARE_TILES = FT - N * TOP // P

    node_table = nc.dram_tensor("node_table", (N, ROW), F32, kind="Internal").ap()
    resid_rows = nc.dram_tensor("resid_rows", (NT * P, D), F32, kind="Internal").ap()
    src_pad = nc.dram_tensor("src_pad", (SLOTS_UP, P), I32, kind="Internal").ap()
    dst_pad = nc.dram_tensor("dst_pad", (SLOTS_UP, P), I32, kind="Internal").ap()
    expert_rows = nc.dram_tensor("expert_rows", (NE * REGION + SPARE_TILES * P, XROW), F32, kind="Internal").ap()

    with ExitStack() as ctx:
        def sem(name):
            return ctx.enter_context(nc.semaphore(name))

        base = nc.sbuf_base + (-nc.sbuf_base) % 32

        class Region:
            def __init__(self, start):
                self.at = start

            def take(self, name, shape, dt=F32):
                t = nc.alloc_sbuf_tensor_at(name, list(shape), dt, offset=self.at)
                self.at += ceil_div(int(np.prod(shape[1:])) * 4, 32) * 32
                assert self.at <= nc.sbuf_usable_end, name
                return t

        small = Region(base)
        ident = small.take("ident", [P, P])
        part = small.take("part", [P, 1])
        eps = small.take("eps", [P, 1])
        expert_of_tile = small.take("expert_of_tile", [P, FT], I32)
        expert_of_tile_f = small.take("expert_of_tile_f", [P, FT])
        row_of_tile = small.take("row_of_tile", [P, FT], I32)
        blank_row = small.take("blank_row", [P, NE], I32)
        early_consts = Region(small.at)
        iota_free = early_consts.take("iota_free", [P, P])
        ones = early_consts.take("ones", [P, P])
        blank = early_consts.take("blank", [P, XROW])
        XR, HR = 5, 3
        xs = small.take("xs", [P, XR, XROW])
        xe = small.take("xe", [P, 2, D])
        xeT = small.take("xeT", [P, 2, KD, P])
        hid = small.take("hid", [P, HR, HALF])
        y = small.take("y", [P, 2, D])
        token_id = small.take("token_id", [P, XR], I32)
        gate = small.take("gate", [P, XR, 3])
        assert early_consts.at <= small.at

        region_acc = Region(small.at)
        acc = region_acc.take("acc", [P, NT + 1, ROW])
        region_vec = Region(small.at)
        b1_all = region_vec.take("b1_all", [P, NE, HID])
        b2_all = region_vec.take("b2_all", [P, NE, D])
        g_all = region_vec.take("g_all", [P, NE, D])
        bn_all = region_vec.take("bn_all", [P, NE, D])
        region_w1 = Region(max(region_acc.at, region_vec.at))
        w1_all = region_w1.take("w1_all", [P, KD, NE, HID])
        region_w2 = Region(region_w1.at)
        w2_all = region_w2.take("w2_all", [P, NE, KH, D])
        w2_end = region_w2.at
        hT = region_w2.take("hT", [P, 2, KH // 2, P])

        early = Region(region_w1.at)
        src_slot = early.take("src_slot", [P, SLOTS_UP], I32)
        dst_slot = early.take("dst_slot", [P, SLOTS_UP])
        pick = early.take("pick", [P, NT + 1, PICK])
        ln_stats = early.take("ln_stats", [P, NT, 2])
        rstd = early.take("rstd", [P, NT])
        node_tile_row = early.take("node_tile_row", [P, SLOTS_UP], I32)
        GB = 4
        early_b = early.at
        gather_ring = early.take("gather_ring", [P, GB, EB, ROW])
        OHB = 3
        onehot = early.take("onehot", [P, OHB, EB, P])
        onehotT = early.take("onehotT", [P, 1, EB, P])
        zbuf = early.take("zbuf", [P, 2, EB, HEADS])
        assert early.at <= nc.sbuf_usable_end

        s1 = Region(early_b)
        iota_slot = s1.take("iota_slot", [P, SLOTS_UP])
        above = s1.take("above", [P, SLOT_GROUPS, SLOTS_UP])
        raw_idx = s1.take("raw_idx", [P, 4, P], I32)
        raw_f = s1.take("raw_f", [P, 2, P])
        x_ring = 6
        s1w = Region(max(region_acc.at, region_vec.at))
        xt = s1w.take("xt", [P, x_ring, D])
        xn = s1w.take("xn", [P, x_ring, D])
        rt = s1w.take("rt", [P, x_ring, D])
        xnT = s1w.take("xnT", [P, 2, KD, P])
        w_ext = s1w.take("w_ext", [P, KD, D + PICK])
        att_rows = s1w.take("att_rows", [P, 2, D])
        w_att = s1w.take("w_att", [P, KD, 2, D])
        st6 = s1w.take("st6", [P, x_ring, 6])
        beta_row = s1w.take("beta_row", [P, D])
        own = s1w.take("own", [P, NT, HEADS])
        own2 = s1w.take("own2", [P, NT, HEADS])
        max_src = s1w.take("max_src", [P, HEADS])
        max_all = s1w.take("max_all", [P, HEADS])
        last_dst = s1w.take("last_dst", [P, SLOT_GROUPS], I32)
        last_tile = s1w.take("last_tile", [P, SLOT_GROUPS], I32)
        key = s1w.take("key", [P, SLOT_GROUPS])
        tile_no = s1w.take("tile_no", [P, SLOT_GROUPS])
        edge_tile = s1w.take("edge_tile", [P, SLOT_GROUPS])
        edge_tile_i = s1w.take("edge_tile_i", [P, SLOT_GROUPS], I32)
        slot_base = s1w.take("slot_base", [P, SLOT_GROUPS])
        pad_src = s1w.take("pad_src", [P, P], I32)
        pad_dst = s1w.take("pad_dst", [P, P], I32)

        s3 = Region(region_w1.at)
        NG = 7
        assert NT % NG == 0
        GROUPS = NT // NG
        square = s3.take("square", [P, 2, NG, D])
        col = s3.take("col", [P, 6, D])
        bias_row, gamma_row, mean_row, scale_row, sd_row = (col[:, i, :] for i in range(5))
        r_ring = s3.take("r_ring", [P, 2, NG, D])
        bn6 = s3.take("bn6", [P, NG, 6])
        mv = s3.take("mv", [P, NT, 2])
        sd1 = s3.take("sd1", [P, NT])
        rs1 = s3.take("rs1", [P, NT])
        v2 = s3.take("v2", [P, NT])
        sd2 = s3.take("sd2", [P, NT])
        rs2 = s3.take("rs2", [P, NT])
        FR = 4
        shared = Region(s3.at)
        xf = s3.take("xf", [P, FR, D])
        xfT = s3.take("xfT", [P, FR, KD, P])
        wr = s3.take("wr", [P, KD, NE])
        br_row = s3.take("br_row", [P, NE])
        lg = s3.take("lg", [P, NT, NE])
        prob = s3.take("prob", [P, NT, NE])
        eq = s3.take("eq", [P, NT, NE])
        first = s3.take("first", [P, 2, NT, NE])
        iota_e = s3.take("iota_e", [P, NT, NE])
        tok = s3.take("tok", [P, NT])
        valid = s3.take("valid", [P, NT])
        top = s3.take("top", [P, 6, NT])
        chosen = s3.take("chosen", [P, NT, NE])
        below = s3.take("below", [P, P])
        totals = s3.take("totals", [P, NT, NE])
        upto = s3.take("upto", [P, NT, NE])
        place = s3.take("place", [P, NT, NE])
        ones_row = s3.take("ones_row", [P, NT])
        ex = s3.take("ex", [P, 6, NE])
        ex_i = s3.take("ex_i", [P, 2, NE], I32)
        cmp_e = shared.take("cmp_e", [P, FT, NE])
        region_e = s3.take("region_e", [P, NE])
        tile_e = s3.take("tile_e", [P, FT])
        tile_iota = s3.take("tile_iota", [P, FT])
        tail = Region(w2_end)
        assert s3.at <= w2_end
        row_of = tail.take("row_of", [P, 2, NT], I32)
        assert FT * NE <= FR * D

        bank = [ctx.enter_context(nc.psum_tensor(f"bank{i}", [P, 512], F32)) for i in range(8)]

        pe, dve, act, pool, sp = (Stream(sem(f"{n}_steps")) for n in ("pe", "dve", "act", "pool", "sp"))
        dmas = []

        def dma_marker(name):
            m = Marker(sem(name))
            dmas.append(m)
            return m

        c_iota = pool.do(lambda e: e.iota(iota_free[:, :], [[1, P]], base=0, channel_multiplier=0,
                                          allow_small_or_imprecise_dtypes=True))
        c_part = pool.do(lambda e: e.iota(part[:, :], [[0, 1]], base=0, channel_multiplier=1,
                                          allow_small_or_imprecise_dtypes=True))
        c_slot = pool.do(lambda e: e.iota(iota_slot[:, :], [[1, SLOTS_UP]], base=0, channel_multiplier=0,
                                          allow_small_or_imprecise_dtypes=True))
        c_tileno = pool.do(lambda e: e.iota(tile_no[:, :], [[P, SLOT_GROUPS]], base=0, channel_multiplier=1,
                                            allow_small_or_imprecise_dtypes=True))
        c_pads = pool.do(lambda e: e.memset(pad_src[:, :], 0))
        c_padd = pool.do(lambda e: e.memset(pad_dst[:, :], (NT + 1) * P))
        c_blank = pool.do(lambda e: e.memset(blank[:, :], 0.0))
        c_ones = dve.do(lambda e: e.memset(ones[:, :], 1.0))
        c_eps = dve.do(lambda e: e.memset(eps[:, :], EPS))
        c_ident = dve.do(lambda e: e.tensor_scalar(ident[:, :], iota_free[:, :], part[:, 0:1], None, ALU.is_equal),
                         [c_iota, c_part])
        m = dve.do(lambda e: e.tensor_scalar(blank[:, TOKEN_COL:TOKEN_COL + 1], part[:, 0:1], float(N), None, ALU.add),
                   [c_part, c_blank])
        c_blank = m
        c_acc = dve.do(lambda e: e.memset(acc[:, NT, :], 0.0))
        c_pick = dve.do(lambda e: e.memset(pick[:, NT, :], 0.0))
        c_xlast = dve.do(lambda e: e.memset(xt[:, (NT - 1) % x_ring, :], 0.0))

        d_edge = dma_marker("edge_lists_padded")
        full = (ET - 1) * P
        for raw, padded, pad in ((src, src_pad, pad_src), (dst, dst_pad, pad_dst)):
            sp.dma(d_edge, lambda e, raw=raw, padded=padded: e.dma_start(
                padded[0:ET - 1, :], raw[0:full].rearrange("(t p) -> t p", p=P)))
            sp.dma(d_edge, lambda e, raw=raw, padded=padded: e.dma_start(
                padded[ET - 1:ET, 0:E - full], raw[full:E].rearrange("(t p) -> t p", t=1)))
            if E - full < P:
                sp.dma(d_edge, lambda e, padded=padded, pad=pad: e.dma_start(
                    padded[ET - 1:ET, E - full:P], pad[0:1, E - full:P]), [c_pads, c_padd])
            sp.dma(d_edge, lambda e, padded=padded, pad=pad: e.dma_start(
                padded[ET:SLOTS_UP, :], pad[0:SLOTS_UP - ET, :]), [c_pads, c_padd])
        edges_padded = d_edge.mark()

        d_w = dma_marker("stage1_weights")
        act.dma(d_w, lambda e: e.dma_start(w_ext[:, :, 0:D], W.rearrange("(k p) n -> p k n", p=P)))
        for i, a in enumerate((att_src, att_dst)):
            act.dma(d_w, lambda e, i=i, a=a: e.dma_start(
                att_rows[:, i, :], a.rearrange("h d -> (h d)").rearrange("(a n) -> a n", a=1).broadcast_to([P, D])))
        act.dma(d_w, lambda e: e.dma_start(beta_row[:, :], beta.rearrange("(a n) -> a n", a=1).broadcast_to([P, D])))
        w_loaded = d_w.mark()

        d_last = dma_marker("last_dst_loaded")
        last_loaded = sp.dma(d_last, lambda e: e.dma_start(
            last_dst[:, :].rearrange("p (c a) -> p c a", a=1),
            dst_pad.rearrange("(c p) k -> p c k", p=P)[:, :, P - 1:P], allow_slow_non_contiguous=True), [edges_padded])

        d_blank = dma_marker("blanks_written")

        def write_blanks():
            for f in range(SPARE_TILES):
                act.dma(d_blank, lambda e, f=f: e.dma_start(
                    expert_rows[NE * REGION + f * P:NE * REGION + (f + 1) * P, :], blank[:, :]), [c_blank])
            return act.dma(d_blank, lambda e: e.dma_start(out[N:N + P, :], blank[:, 0:D]), [c_blank])

        for k in range(KD):
            for i in range(2):
                m = dve.do(lambda e, k=k, i=i: e.tensor_tensor(w_att[:, k, i, :], w_ext[:, k, 0:D], att_rows[:, i, :],
                                                               ALU.mult), [w_loaded])
        w_folded = dve.do(lambda e: e.tensor_reduce(
            w_ext[:, :, D:D + PICK].rearrange("p k (i h) -> p k i h", i=2),
            w_att[:, :, :, :].rearrange("p k i (h d) -> p k i h d", d=DH), AX.X, ALU.add), [m])

        d_x = [dma_marker(f"x_loaded{i}") for i in range(x_ring)]
        d_t = dma_marker("node_table_written")
        d_r = [dma_marker(f"resid_written{i}") for i in range(x_ring)]
        xn_made, resid_made, xnT_ready, rows_done, tr_done, table_marks = {}, {}, {}, {}, {}, None
        rs_made, sd_made, stat_made, acc_copied, x_marks, resid_marks = {}, {}, {}, {}, {}, {}

        def rows_of(n):
            return LAST if n == NT - 1 else P

        def s1_load(n):
            after = [c_xlast]
            if n >= x_ring:
                after += [xn_made[n - x_ring], resid_made[n - x_ring]]
            x_marks[n] = sp.dma(d_x[n % x_ring], lambda e: e.dma_start(
                xt[0:rows_of(n), n % x_ring, :], x[n * P:n * P + rows_of(n), :]), after)

        def s1_stats(n):
            j = n % x_ring
            m = dve.do(lambda e: e.bn_stats(st6[:, j, :], xt[:, j, :]), [x_marks[n], c_xlast])
            stat_made[n] = dve.do(lambda e: e.bn_aggr(ln_stats[:, n, :], st6[:, j, :]), [m])
            sd_made[n] = act.do(lambda e: e.activation(rstd[:, n:n + 1], ln_stats[:, n, 1:2], ACT.Sqrt, bias=eps[:, :]),
                                [stat_made[n], c_eps])

        def s1_norm(n):
            j = n % x_ring
            m = dve.do(lambda e: e.reciprocal(rstd[:, n:n + 1], rstd[:, n:n + 1]), [sd_made[n]])
            after = [m, stat_made[n]]
            if n >= x_ring:
                after += [tr_done[n - x_ring], resid_made[n - x_ring]]
            xn_made[n] = dve.do(lambda e: e.tensor_scalar(xn[:, j, :], xt[:, j, :], ln_stats[:, n, 0:1],
                                                          rstd[:, n:n + 1], ALU.subtract, ALU.mult), after)
            after = [xn_made[n]] + ([resid_marks[n - x_ring]] if n >= x_ring else [])
            m = pool.do(lambda e: e.tensor_tensor(rt[:, j, :], xt[:, j, :], xn[:, j, :], ALU.add), after)
            resid_made[n] = pool.do(lambda e: e.tensor_tensor(rt[:, j, :], rt[:, j, :], beta_row[:, :], ALU.add),
                                    [m, w_loaded])

        def s1_turn(n):
            j, q = n % x_ring, n % 2
            after = [xn_made[n], c_ident] + ([xnT_ready[n - 2]] if n >= 2 else [])
            for k in range(KD):
                tr_done[n] = pe.do(lambda e, k=k: e.transpose(bank[q][:, k * P:(k + 1) * P],
                                                              xn[:, j, k * P:(k + 1) * P], ident[:, :]), after)
            after = [tr_done[n]] + ([rows_done[n - 2]] if n >= 2 else [])
            xnT_ready[n] = act.do(lambda e: e.activation(xnT[:, q, :, :].rearrange("p k m -> p (k m)"),
                                                         bank[q][:, 0:D], ACT.Copy), after)

        def s1_product(n):
            q = n % 2
            after = [xnT_ready[n], w_folded] + ([acc_copied[n - 2][0], acc_copied[n - 2][1]] if n >= 2 else [])
            for k in range(KD):
                rows_done[n] = pe.do(lambda e, k=k: e.matmul(bank[2 + q][:, 0:D + PICK], xnT[:, q, k, :], w_ext[:, k, :],
                                                             start=(k == 0), stop=(k == KD - 1)), after)

        def s1_keep(n):
            q = n % 2
            a = dve.do(lambda e: e.tensor_copy(acc[:, n, :], bank[2 + q][:, 0:ROW]), [rows_done[n]])
            b = act.do(lambda e: e.activation(pick[:, n, 0:HEADS], bank[2 + q][:, ROW:D + PICK], ACT.Copy),
                       [a])
            acc_copied[n] = (a, b)

        def s1_store(n):
            j = n % x_ring
            resid_marks[n] = act.dma(d_r[j], lambda e: e.dma_start(resid_rows[n * P:(n + 1) * P, :], rt[:, j, :]),
                                     [resid_made[n]])
            sp.dma(d_t, lambda e: e.dma_start(node_table[n * P:n * P + rows_of(n), :], acc[0:rows_of(n), n, :]),
                   [acc_copied[n][0]])

        d_raw = [dma_marker(f"slot_rows{i}") for i in range(4)]

        def slot_keys():
            m = dve.do(lambda e: e.tensor_single_scalar(last_tile[:, :], last_dst[:, :], 7, ALU.arith_shift_right),
                       [last_loaded])
            m = dve.do(lambda e: e.tensor_copy(key[:, :], last_tile[:, :]), [m])
            m = dve.do(lambda e: e.scalar_tensor_tensor(key[:, :], key[:, :], float(NT - 1), tile_no[:, :],
                                                        ALU.min, ALU.add), [m, c_tileno])
            for c in range(SLOT_GROUPS):
                above_made = dve.do(lambda e, c=c: e.tensor_scalar(above[:, c, :], iota_slot[:, :], key[:, c:c + 1], None,
                                                                   ALU.is_gt), [m, c_slot])
            for g in range(SLOT_GROUPS):
                for c in range(SLOT_GROUPS):
                    t_part = pe.do(lambda e, g=g, c=c: e.matmul(bank[4][:, g:g + 1], above[:, c, g * P:(g + 1) * P],
                                                                ones[:, 0:1], start=(c == 0), stop=(c == SLOT_GROUPS - 1)),
                                   [above_made, c_ones])
            hw = SLOTS_UP // 2
            for h in range(2):
                for c in range(SLOT_GROUPS):
                    t_row = pe.do(lambda e, h=h, c=c: e.matmul(bank[5 + h][:, 0:hw], ones[:, :],
                                                               above[:, c, h * hw:(h + 1) * hw], start=(c == 0),
                                                               stop=(c == SLOT_GROUPS - 1)), [])
            for h in range(2):
                row_made = dve.do(lambda e, h=h: e.tensor_tensor(
                    node_tile_row[:, h * hw:(h + 1) * hw], iota_slot[:, h * hw:(h + 1) * hw], bank[5 + h][:, 0:hw],
                    ALU.subtract), [t_row])
            a = dve.do(lambda e: e.tensor_copy(edge_tile_i[:, :], bank[4][:, 0:SLOT_GROUPS]), [t_part])
            b = dve.do(lambda e: e.tensor_tensor(slot_base[:, :], tile_no[:, :], bank[4][:, 0:SLOT_GROUPS],
                                                 ALU.subtract), [t_part])
            b = dve.do(lambda e: e.tensor_single_scalar(slot_base[:, :], slot_base[:, :], float(P), ALU.mult), [b])
            return row_made, a, b

        tables = {}

        def slot_fetch(i):
            g, which = divmod(i, 2)
            _, idx_made, _ = tables["keys"]
            after = [idx_made, edges_padded] + ([tables["float", i - 4]] if i >= 4 else [])
            tables["got", i] = pool.dma(d_raw[i % 4], lambda e: e.indirect_dma_start(
                out=raw_idx[:, i % 4, :], out_offset=None, in_=(src_pad, dst_pad)[which],
                in_offset=bass.IndirectOffsetOnAxis(ap=edge_tile_i[:, g:g + 1], axis=0)), after)

        def slot_table(i):
            g, which = divmod(i, 2)
            _, _, base_made = tables["keys"]
            after = [tables["got", i]] + ([tables["turned", i - 2]] if i >= 2 else [])
            m = dve.do(lambda e: e.tensor_copy(raw_f[:, which, :], raw_idx[:, i % 4, :]), after)
            tables["float", i] = m
            if which:
                m = dve.do(lambda e: e.tensor_scalar(raw_f[:, which, :], raw_f[:, which, :], slot_base[:, g:g + 1], None,
                                                     ALU.subtract), [m, base_made])
            tables["turned", i] = pe.do(lambda e: e.transpose(bank[7][:, which * P:(which + 1) * P], raw_f[:, which, :],
                                                              ident[:, :]),
                                        [m, c_ident] + ([tables["kept", i - 2]] if i >= 2 else []))
            to = (src_slot, dst_slot)[which]
            tables["kept", i] = dve.do(lambda e: e.tensor_copy(to[:, g * P:(g + 1) * P],
                                                               bank[7][:, which * P:(which + 1) * P]),
                                       [tables["turned", i]])

        AHEAD_X = 3
        for n in range(AHEAD_X):
            s1_load(n)
        for n in range(NT + 4):
            if n + AHEAD_X < NT:
                s1_load(n + AHEAD_X)
            if n == 12:
                tables["keys"] = slot_keys()
            if 15 <= n < 15 + 2 * SLOT_GROUPS:
                slot_fetch(n - 15)
            if 18 <= n < 18 + 2 * SLOT_GROUPS:
                slot_table(n - 18)
            if n < NT:
                s1_stats(n)
            if 2 <= n <= NT + 1:
                s1_norm(n - 2)
                s1_turn(n - 2)
            if 3 <= n <= NT + 2:
                s1_product(n - 3)
            if 4 <= n:
                s1_keep(n - 4)
                s1_store(n - 4)
        spare_zero = write_blanks()
        table_written = d_t.mark()
        slots_ready = tables["kept", 2 * SLOT_GROUPS - 1]
        rows_ready = acc_copied[NT - 1]
        row_made = tables["keys"][0]

        m = dve.do(lambda e: e.tensor_reduce(max_src[:, :], acc[:, 0:NT, D:ROW].rearrange("p n h -> p h n"),
                                             AX.X, ALU.max), [rows_ready[0]])
        all_max = pool.do(lambda e: e.partition_all_reduce(max_all[:, :], max_src[:, :], P, bass.bass_isa.ReduceOp.max), [m])
        shift_ap = pick[:, 0:NT, HEADS:PICK]
        a_dst_ap = pick[:, 0:NT, 0:HEADS]
        m = dve.do(lambda e: e.tensor_tensor(own[:, :, :], a_dst_ap, max_all[:, :].rearrange("p (a h) -> p a h", a=1)
                                             .broadcast_to([P, NT, HEADS]), ALU.add), [all_max, rows_ready[1]])
        shift_made = dve.do(lambda e: e.scalar_tensor_tensor(shift_ap, own[:, :, :], NEG_SLOPE, own[:, :, :],
                                                             ALU.mult, ALU.max), [m])
        m = dve.do(lambda e: e.tensor_tensor(own2[:, :, :], a_dst_ap, acc[:, 0:NT, D:ROW], ALU.add), [rows_ready[1]])
        m = dve.do(lambda e: e.scalar_tensor_tensor(own[:, :, :], own2[:, :, :], NEG_SLOPE, own2[:, :, :],
                                                    ALU.mult, ALU.max), [m, shift_made])
        m = dve.do(lambda e: e.tensor_tensor(own[:, :, :], own[:, :, :], shift_ap, ALU.subtract), [m])
        own_weight = act.do(lambda e: e.activation(acc[:, 0:NT, D:ROW], own[:, :, :], ACT.Exp), [m, table_written])
        for g in range(GROUPS):
            acc_started = dve.do(lambda e, g=g: e.tensor_tensor(
                acc[:, g * NG:(g + 1) * NG, 0:D].rearrange("p n (h d) -> p n h d", d=DH),
                acc[:, g * NG:(g + 1) * NG, 0:D].rearrange("p n (h d) -> p n h d", d=DH),
                acc[:, g * NG:(g + 1) * NG, D:ROW].rearrange("p n (h a) -> p n h a", a=1)
                .broadcast_to([P, NG, HEADS, DH]), ALU.mult), [own_weight, table_written])

        d_w1 = dma_marker("w1_loaded")
        for ee in range(NE):
            w1_ready = sp.dma(d_w1, lambda e, ee=ee: e.dma_start(
                w1_all[:, :, ee, :], W1[ee].rearrange("(k p) h -> p k h", p=P)),
                [acc_started, own_weight, all_max, edges_padded, resid_made[NT - 1],
                 slots_ready] + [r.mark() for r in d_r])

        d_g = [[dma_marker(f"gathered{b}_{j}") for j in range(EB)] for b in range(GB)]
        OHT, AGG = (0, 1), (3, 4, 5, 6)
        PICKS = (2, 7)
        gat, oh, ohT, ohTc, pk, zz, wgt, msg, agg, added = ({} for _ in range(10))

        def e_gather(b):
            for j in range(EB):
                s = b * EB + j
                after = [slots_ready, table_written]
                if b >= GB:
                    after.append(agg[b - GB, EB - 1])
                else:
                    after.append(row_made)
                gat[b, j] = pool.dma(d_g[b % GB][j], lambda e, s=s, j=j: e.indirect_dma_start(
                    out=gather_ring[:, b % GB, j, :], out_offset=None, in_=node_table,
                    in_offset=bass.IndirectOffsetOnAxis(ap=src_slot[:, s:s + 1], axis=0)), after)

        def e_onehot(b, j):
            s = b * EB + j
            after = [slots_ready] + ([agg[b - OHB, EB - 1]] if b >= OHB else [])
            oh[b, j] = dve.do(lambda e: e.tensor_scalar(onehot[:, b % OHB, j, :], iota_free[:, :],
                                                        dst_slot[:, s:s + 1], None, ALU.is_equal), after)

        def e_turn(b):
            for h in range(2):
                after = [ohTc[b - 1, h]] if b >= 1 else list(acc_copied[NT - 1]) + [slots_ready]
                for j in range(4 * h, 4 * h + 4):
                    ohT[b, h] = pe.do(lambda e, j=j, h=h: e.transpose(
                        bank[OHT[h]][:, (j % 4) * P:(j % 4 + 1) * P], onehot[:, b % OHB, j, :], ident[:, :]),
                        after + [oh[b, j]])
                ohTc[b, h] = act.do(lambda e, h=h: e.activation(
                    onehotT[:, 0, 4 * h:4 * h + 4, :].rearrange("p j m -> p (j m)"), bank[OHT[h]][:, :], ACT.Copy),
                    [ohT[b, h]] + ([pk[b - 1]] if b >= 1 else []))

        reg = {}

        def load_tiles(stream, name, b):
            def go(e):
                _, values = nc.values_load_multi_w_load_instructions(
                    node_tile_row[0:1, b * EB:(b + 1) * EB], engines=[e.engine], min_val=0, max_val=NT,
                    skip_runtime_bounds_check_because=IN_RANGE)
                reg[name, b] = values
            stream.quiet(go, [row_made])

        def e_pick(b):
            load_tiles(pe, "pe", b)
            for j in range(EB):
                after = [ohTc[b, j // 4], shift_made] + ([zz[b - 2]] if b >= 2 else [])
                at = j * PICK
                pk[b] = pe.do(lambda e, j=j, at=at: e.matmul(
                    bank[PICKS[b % 2]][:, at:at + PICK], onehotT[:, 0, j, :],
                    pick[:, bass.ds(reg["pe", b][j], 1), :], start=True, stop=True), after)

        def picked(b, lo):
            return bank[PICKS[b % 2]][:, 0:EB * PICK].rearrange("p (j c) -> p j c", c=PICK)[:, :, lo:lo + HEADS]

        def e_z(b):
            return dve.do(lambda e: e.tensor_tensor(zbuf[:, 0, :, :], gather_ring[:, b % GB, :, D:ROW], picked(b, 0),
                                                    ALU.add), [gat[b, j] for j in range(EB)] + [pk[b]])

        def e_leaky(b, m):
            return dve.do(lambda e: e.scalar_tensor_tensor(zbuf[:, 1, :, :], zbuf[:, 0, :, :], NEG_SLOPE,
                                                           zbuf[:, 0, :, :], ALU.mult, ALU.max),
                          [m] + ([wgt[b - 1]] if b >= 1 else []))

        def e_shift(b, m):
            zz[b] = dve.do(lambda e: e.tensor_tensor(zbuf[:, 1, :, :], zbuf[:, 1, :, :], picked(b, HEADS),
                                                     ALU.subtract), [m])
            return zz[b]

        def e_bound(b, m):
            return dve.do(lambda e: e.tensor_single_scalar(zbuf[:, 1, :, :], zbuf[:, 1, :, :], 0.0, ALU.min), [m])

        def e_weight(b, m):
            wgt[b] = act.do(lambda e: e.activation(gather_ring[:, b % GB, :, D:ROW], zbuf[:, 1, :, :], ACT.Exp), [m])

        def e_message(b):
            v = lambda: gather_ring[:, b % GB, :, 0:D].rearrange("p j (h d) -> p j h d", d=DH)
            msg[b] = dve.do(lambda e: e.tensor_tensor(
                v(), v(), gather_ring[:, b % GB, :, D:ROW].rearrange("p j (h a) -> p j h a", a=1)
                .broadcast_to([P, EB, HEADS, DH]), ALU.mult), [wgt[b]])

        def e_sum(b):
            for j in range(EB):
                s = b * EB + j
                after = [msg[b], wgt[b], oh[b, j]]
                if s >= len(AGG):
                    after.append(lambda s=s: added[s - len(AGG)])
                agg[b, j] = pe.do(lambda e, s=s, j=j: e.matmul(
                    bank[AGG[s % len(AGG)]][:, 0:ROW], onehot[:, b % OHB, j, :], gather_ring[:, b % GB, j, :],
                    start=True, stop=True), after)

        def e_add(b, j):
            s = b * EB + j
            after = [agg[b, j], acc_started] + ([added[s - 1]] if s else [])

            def go(e):
                a = acc[:, bass.ds(reg["dve", b][j], 1), :]
                return e.tensor_tensor(a, a, bank[AGG[s % len(AGG)]][:, 0:ROW].rearrange("p (a c) -> p a c", a=1), ALU.add)
            added[s] = dve.do(go, after)

        for j in range(EB):
            e_onehot(0, j)
        e_turn(0)
        e_pick(0)
        for b in range(BATCHES + 1):
            now, nxt = b < BATCHES, b + 1 < BATCHES
            if b:
                load_tiles(dve, "dve", b - 1)
            if now:
                e_gather(b)
                m = e_z(b)
            for j in range(EB):
                if nxt:
                    e_onehot(b + 1, j)
                if now and j in (0, 1, 2):
                    m = (e_leaky, e_shift, e_bound)[j](b, m)
                    if j == 2:
                        e_weight(b, m)
                if b:
                    e_add(b - 1, j)
            if now:
                e_message(b)
            if nxt:
                e_turn(b + 1)
                e_pick(b + 1)
            if now:
                e_sum(b)
        edges_done = added[SLOTS - 1]

        ring_free = [edges_done, agg[BATCHES - 1, EB - 1], wgt[BATCHES - 1]]
        d_c = dma_marker("stage3_rows")
        for to, of in ((bias_row, bias), (gamma_row, gamma)):
            act.dma(d_c, lambda e, to=to, of=of: e.dma_start(to, of.rearrange("(a n) -> a n", a=1).broadcast_to([P, D])),
                    ring_free)
        act.dma(d_c, lambda e: e.dma_start(wr[:, :, :], Wr.rearrange("(k p) n -> p k n", p=P)), ring_free)
        act.dma(d_c, lambda e: e.dma_start(br_row[:, :], br.rearrange("(a n) -> a n", a=1).broadcast_to([P, NE])),
                ring_free)
        c_rows = d_c.mark()

        def tiles(g):
            return slice(g * NG, (g + 1) * NG)

        m = dve.do(lambda e: e.reciprocal(acc[:, 0:NT, D:ROW], acc[:, 0:NT, D:ROW]), [edges_done])
        summed = None
        for g in range(GROUPS):
            v = lambda g=g: acc[:, tiles(g), 0:D].rearrange("p n (h d) -> p n h d", d=DH)
            a = dve.do(lambda e, g=g, v=v: e.tensor_tensor(v(), v(), acc[:, tiles(g), D:ROW].rearrange(
                "p n (h a) -> p n h a", a=1).broadcast_to([P, NG, HEADS, DH]), ALU.mult), [m])
            for n in range(g * NG, (g + 1) * NG):
                r = rows_of(n)
                summed = pe.do(lambda e, n=n, r=r: e.matmul(bank[7][:, 0:D], ones[0:r, :], acc[0:r, n, 0:D],
                                                            start=(n == 0), stop=(n == NT - 1)), [a])
        m = dve.do(lambda e: e.scalar_tensor_tensor(mean_row, bank[7][:, 0:D], 1.0 / N, bias_row, ALU.mult, ALU.add),
                   [summed, c_rows])
        mean_made = dve.do(lambda e: e.tensor_tensor(mean_row, bias_row, mean_row, ALU.subtract), [m])
        sq, sq_used = {}, {}
        for g in range(GROUPS):
            a = dve.do(lambda e, g=g: e.tensor_tensor(
                acc[:, tiles(g), 0:D], acc[:, tiles(g), 0:D],
                mean_row.rearrange("p (a d) -> p a d", a=1).broadcast_to([P, NG, D]), ALU.add), [mean_made, summed])
            sq[g] = act.do(lambda e, g=g: e.activation(square[:, g % 2, :, :], acc[:, tiles(g), 0:D], ACT.Square),
                           [a] + ([sq_used[g - 2]] if g >= 2 else ring_free))
            for n in range(g * NG, (g + 1) * NG):
                r = rows_of(n)
                sq_used[g] = pe.do(lambda e, n=n, g=g, r=r: e.matmul(
                    bank[6][:, 0:D], ones[0:r, :], square[0:r, g % 2, n % NG, :],
                    start=(n == 0), stop=(n == NT - 1)), [sq[g]])
        centred = a
        m = act.do(lambda e: e.activation(sd_row, bank[6][:, 0:D], ACT.Sqrt, bias=eps[:, :], scale=1.0 / N),
                   [sq_used[GROUPS - 1]])
        m = dve.do(lambda e: e.reciprocal(scale_row, sd_row), [m])
        scale_made = dve.do(lambda e: e.tensor_tensor(scale_row, scale_row, gamma_row, ALU.mult), [m, c_rows])

        d_ri = [dma_marker(f"resid_loaded{i}") for i in range(2)]
        d_o = dma_marker("out_started")
        xf_made, xf_turned, xfT_made, lg_done, row_ready, x1_used = {}, {}, {}, {}, {}, {}
        r_loaded, x1_made, rs_done = {}, {}, {}

        def resid_load(g):
            r_loaded[g] = sp.dma(d_ri[g % 2], lambda e: e.dma_start(
                r_ring[:, g % 2, :, :], resid_rows[g * NG * P:(g + 1) * NG * P, :].rearrange("(n p) d -> p n d", p=P)),
                ring_free + [r.mark() for r in d_r] + ([x1_made[g - 2]] if g >= 2 else []))

        def x1_stage(g):
            t = tiles(g)
            a = dve.do(lambda e: e.tensor_tensor(acc[:, t, 0:D], acc[:, t, 0:D],
                                                 scale_row.rearrange("p (a d) -> p a d", a=1).broadcast_to([P, NG, D]),
                                                 ALU.mult), [scale_made, sq[GROUPS - 1]])
            yield
            a = x1_made[g] = dve.do(lambda e: e.tensor_tensor(acc[:, t, 0:D], acc[:, t, 0:D],
                                                              r_ring[:, g % 2, :, :], ALU.add), [a, r_loaded[g]])
            for n in range(g * NG, (g + 1) * NG):
                sp.dma(d_o, lambda e, n=n: e.dma_start(out[n * P:n * P + rows_of(n), :], acc[0:rows_of(n), n, 0:D]), [a])
            x1_stored[g] = d_o.mark()
            for i in range(NG):
                yield
                b = dve.do(lambda e, i=i: e.bn_stats(bn6[:, i, :], acc[:, g * NG + i, 0:D]), [a])
            for i in range(NG):
                yield
                b = dve.do(lambda e, i=i: e.bn_aggr(mv[:, g * NG + i, :], bn6[:, i, :]), [b])
            var = mv[:, t, 1:2].rearrange("p n a -> p (n a)")
            m = act.do(lambda e: e.activation(sd1[:, t], var, ACT.Sqrt, bias=eps[:, :]), [b])
            yield
            m = dve.do(lambda e: e.reciprocal(rs1[:, t], sd1[:, t]), [m])
            yield
            m = dve.do(lambda e: e.tensor_tensor(v2[:, t], var, rs1[:, t], ALU.mult), [m])
            yield
            m = dve.do(lambda e: e.tensor_tensor(v2[:, t], v2[:, t], rs1[:, t], ALU.mult), [m])
            m = act.do(lambda e: e.activation(sd2[:, t], v2[:, t], ACT.Sqrt, bias=eps[:, :]), [m])
            yield
            rs_done[g] = dve.do(lambda e: e.reciprocal(rs2[:, t], sd2[:, t]), [m])
            for n in range(g * NG, (g + 1) * NG):
                yield
                xf_stage(n)

        def xf_stage(n):
            q, g = n % FR, n // NG
            after = [rs_done[g]] + ([xf_turned[n - FR], row_ready[n - FR]] if n >= FR else [])
            xf_made[n] = dve.do(lambda e: e.tensor_scalar(xf[:, q, :], acc[:, n, 0:D], mv[:, n, 0:1], rs1[:, n:n + 1],
                                                          ALU.subtract, ALU.mult), after)
            for k in range(KD):
                xf_turned[n] = pe.do(lambda e, k=k: e.transpose(bank[q][:, k * P:(k + 1) * P],
                                                                xf[:, q, k * P:(k + 1) * P], ident[:, :]),
                                     [xf_made[n]] + ([xfT_made[n - FR]] if n >= FR else []))
            xfT_made[n] = act.do(lambda e: e.activation(xfT[:, q, :, :].rearrange("p k m -> p (k m)"), bank[q][:, 0:D],
                                                        ACT.Copy), [xf_turned[n]] + ([lg_done[n - FR]] if n >= FR else []))
            row_ready[n] = act.do(lambda e: e.activation(acc[:, n, 0:D], xf[:, q, :], ACT.Copy, scale=rs2[:, n:n + 1]),
                                  [xf_made[n], x1_stored[g]])
            for k in range(KD):
                lg_done[n] = pe.do(lambda e, k=k: e.matmul(
                    bank[LG[g % 2]][:, (n % NG) * NE:(n % NG + 1) * NE], xfT[:, q, k, :], wr[:, k, :],
                    start=(k == 0), stop=(k == KD - 1)),
                    [xfT_made[n], c_rows, scale_made] + ([lg_read[g - 2]] if g >= 2 else []))

        x1_stored, lg_read, rank_read, tot_read = {}, {}, {}, {}
        LG, RANK, TOT = (4, 5), 6, 7
        c_e = pool.do(lambda e: e.iota(iota_e[:, :, :], [[0, NT], [1, NE]], base=0, channel_multiplier=0,
                                       allow_small_or_imprecise_dtypes=True), ring_free)
        c_tok = pool.do(lambda e: e.iota(tok[:, :], [[P, NT]], base=0, channel_multiplier=1,
                                         allow_small_or_imprecise_dtypes=True), ring_free)
        c_ti = pool.do(lambda e: e.iota(tile_iota[:, :], [[P, FT]], base=0, channel_multiplier=0,
                                        allow_small_or_imprecise_dtypes=True), ring_free)
        c_re = pool.do(lambda e: e.iota(region_e[:, :], [[REGION, NE]], base=0, channel_multiplier=0,
                                        allow_small_or_imprecise_dtypes=True), ring_free)
        c_valid = dve.do(lambda e: e.tensor_single_scalar(valid[:, :], tok[:, :], float(N), ALU.is_lt), [c_tok])
        c_below = dve.do(lambda e: e.tensor_scalar(below[:, :], iota_free[:, :], part[:, 0:1], None, ALU.is_gt),
                         ring_free)
        c_or = dve.do(lambda e: e.memset(ones_row[:, :], 1.0), ring_free)

        def tt(o, a, b, op, after):
            return dve.do(lambda e: e.tensor_tensor(o, a, b, op), after)

        def reduce_e(o, a, op, after):
            return dve.do(lambda e: e.tensor_reduce(o, a, AX.X, op), after)

        d_s = dma_marker("dispatched")

        def route(g):
            t = tiles(g)

            def per_tile(ap):
                return ap.rearrange("p (n a) -> p n a", a=1).broadcast_to([P, NG, NE])

            def per_expert(ap):
                return ap.rearrange("p (a h) -> p a h", a=1).broadcast_to([P, NG, NE])

            L3, P3, Q3, C3, IE = (z[:, t, :] for z in (lg, prob, eq, chosen, iota_e))
            TP = [top[:, i, t] for i in range(6)]
            last = g * NG + NG - 1
            m = lg_read[g] = tt(L3, bank[LG[g % 2]][:, 0:NG * NE].rearrange("p (n a) -> p n a", a=NE),
                                per_expert(br_row[:, :]), ALU.add, [lg_done[last], c_rows])
            yield
            m = reduce_e(TP[0], L3, ALU.max, [m])
            yield
            m = tt(L3, L3, per_tile(TP[0]), ALU.subtract, [m])
            m = act.do(lambda e: e.activation(P3, L3, ACT.Exp), [m])
            yield
            m = reduce_e(TP[1], P3, ALU.add, [m])
            yield
            m = dve.do(lambda e: e.reciprocal(TP[1], TP[1]), [m])
            yield
            m = tt(P3, P3, per_tile(TP[1]), ALU.mult, [m])
            for c in range(TOP):
                F3 = first[:, c, t, :]
                yield
                m = reduce_e(TP[2 + c], P3, ALU.max, [m])
                yield
                m = tt(Q3, P3, per_tile(TP[2 + c]), ALU.is_equal, [m])
                yield
                m = dve.do(lambda e, F3=F3: e.scalar_tensor_tensor(F3, IE, float(NE), Q3, ALU.subtract, ALU.mult),
                           [m, c_e])
                yield
                m = reduce_e(TP[4], F3, ALU.min, [m])
                yield
                m = dve.do(lambda e: e.tensor_single_scalar(TP[4], TP[4], float(NE), ALU.add), [m])
                if c == 0:
                    yield
                    m = dve.do(lambda e: e.tensor_copy(acc[:, t, FIRST_COL:FIRST_COL + 1].rearrange("p n a -> p (n a)"),
                                                       TP[4]), [m])
                yield
                m = tt(F3, IE, per_tile(TP[4]), ALU.is_equal, [m])
                if c == 0:
                    yield
                    m = dve.do(lambda e, F3=F3: e.scalar_tensor_tensor(P3, F3, -2.0, P3, ALU.mult, ALU.add), [m])
            yield
            k = tt(C3, first[:, 0, t, :], first[:, 1, t, :], ALU.add, [m])
            yield
            k = tt(C3, C3, per_tile(valid[:, t]), ALU.mult, [k, c_valid])
            flat = chosen[:, t, :].rearrange("p n a -> p (n a)")
            rank_done = pe.do(lambda e: e.matmul(bank[RANK][:, 0:NG * NE], below[:, :], flat, start=True, stop=True),
                              [k, c_below, scale_made] + ([rank_read[g - 1]] if g else []))
            tot_done = pe.do(lambda e: e.matmul(bank[TOT][:, 0:NG * NE], ones[:, :], flat, start=True, stop=True),
                             [k] + ([tot_read[g - 1]] if g else []))
            yield
            m = tt(TP[5], TP[2], TP[3], ALU.add, [m])
            yield
            m = dve.do(lambda e: e.reciprocal(TP[5], TP[5]), [m])
            for c in range(TOP):
                yield
                w = tt(acc[:, t, W_COL + c:W_COL + c + 1].rearrange("p n a -> p (n a)"), TP[2 + c], TP[5], ALU.mult, [m])
            yield
            w = dve.do(lambda e: e.tensor_copy(acc[:, t, TOKEN_COL:TOKEN_COL + 1].rearrange("p n a -> p (n a)"),
                                               tok[:, t]), [w, c_tok])
            yield
            m = tot_read[g] = dve.do(lambda e: e.tensor_copy(totals[:, t, :].rearrange("p n a -> p (n a)"),
                                                             bank[TOT][:, 0:NG * NE]), [tot_done])
            for ee in range(NE):
                before = upto[:, g * NG - 1, ee:ee + 1] if g else 0.0
                if ee % 2 == 0:
                    yield
                mm = dve.do(lambda e, ee=ee, before=before: e.tensor_tensor_scan(
                    upto[:, t, ee:ee + 1].rearrange("p n a -> p (n a)"), ones_row[:, 0:NG],
                    totals[:, t, ee:ee + 1].rearrange("p n a -> p (n a)"), before, ALU.mult, ALU.add),
                    [m, c_or] + ([counted[g - 1]] if g else []))
            counted[g] = mm
            PL = place[:, t, :]
            yield
            m = tt(PL, upto[:, t, :], totals[:, t, :], ALU.subtract, [mm])
            yield
            m = rank_read[g] = tt(PL, PL, bank[RANK][:, 0:NG * NE].rearrange("p (n a) -> p n a", a=NE), ALU.add,
                                  [m, rank_done])
            yield
            m = tt(PL, PL, per_expert(region_e[:, :]), ALU.add, [m, c_re])
            for c in range(TOP):
                yield
                m = tt(Q3, PL, first[:, c, t, :], ALU.mult, [m])
                yield
                m = reduce_e(TP[c], Q3, ALU.add, [m])
                yield
                m = dve.do(lambda e, c=c: e.tensor_copy(row_of[:, c, t], TP[c]), [m])
                for n in range(g * NG, (g + 1) * NG):
                    r = rows_of(n)
                    pool.dma(d_s, lambda e, n=n, c=c, r=r: e.indirect_dma_start(
                        out=expert_rows, out_offset=bass.IndirectOffsetOnAxis(ap=row_of[0:r, c, n:n + 1], axis=0),
                        in_=acc[0:r, n, 0:XROW], in_offset=None), [m, w, row_ready[n]])

        counted = {}

        def alternate(*makers):
            live = list(makers)
            while live:
                for one in list(live):
                    if next(one, live) is live:
                        live.remove(one)

        for g in range(GROUPS + 1):
            if g < GROUPS:
                resid_load(g)
            alternate(*([x1_stage(g)] if g < GROUPS else []), *([route(g - 1)] if g else []))
        mm = counted[GROUPS - 1]

        count = upto[:, NT - 1, :]
        m = dve.do(lambda e: e.tensor_single_scalar(ex[:, 0, :], count, float(P - 1), ALU.add), [mm])
        m = dve.do(lambda e: e.tensor_copy(ex_i[:, 0, :], ex[:, 0, :]), [m])
        m = dve.do(lambda e: e.tensor_single_scalar(ex_i[:, 1, :], ex_i[:, 0, :], 7, ALU.arith_shift_right), [m])
        m = dve.do(lambda e: e.tensor_copy(ex[:, 1, :], ex_i[:, 1, :]), [m])
        blank_known = tt(blank_row[:, :], count, region_e[:, :], ALU.add, [mm, c_re])
        ends = dve.do(lambda e: e.tensor_tensor_scan(ex[:, 2, :], ones_row[:, 0:NE], ex[:, 1, :], 0.0, ALU.mult,
                                                     ALU.add), [m])
        m = dve.do(lambda e: e.tensor_scalar(ex[:, 3, :], ex[:, 1, :], -float(P), float(REGION), ALU.mult, ALU.add), [ends])
        m = dve.do(lambda e: e.tensor_single_scalar(ex[:, 2, :], ex[:, 2, :], float(P), ALU.mult), [m])
        m = tt(cmp_e[:, :, :], tile_iota[:, :].rearrange("p (s a) -> p s a", a=1).broadcast_to([P, FT, NE]),
               ex[:, 2, :].rearrange("p (a h) -> p a h", a=1).broadcast_to([P, FT, NE]), ALU.is_ge, [m, c_ti, xf_turned[NT - 1], row_ready[NT - 1]])
        k = reduce_e(tile_e[:, :], cmp_e[:, :, :], ALU.add, [m])
        k = dve.do(lambda e: e.tensor_single_scalar(expert_of_tile_f[:, :], tile_e[:, :], float(NE - 1), ALU.min), [k])
        k = dve.do(lambda e: e.tensor_copy(expert_of_tile[:, :], expert_of_tile_f[:, :]), [k])
        m = tt(cmp_e[:, :, :], cmp_e[:, :, :], ex[:, 3, :].rearrange("p (a h) -> p a h", a=1)
               .broadcast_to([P, FT, NE]), ALU.mult, [k])
        m = reduce_e(tile_e[:, :], cmp_e[:, :, :], ALU.add, [m])
        experts_known = tt(row_of_tile[:, :], tile_e[:, :], tile_iota[:, :], ALU.add, [m])
        d_tail = dma_marker("region_tails_blanked")
        for ee in range(NE):
            def load_blank(e, ee=ee):
                _, values = nc.values_load_multi_w_load_instructions(
                    blank_row[0:1, ee:ee + 1], engines=[e.engine], min_val=ee * REGION, max_val=ee * REGION + N,
                    skip_runtime_bounds_check_because=IN_RANGE)
                reg["blank", ee] = values[0]
            sp.quiet(load_blank, [blank_known])
            sp.dma(d_tail, lambda e, ee=ee: e.dma_start(expert_rows[bass.ds(reg["blank", ee], P), :], blank[:, :]),
                   [spare_zero])
        dispatched = [d_s.mark(), d_tail.mark(), d_blank.mark()]
        placed = experts_known
        rank_done = rank_read[GROUPS - 1]

        d_w2 = dma_marker("w2_loaded")
        for ee in range(NE):
            w2_ready = sp.dma(d_w2, lambda e, ee=ee: e.dma_start(
                w2_all[:, ee, :, :], W2[ee].rearrange("(c p) d -> p c d", p=P)), [experts_known, row_ready[NT - 1]])
        d_v = dma_marker("expert_vectors_loaded")
        for to, of in ((g_all, ln_g), (bn_all, ln_b), (b1_all, b1), (b2_all, b2)):
            v_ready = sp.dma(d_v, lambda e, to=to, of=of: e.dma_start(
                to[:, :, :].rearrange("p e d -> p (e d)"),
                of.rearrange("e d -> (e d)").rearrange("(a n) -> a n", a=1).broadcast_to([P, of.shape[0] * of.shape[1]])),
                dispatched)

        d_xs = [dma_marker(f"expert_rows_loaded{i}") for i in range(XR)]
        d_y = dma_marker("out_added")
        XT, HB, TB, YB = 0, (1, 2, 3, 4), (5, 6), 7
        loaded, gone, xe_made, xeT_made, turned, h_done, h_biased, h_act, hT_turned, hT_made, y_done, y_made, y_sent = (
            {} for _ in range(13))
        ereg, gate_made = {}, {}
        EL = 4

        def expert_regs(stream, name, s):
            if s % EL == 0:
                def go(e):
                    hi = min(s + EL, FT)
                    _, values = nc.values_load_multi_w_load_instructions(
                        expert_of_tile[0:1, s:hi], engines=[e.engine], min_val=0, max_val=NE - 1,
                        skip_runtime_bounds_check_because=IN_RANGE)
                    for i in range(s, hi):
                        ereg[name, i] = values[i - s]
                stream.quiet(go, [experts_known])

        def f_load(s):
            after = dispatched + ([y_made[s - XR]] if s >= XR else [])
            if s % EL == 0:
                def go(e):
                    hi = min(s + EL, FT)
                    _, values = nc.values_load_multi_w_load_instructions(
                        row_of_tile[0:1, s:hi], engines=[e.engine], min_val=0, max_val=NE * REGION + (SPARE_TILES - 1) * P,
                        skip_runtime_bounds_check_because=IN_RANGE)
                    for i in range(s, hi):
                        ereg["row", i] = values[i - s]
                sp.quiet(go, [experts_known])
            loaded[s] = sp.dma(d_xs[s % XR], lambda e: e.dma_start(
                xs[:, s % XR, :], expert_rows[bass.ds(ereg["row", s], P), :]), after)

        def f_input(s):
            q = s % 2
            expert_regs(dve, "dve", s)
            three = lambda t: t.rearrange("p (a d) -> p a d", a=1)
            m = dve.do(lambda e: e.tensor_tensor(three(xe[:, q, :]), three(xs[:, s % XR, 0:D]),
                                                 g_all[:, bass.ds(ereg["dve", s], 1), :], ALU.mult),
                       [loaded[s], v_ready] + ([turned[s - 2]] if s >= 2 else []))
            gone[s] = dve.do(lambda e: e.tensor_copy(token_id[:, s % XR:s % XR + 1],
                                                     xs[:, s % XR, TOKEN_COL:TOKEN_COL + 1]),
                             [loaded[s]] + ([y_sent[s - XR]] if s >= XR else []))
            for c, op in enumerate((ALU.is_equal, ALU.not_equal)):
                made = dve.do(lambda e, c=c, op=op: e.tensor_scalar(
                    gate[:, s % XR, c:c + 1], xs[:, s % XR, FIRST_COL:FIRST_COL + 1], expert_of_tile_f[:, s:s + 1],
                    xs[:, s % XR, W_COL + c:W_COL + c + 1], op, ALU.mult),
                    [loaded[s], experts_known] + ([y_made[s - XR]] if s >= XR else []))
            xe_made[s] = dve.do(lambda e: e.tensor_tensor(three(xe[:, q, :]), three(xe[:, q, :]),
                                                          bn_all[:, bass.ds(ereg["dve", s], 1), :], ALU.add), [m])
            gate_made[s] = dve.do(lambda e: e.tensor_tensor(gate[:, s % XR, 2:3], gate[:, s % XR, 0:1],
                                                            gate[:, s % XR, 1:2], ALU.add), [made])

        def f_input_turn(s):
            q = s % 2
            for k in range(KD):
                turned[s] = pe.do(lambda e, k=k: e.transpose(bank[XT][:, k * P:(k + 1) * P],
                                                             xe[:, q, k * P:(k + 1) * P], ident[:, :]),
                                  [xe_made[s]] + ([xeT_made[s - 1]] if s else [rank_done, placed]))
            xeT_made[s] = act.do(lambda e: e.activation(xeT[:, q, :, :].rearrange("p k m -> p (k m)"),
                                                        bank[XT][:, 0:D], ACT.Copy),
                                 [turned[s]] + ([h_done[s - 2, 1]] if s >= 2 else []))

        def f_hidden(s):
            q = s % 2
            expert_regs(pe, "pe", s)
            for h in range(2):
                i = 2 * s + h
                bk = bank[HB[i % 4]]
                for k in range(KD):
                    h_done[s, h] = pe.do(lambda e, k=k, h=h, bk=bk: e.matmul(
                        bk[:, :], xeT[:, q, k, :],
                        w1_all[:, k, bass.ds(ereg["pe", s], 1), h * HALF:(h + 1) * HALF],
                        start=(k == 0), stop=(k == KD - 1)),
                        [xeT_made[s], w1_ready] + ([h_biased[(i - 4) // 2, h]] if i >= 4 else []))
                h_biased[s, h] = dve.do(lambda e, h=h, i=i, bk=bk: e.tensor_tensor(
                    hid[:, i % HR, :].rearrange("p (a n) -> p a n", a=1), bk[:, :].rearrange("p (a n) -> p a n", a=1),
                    b1_all[:, bass.ds(ereg["dve", s], 1), h * HALF:(h + 1) * HALF], ALU.add),
                    [h_done[s, h], v_ready] + ([hT_turned[(i - HR) // 2, (i - HR) % 2]] if i >= HR else []))
                h_act[s, h] = act.do(lambda e, i=i: e.activation(hid[:, i % HR, :], hid[:, i % HR, :], ACT.Gelu),
                                     [h_biased[s, h]])

        def f_turn(s, h):
            i = 2 * s + h
            tb = bank[TB[h]]
            for c in range(4):
                hT_turned[s, h] = pe.do(lambda e, c=c: e.transpose(
                    tb[:, c * P:(c + 1) * P], hid[:, i % HR, c * P:(c + 1) * P], ident[:, :]),
                    [h_act[s, h]] + ([hT_made[s - 1, h]] if s else []))
            hT_made[s, h] = act.do(lambda e: e.activation(hT[:, h, :, :].rearrange("p c m -> p (c m)"), tb[:, :],
                                                          ACT.Copy),
                                   [hT_turned[s, h]] + ([y_done[s - 1, h]] if s else [w2_ready]))

        def f_output(s, h):
            q = s % 2
            for c in range(4):
                y_done[s, h] = pe.do(lambda e, c=c: e.matmul(
                    bank[YB][:, 0:D], hT[:, h, c, :],
                    w2_all[:, bass.ds(ereg["pe", s], 1), 4 * h + c, :],
                    start=(h == 0 and c == 0), stop=(h == 1 and c == 3)),
                    [hT_made[s, h], w2_ready] + ([y_made[s - 1]] if s else []))

        def f_finish(s):
            q = s % 2
            m = dve.do(lambda e: e.tensor_tensor(
                y[:, q, :].rearrange("p (a d) -> p a d", a=1),
                bank[YB][:, 0:D].rearrange("p (a d) -> p a d", a=1),
                b2_all[:, bass.ds(ereg["dve", s], 1), :], ALU.add), [y_done[s, 1]] + ([y_sent[s - 2]] if s >= 2 else []))
            y_made[s] = dve.do(lambda e: e.tensor_scalar(y[:, q, :], y[:, q, :], gate[:, s % XR, 2:3], None, ALU.mult),
                               [m, gate_made[s]])
            y_sent[s] = pool.dma(d_y, lambda e: e.indirect_dma_start(
                out=out, out_offset=bass.IndirectOffsetOnAxis(ap=token_id[:, s % XR:s % XR + 1], axis=0),
                in_=y[:, q, :], in_offset=None, compute_op=ALU.add),
                [y_made[s], gone[s], d_o.mark(), spare_zero] + ([y_sent[s - 1]] if s else []))

        AHEAD = 3
        for s in range(AHEAD):
            f_load(s)
        f_input(0)
        f_input_turn(0)
        f_input(1)
        for s in range(FT + 1):
            if s + AHEAD < FT:
                f_load(s + AHEAD)
            if s < FT:
                f_hidden(s)
                if s + 1 < FT:
                    f_input_turn(s + 1)
                if s + 2 < FT:
                    f_input(s + 2)
            if s:
                f_output(s - 1, 0)
                f_output(s - 1, 1)
                f_finish(s - 1)
            if s < FT:
                f_turn(s, 0)
                f_turn(s, 1)

        sp.quiet(lambda e: None, [m_.mark() for m_ in dmas if m_.count])

        block = ctx.enter_context(nc.Block())

        @block.sync
        def _(e):
            sp.play(e)

        @block.gpsimd
        def _(e):
            pool.play(e)

        @block.scalar
        def _(e):
            act.play(e)

        @block.vector
        def _(e):
            dve.play(e)

        @block.tensor
        def _(e):
            pe.play(e)


INPUTS = ["x", "src", "dst", "L0_gnn_W", "L0_gnn_att_src", "L0_gnn_att_dst", "L0_gnn_bias", "L0_gnn_gamma",
          "L0_gnn_beta", "L0_ffn_Wr", "L0_ffn_br", "L0_ffn_ln_g", "L0_ffn_ln_b", "L0_ffn_W1", "L0_ffn_b1",
          "L0_ffn_W2", "L0_ffn_b2"]


def kernel(**inputs):
    import numpy as _np
    import concourse.bacc as _bacc
    from concourse import mybir as _mybir
    from concourse.bass_utils import run_bass_kernel_spmd as _run

    nc = _bacc.Bacc("TRN2", target_bir_lowering=False, num_devices=1)
    arrays, args = {}, []
    for name in INPUTS:
        a = _np.ascontiguousarray(inputs[name])
        arrays[f"in_{name}"] = a
        args.append(nc.dram_tensor(f"in_{name}", a.shape, _mybir.dt.from_np(a.dtype), kind="ExternalInput").ap())
    n, d = inputs["x"].shape
    args.append(nc.dram_tensor("out_rows", (n + 128, d), _mybir.dt.float32, kind="ExternalOutput").ap())
    build_gnn_moe(nc, *args)
    r = _run(nc, [arrays], core_ids=[0])
    return r.results[0]["out_rows"][:n]
```

```python
from contextlib import ExitStack

import numpy as np

import concourse.bass as bass
from concourse import mybir

ALU = mybir.AluOpType
ACT = mybir.ActivationFunctionType
AX = mybir.AxisListType
F32 = mybir.dt.float32
I32 = mybir.dt.int32
F16 = mybir.dt.float16
P = 128
NEG_SLOPE = 0.2
EPS = 1e-5
IN_RANGE = "the value is worked out on the chip within the shapes' bounds, whatever the data"


def ceil_div(a, b):
    return -(-a // b)


class Marker:

    def __init__(self, sem):
        self.sem, self.count = sem, 0

    def mark(self):
        return (self.sem, self.count)


class Stream(Marker):

    def __init__(self, sem):
        super().__init__(sem)
        self.steps = []

    def do(self, fn, after=()):
        self.count += 1
        self.steps.append((tuple(after), fn, self.sem, 1))
        return self.mark()

    def quiet(self, fn, after=()):
        self.steps.append((tuple(after), fn, None, 0))

    def dma(self, marker, fn, after=()):
        marker.count += 16
        self.steps.append((tuple(after), fn, marker.sem, 16))
        return marker.mark()

    def play(self, engine):
        passed = {}
        for after, fn, sem, step in self.steps:
            for item in after:
                waited, value = item() if callable(item) else item
                if passed.get(id(waited), 0) < value:
                    engine.wait_ge(waited, value)
                    passed[id(waited)] = value
            made = fn(engine)
            if sem is not None:
                made.then_inc(sem, step)


def build_gnn_moe(nc, x, src, dst, W, att_src, att_dst, bias, gamma, beta,
                  Wr, br, ln_g, ln_b, W1, b1, W2, b2, out):
    N, D = x.shape
    HEADS, DH = att_src.shape
    E = src.shape[0]
    NE, _, HID = W1.shape
    KD = D // P
    KH = HID // P
    NT = ceil_div(N, P)
    LAST = N - (NT - 1) * P
    ET = ceil_div(E, P)
    SLOT_GROUPS = ceil_div(ET + NT, P)
    SLOTS_UP = SLOT_GROUPS * P
    EB = 8
    SLOTS = ceil_div(ET + NT - 1, EB) * EB
    BATCHES = SLOTS // EB
    assert ET + 1 <= SLOTS_UP and SLOTS <= SLOTS_UP and SLOTS - ET <= NT
    ROW = D + HEADS
    PICK = 2 * HEADS
    TOP = 2
    SAFE_RANGE = 60.0
    FAR_BELOW = -1e38
    FT = (N * TOP - NE) // P + NE
    XROW = D + 4
    W_COL, TOKEN_COL, FIRST_COL = D, D + 2, D + 3
    REGION = (NT + 1) * P
    SPARE_TILES = FT - N * TOP // P

    node_table = nc.dram_tensor("node_table", (N, ROW), F32, kind="Internal").ap()
    resid_rows = nc.dram_tensor("resid_rows", (NT * P, D), F32, kind="Internal").ap()
    src_pad = nc.dram_tensor("src_pad", (SLOTS_UP, P), I32, kind="Internal").ap()
    dst_pad = nc.dram_tensor("dst_pad", (SLOTS_UP, P), I32, kind="Internal").ap()
    segment_max = nc.dram_tensor("segment_max", ((NT + 1) * P, HEADS), F32, kind="Internal").ap()
    expert_rows = nc.dram_tensor("expert_rows", (NE * REGION + SPARE_TILES * P, XROW), F32, kind="Internal").ap()

    with ExitStack() as ctx:
        def sem(name):
            return ctx.enter_context(nc.semaphore(name))

        base = nc.sbuf_base + (-nc.sbuf_base) % 32

        class Region:
            def __init__(self, start):
                self.at = start

            def take(self, name, shape, dt=F32):
                t = nc.alloc_sbuf_tensor_at(name, list(shape), dt, offset=self.at)
                self.at += ceil_div(int(np.prod(shape[1:])) * (2 if dt == F16 else 4), 32) * 32
                assert self.at <= nc.sbuf_usable_end, name
                return t

        small = Region(base)
        ident = small.take("ident", [P, P])
        part = small.take("part", [P, 1])
        eps = small.take("eps", [P, 1])
        wide_flag = small.take("wide_flag", [P, 1], I32)
        expert_of_tile = small.take("expert_of_tile", [P, FT], I32)
        expert_of_tile_f = small.take("expert_of_tile_f", [P, FT])
        row_of_tile = small.take("row_of_tile", [P, FT], I32)
        blank_row = small.take("blank_row", [P, NE], I32)
        iota_free = small.take("iota_free", [P, P])
        ones = small.take("ones", [P, P])
        blank = small.take("blank", [P, XROW])
        B1_COL, G_COL, LB_COL = 0, KH, KH + KD
        PRE_COL, HS_COL, Y_COL, COLS = KH + 2 * KD, KH + 2 * KD + 1, KH + 2 * KD + 2, KH + 2 * KD + 3
        VECS = NE * (KH + 2 * KD)
        assert VECS <= P
        vec_rows = small.take("vec_rows", [P, P])
        vecs = small.take("vecs", [P, VECS])
        expert_cols = small.take("expert_cols", [P, NE, COLS])
        vec_max = small.take("vec_max", [P, 3, NE])
        vec_top = small.take("vec_top", [P, 3, NE])
        w_max = small.take("w_max", [P, 2, NE])
        w_top = small.take("w_top", [P, 2, NE])
        piece_max = small.take("piece_max", [P, 4])
        x_bound = small.take("x_bound", [P, NE])
        h_bound = small.take("h_bound", [P, NE])
        scale = small.take("scale", [P, 4, NE], I32)
        unscale = small.take("unscale", [P, 4, NE], I32)
        exponent = small.take("exponent", [P, 4, NE], I32)

        region_acc = Region(small.at)
        acc = region_acc.take("acc", [P, NT + 1, ROW])
        XR, CR = 5, 4
        ffn = Region(small.at)
        b2_all = ffn.take("b2_all", [P, NE, D])
        xs = ffn.take("xs", [P, XR, XROW])
        xe = ffn.take("xe", [P, 2, KD, P])
        xe_hi = ffn.take("xe_hi", [P, 2, KD, P], F16)
        xe_lo = ffn.take("xe_lo", [P, 2, KD, P], F16)
        HR = 3
        hid = ffn.take("hid", [P, HR, KH // 2, P])
        hid_hi = ffn.take("hid_hi", [P, 2, KH, P], F16)
        hid_lo = ffn.take("hid_lo", [P, 2, KH, P], F16)
        y = ffn.take("y", [P, 2, D])
        token_id = ffn.take("token_id", [P, XR], I32)
        gate = ffn.take("gate", [P, XR, 3])
        cols = ffn.take("cols", [P, CR, COLS])
        w2_stage_b = ffn.take("w2_stage_b", [P, 2, KH, D])
        assert ffn.at <= region_acc.at
        region_w1 = Region(region_acc.at)
        w1_hi = region_w1.take("w1_hi", [P, KD, NE, HID], F16)
        w1_lo = region_w1.take("w1_lo", [P, KD, NE, HID], F16)
        region_w2 = Region(region_w1.at)
        w2_hi = region_w2.take("w2_hi", [P, NE, KH, D], F16)
        w2_lo = region_w2.take("w2_lo", [P, NE, KH, D], F16)
        w2_end = region_w2.at

        early = Region(region_w1.at)
        src_slot = early.take("src_slot", [P, SLOTS_UP], I32)
        dst_slot = early.take("dst_slot", [P, SLOTS_UP])
        pick = early.take("pick", [P, NT + 1, PICK])
        ln_stats = early.take("ln_stats", [P, NT, 2])
        rstd = early.take("rstd", [P, NT])
        node_tile_row = early.take("node_tile_row", [P, SLOTS_UP], I32)
        w1_stage = early.take("w1_stage", [P, KD, HID])
        GB = 4
        early_b = early.at
        gather_ring = early.take("gather_ring", [P, GB, EB, ROW])
        OHB = 3
        onehot = early.take("onehot", [P, OHB, EB, P])
        onehotT = early.take("onehotT", [P, 1, EB, P])
        zbuf = early.take("zbuf", [P, 2, EB, HEADS])
        assert early.at <= nc.sbuf_usable_end

        s1 = Region(early_b)
        iota_slot = s1.take("iota_slot", [P, SLOTS_UP])
        above = s1.take("above", [P, SLOTS_UP])
        raw_idx = s1.take("raw_idx", [P, 4, P], I32)
        raw_f = s1.take("raw_f", [P, 2, P])
        x_ring = 8
        s1w = Region(region_acc.at)
        xt = s1w.take("xt", [P, x_ring, D])
        xn = s1w.take("xn", [P, x_ring, D])
        rt = s1w.take("rt", [P, x_ring, D])
        xnT = s1w.take("xnT", [P, 2, KD, P])
        w_ext = s1w.take("w_ext", [P, KD, D + PICK])
        att_rows = s1w.take("att_rows", [P, 2, D])
        w_att = s1w.take("w_att", [P, KD, 2, D])
        st6 = s1w.take("st6", [P, x_ring, 6])
        beta_row = s1w.take("beta_row", [P, D])
        own = s1w.take("own", [P, NT, HEADS])
        own2 = s1w.take("own2", [P, NT, HEADS])
        max_src = s1w.take("max_src", [P, 2, HEADS])
        max_all = s1w.take("max_all", [P, 2, HEADS])
        src_range = s1w.take("src_range", [P, HEADS])
        wide = s1w.take("wide", [P, 2])
        m_col = s1w.take("m_col", [P, 3], I32)
        m_to = s1w.take("m_to", [P, 2], I32)
        m_to_f = s1w.take("m_to_f", [P, 4])
        m_row = s1w.take("m_row", [P, 2, P], I32)
        m_row_f = s1w.take("m_row_f", [P, 2, P])
        m_reset = s1w.take("m_reset", [P, 1 + P])
        spare_row = s1w.take("spare_row", [P, 1])
        m_rows = s1w.take("m_rows", [P, ROW])
        m_scan = s1w.take("m_scan", [P, P])
        m_carry = s1w.take("m_carry", [P, 1])
        m_out = s1w.take("m_out", [P, HEADS])
        m_table = s1w.take("m_table", [P, NT, HEADS])
        last_dst = s1w.take("last_dst", [P, SLOT_GROUPS], I32)
        last_tile = s1w.take("last_tile", [P, SLOT_GROUPS], I32)
        key = s1w.take("key", [P, SLOT_GROUPS])
        tile_no = s1w.take("tile_no", [P, SLOT_GROUPS])
        edge_tile = s1w.take("edge_tile", [P, SLOT_GROUPS])
        edge_tile_i = s1w.take("edge_tile_i", [P, SLOT_GROUPS], I32)
        slot_base = s1w.take("slot_base", [P, SLOT_GROUPS])
        pad_src = s1w.take("pad_src", [P, P], I32)
        pad_dst = s1w.take("pad_dst", [P, P], I32)

        s3 = Region(region_w1.at)
        NG = 7
        assert NT % NG == 0
        GROUPS = NT // NG
        square = s3.take("square", [P, 2, NG, D])
        col = s3.take("col", [P, 6, D])
        bias_row, gamma_row, mean_row, scale_row, sd_row = (col[:, i, :] for i in range(5))
        r_ring = s3.take("r_ring", [P, 2, NG, D])
        bn6 = s3.take("bn6", [P, NG, 6])
        mv = s3.take("mv", [P, NT, 2])
        sd1 = s3.take("sd1", [P, NT])
        rs1 = s3.take("rs1", [P, NT])
        v2 = s3.take("v2", [P, NT])
        sd2 = s3.take("sd2", [P, NT])
        rs2 = s3.take("rs2", [P, NT])
        FR = 4
        shared = Region(s3.at)
        xf = s3.take("xf", [P, FR, D])
        xfT = s3.take("xfT", [P, FR, KD, P])
        wr = s3.take("wr", [P, KD, NE])
        br_row = s3.take("br_row", [P, NE])
        lg = s3.take("lg", [P, NT, NE])
        prob = s3.take("prob", [P, NT, NE])
        eq = s3.take("eq", [P, NT, NE])
        first = s3.take("first", [P, 2, NT, NE])
        iota_e = s3.take("iota_e", [P, NT, NE])
        tok = s3.take("tok", [P, NT])
        valid = s3.take("valid", [P, NT])
        top = s3.take("top", [P, 6, NT])
        chosen = s3.take("chosen", [P, NT, NE])
        below = s3.take("below", [P, P])
        totals = s3.take("totals", [P, NT, NE])
        upto = s3.take("upto", [P, NT, NE])
        place = s3.take("place", [P, NT, NE])
        ones_row = s3.take("ones_row", [P, NT])
        ex = s3.take("ex", [P, 6, NE])
        ex_i = s3.take("ex_i", [P, 2, NE], I32)
        cmp_e = shared.take("cmp_e", [P, FT, NE])
        region_e = s3.take("region_e", [P, NE])
        tile_e = s3.take("tile_e", [P, FT])
        tile_iota = s3.take("tile_iota", [P, FT])
        tail = Region(w2_end)
        assert s3.at <= w2_end
        row_of = tail.take("row_of", [P, 2, NT], I32)
        w2_stage_a = tail.take("w2_stage_a", [P, 2, KH, D])
        assert FT * NE <= FR * D

        bank = [ctx.enter_context(nc.psum_tensor(f"bank{i}", [P, 512], F32)) for i in range(8)]

        pe, dve, act, pool, sp = (Stream(sem(f"{n}_steps")) for n in ("pe", "dve", "act", "pool", "sp"))
        dmas = []

        def dma_marker(name):
            m = Marker(sem(name))
            dmas.append(m)
            return m

        c_iota = pool.do(lambda e: e.iota(iota_free[:, :], [[1, P]], base=0, channel_multiplier=0,
                                          allow_small_or_imprecise_dtypes=True))
        c_part = pool.do(lambda e: e.iota(part[:, :], [[0, 1]], base=0, channel_multiplier=1,
                                          allow_small_or_imprecise_dtypes=True))
        c_slot = pool.do(lambda e: e.iota(iota_slot[:, :], [[1, SLOTS_UP]], base=0, channel_multiplier=0,
                                          allow_small_or_imprecise_dtypes=True))
        c_tileno = pool.do(lambda e: e.iota(tile_no[:, :], [[P, SLOT_GROUPS]], base=0, channel_multiplier=1,
                                            allow_small_or_imprecise_dtypes=True))
        c_pads = pool.do(lambda e: e.memset(pad_src[:, :], 0))
        c_padd = pool.do(lambda e: e.memset(pad_dst[:, :], (NT + 1) * P))
        c_blank = pool.do(lambda e: e.memset(blank[:, :], 0.0))
        c_ones = dve.do(lambda e: e.memset(ones[:, :], 1.0))
        c_eps = dve.do(lambda e: e.memset(eps[:, :], EPS))
        c_ident = dve.do(lambda e: e.tensor_scalar(ident[:, :], iota_free[:, :], part[:, 0:1], None, ALU.is_equal),
                         [c_iota, c_part])
        m = dve.do(lambda e: e.tensor_scalar(blank[:, TOKEN_COL:TOKEN_COL + 1], part[:, 0:1], float(N), None, ALU.add),
                   [c_part, c_blank])
        c_blank = m
        c_acc = dve.do(lambda e: e.memset(acc[:, NT, :], 0.0))
        c_pick = dve.do(lambda e: e.memset(pick[:, NT, :], 0.0))
        c_xlast = dve.do(lambda e: e.memset(xt[:, (NT - 1) % x_ring, :], 0.0))

        d_edge = dma_marker("edge_lists_padded")
        full = (ET - 1) * P
        for raw, padded, pad in ((src, src_pad, pad_src), (dst, dst_pad, pad_dst)):
            sp.dma(d_edge, lambda e, raw=raw, padded=padded: e.dma_start(
                padded[0:ET - 1, :], raw[0:full].rearrange("(t p) -> t p", p=P)))
            sp.dma(d_edge, lambda e, raw=raw, padded=padded: e.dma_start(
                padded[ET - 1:ET, 0:E - full], raw[full:E].rearrange("(t p) -> t p", t=1)))
            if E - full < P:
                sp.dma(d_edge, lambda e, padded=padded, pad=pad: e.dma_start(
                    padded[ET - 1:ET, E - full:P], pad[0:1, E - full:P]), [c_pads, c_padd])
            sp.dma(d_edge, lambda e, padded=padded, pad=pad: e.dma_start(
                padded[ET:SLOTS_UP, :], pad[0:SLOTS_UP - ET, :]), [c_pads, c_padd])
        edges_padded = d_edge.mark()

        d_w = dma_marker("stage1_weights")
        act.dma(d_w, lambda e: e.dma_start(w_ext[:, :, 0:D], W.rearrange("(k p) n -> p k n", p=P)))
        for i, a in enumerate((att_src, att_dst)):
            act.dma(d_w, lambda e, i=i, a=a: e.dma_start(
                att_rows[:, i, :], a.rearrange("h d -> (h d)").rearrange("(a n) -> a n", a=1).broadcast_to([P, D])))
        act.dma(d_w, lambda e: e.dma_start(beta_row[:, :], beta.rearrange("(a n) -> a n", a=1).broadcast_to([P, D])))
        w_loaded = d_w.mark()
        d_vec = dma_marker("vectors_loaded")
        for at, of in ((0, b1), (NE * KH, ln_g), (NE * (KH + KD), ln_b)):
            n = NE * of.shape[1] // P
            act.dma(d_vec, lambda e, at=at, of=of, n=n: e.dma_start(
                vec_rows[at:at + n, :], of.rearrange("x (c p) -> (x c) p", p=P)))

        d_last = dma_marker("last_dst_loaded")
        last_loaded = sp.dma(d_last, lambda e: e.dma_start(
            last_dst[:, :].rearrange("p (c a) -> p c a", a=1),
            dst_pad.rearrange("(c p) k -> p c k", p=P)[:, :, P - 1:P], allow_slow_non_contiguous=True), [edges_padded])

        d_blank = dma_marker("blanks_written")

        def write_blanks():
            for f in range(SPARE_TILES):
                act.dma(d_blank, lambda e, f=f: e.dma_start(
                    expert_rows[NE * REGION + f * P:NE * REGION + (f + 1) * P, :], blank[:, :]), [c_blank])
            return act.dma(d_blank, lambda e: e.dma_start(out[N:N + P, :], blank[:, 0:D]), [c_blank])

        for k in range(KD):
            for i in range(2):
                m = dve.do(lambda e, k=k, i=i: e.tensor_tensor(w_att[:, k, i, :], w_ext[:, k, 0:D], att_rows[:, i, :],
                                                               ALU.mult), [w_loaded])
        w_folded = dve.do(lambda e: e.tensor_reduce(
            w_ext[:, :, D:D + PICK].rearrange("p k (i h) -> p k i h", i=2),
            w_att[:, :, :, :].rearrange("p k i (h d) -> p k i h d", d=DH), AX.X, ALU.add), [m])

        d_x = [dma_marker(f"x_loaded{i}") for i in range(x_ring // 2)]
        d_t = dma_marker("node_table_written")
        d_r = [dma_marker(f"resid_written{i}") for i in range(x_ring // 2)]
        xn_made, resid_made, xnT_ready, rows_done, tr_done, table_marks = {}, {}, {}, {}, {}, None
        beta_added, sd_made, stat_made, acc_copied, x_marks, resid_marks = {}, {}, {}, {}, {}, {}

        def rows_of(n):
            return LAST if n == NT - 1 else P

        def pair_of(n):
            return [n] if n + 1 == NT else [n, n + 1]

        def both(dram, ring, pair):
            n, k = pair[0], len(pair)
            if rows_of(pair[-1]) < P:
                return dram[n * P:n * P + LAST, :], ring[0:LAST, n % x_ring, :]
            return (dram[n * P:(n + k) * P, :].rearrange("(k p) d -> p k d", p=P),
                    ring[:, n % x_ring:n % x_ring + k, :])

        def s1_load(pair):
            after = [c_xlast]
            for n in pair:
                if n >= x_ring:
                    after += [xn_made[n - x_ring], beta_added[n - x_ring]]
            of, to = both(x, xt, pair)
            mark = sp.dma(d_x[pair[0] % x_ring // 2], lambda e: e.dma_start(to, of), after)
            for n in pair:
                x_marks[n] = mark

        def s1_stats(n):
            j = n % x_ring
            m = dve.do(lambda e: e.bn_stats(st6[:, j, :], xt[:, j, :]), [x_marks[n], c_xlast])
            beta_added[n] = pool.do(lambda e: e.tensor_tensor(rt[:, j, :], xt[:, j, :], beta_row[:, :], ALU.add),
                                    [x_marks[n], c_xlast, w_loaded] + ([resid_marks[n - x_ring]] if n >= x_ring else []))
            stat_made[n] = dve.do(lambda e: e.bn_aggr(ln_stats[:, n, :], st6[:, j, :]), [m])
            sd_made[n] = act.do(lambda e: e.activation(rstd[:, n:n + 1], ln_stats[:, n, 1:2], ACT.Sqrt, bias=eps[:, :]),
                                [stat_made[n], c_eps])

        def s1_norm(n):
            j = n % x_ring
            m = dve.do(lambda e: e.reciprocal(rstd[:, n:n + 1], rstd[:, n:n + 1]), [sd_made[n]])
            after = [m, stat_made[n]]
            if n >= x_ring:
                after += [tr_done[n - x_ring], resid_made[n - x_ring]]
            xn_made[n] = dve.do(lambda e: e.tensor_scalar(xn[:, j, :], xt[:, j, :], ln_stats[:, n, 0:1],
                                                          rstd[:, n:n + 1], ALU.subtract, ALU.mult), after)

        def s1_resid(n):
            j = n % x_ring
            resid_made[n] = dve.do(lambda e: e.tensor_tensor(rt[:, j, :], rt[:, j, :], xn[:, j, :], ALU.add),
                                   [xn_made[n], beta_added[n]])

        def s1_turn(n):
            j, q = n % x_ring, n % 2
            after = [xn_made[n], c_ident] + ([xnT_ready[n - 2]] if n >= 2 else [])
            for k in range(KD):
                tr_done[n] = pe.do(lambda e, k=k: e.transpose(bank[q][:, k * P:(k + 1) * P],
                                                              xn[:, j, k * P:(k + 1) * P], ident[:, :]), after)
            after = [tr_done[n]] + ([rows_done[n - 2]] if n >= 2 else [])
            xnT_ready[n] = act.do(lambda e: e.activation(xnT[:, q, :, :].rearrange("p k m -> p (k m)"),
                                                         bank[q][:, 0:D], ACT.Copy), after)

        def s1_product(n):
            q = n % 2
            after = [xnT_ready[n], w_folded] + ([acc_copied[n - 3][0], acc_copied[n - 3][1]] if n >= 3 else [])
            for k in range(KD):
                rows_done[n] = pe.do(lambda e, k=k: e.matmul(bank[2 + n % 3][:, 0:D + PICK], xnT[:, q, k, :], w_ext[:, k, :],
                                                             start=(k == 0), stop=(k == KD - 1)), after)

        def s1_keep(n):
            q = n % 2
            a = act.do(lambda e: e.activation(acc[:, n, :], bank[2 + n % 3][:, 0:ROW], ACT.Copy), [rows_done[n]])
            b = act.do(lambda e: e.activation(pick[:, n, 0:HEADS], bank[2 + n % 3][:, ROW:D + PICK], ACT.Copy),
                       [a])
            acc_copied[n] = (a, b)

        def s1_store(pair):
            n, k = pair[0], len(pair)
            of, to = rt[:, n % x_ring:n % x_ring + k, :], resid_rows[n * P:(n + k) * P, :].rearrange("(k p) d -> p k d", p=P)
            mark = sp.dma(d_r[n % x_ring // 2], lambda e: e.dma_start(to, of), [resid_made[m] for m in pair])
            for m in pair:
                resid_marks[m] = mark
            r = rows_of(pair[-1])
            rows, table = acc[0:r, n, :], node_table[n * P:(n + k - 1) * P + r, :]
            if k == 2:
                rows, table = acc[:, n:n + 2, :], table.rearrange("(k p) d -> p k d", p=P)
            sp.dma(d_t, lambda e: e.dma_start(table, rows), [acc_copied[m][0] for m in pair])

        d_raw = [dma_marker(f"slot_rows{i}") for i in range(4)]

        tables = {}
        SLOT_TURN = (7, 5)

        def slot_count(c):
            if c == 0:
                m = dve.do(lambda e: e.tensor_single_scalar(last_tile[:, :], last_dst[:, :], 7, ALU.arith_shift_right),
                           [last_loaded])
                m = dve.do(lambda e: e.tensor_copy(key[:, :], last_tile[:, :]), [m])
                m = dve.do(lambda e: e.scalar_tensor_tensor(key[:, :], key[:, :], float(NT - 1), tile_no[:, :],
                                                            ALU.min, ALU.add), [m, c_tileno])
                m = dve.do(lambda e: e.tensor_scalar(above[:, :], iota_slot[:, :], key[:, 0:1], None, ALU.is_gt),
                           [m, c_slot])
            else:
                m = dve.do(lambda e: e.scalar_tensor_tensor(above[:, :], iota_slot[:, :], key[:, c:c + 1],
                                                            above[:, :], ALU.is_gt, ALU.add), [tables["counted"]])
            tables["counted"] = m

        hw = SLOTS_UP // 2

        def slot_sums():
            for g in range(SLOT_GROUPS):
                tables["parts"] = pe.do(lambda e, g=g: e.matmul(
                    bank[7][:, g:g + 1], above[:, g * P:(g + 1) * P], ones[:, 0:1], start=True, stop=True),
                    [tables["counted"], c_ones])
            for h in range(2):
                tables["row"] = pe.do(lambda e, h=h: e.matmul(
                    bank[5 + h][:, 0:hw], ones[:, :], above[:, h * hw:(h + 1) * hw], start=True, stop=True), [])

        def slot_keys():
            t_part, t_row = tables["parts"], tables["row"]
            a = dve.do(lambda e: e.tensor_copy(edge_tile_i[:, :], bank[7][:, 0:SLOT_GROUPS]), [t_part])
            b = dve.do(lambda e: e.tensor_tensor(slot_base[:, :], tile_no[:, :], bank[7][:, 0:SLOT_GROUPS],
                                                 ALU.subtract), [t_part])
            for h in range(2):
                row_made = dve.do(lambda e, h=h: e.tensor_tensor(
                    node_tile_row[:, h * hw:(h + 1) * hw], iota_slot[:, h * hw:(h + 1) * hw], bank[5 + h][:, 0:hw],
                    ALU.subtract), [t_row])
            b = dve.do(lambda e: e.tensor_single_scalar(slot_base[:, :], slot_base[:, :], float(P), ALU.mult), [b])
            tables["keys"] = (row_made, a, b)

        def slot_fetch(i):
            g, which = divmod(i, 2)
            _, idx_made, _ = tables["keys"]
            after = [idx_made, edges_padded] + ([tables["float", i - 4]] if i >= 4 else [])
            tables["got", i] = pool.dma(d_raw[i % 4], lambda e: e.indirect_dma_start(
                out=raw_idx[:, i % 4, :], out_offset=None, in_=(src_pad, dst_pad)[which],
                in_offset=bass.IndirectOffsetOnAxis(ap=edge_tile_i[:, g:g + 1], axis=0)), after)

        def slot_table(i):
            g, which = divmod(i, 2)
            _, _, base_made = tables["keys"]
            after = [tables["got", i]] + ([tables["turned", i - 2]] if i >= 2 else [])
            m = dve.do(lambda e: e.tensor_copy(raw_f[:, which, :], raw_idx[:, i % 4, :]), after)
            tables["float", i] = m
            if which:
                m = dve.do(lambda e: e.tensor_scalar(raw_f[:, which, :], raw_f[:, which, :], slot_base[:, g:g + 1], None,
                                                     ALU.subtract), [m, base_made])
            tables["turned", i] = pe.do(lambda e: e.transpose(bank[SLOT_TURN[which]][:, 0:P], raw_f[:, which, :],
                                                              ident[:, :]),
                                        [m, c_ident, tables["keys"][0], tables["keys"][2]] + ([tables["kept", i - 2]] if i >= 2 else []))

        def slot_keep(i):
            g, which = divmod(i, 2)
            to = (src_slot, dst_slot)[which]
            tables["kept", i] = dve.do(lambda e: e.tensor_copy(to[:, g * P:(g + 1) * P],
                                                               bank[SLOT_TURN[which]][:, 0:P]),
                                       [tables["turned", i]])

        assert NT % 2 == 1 and x_ring % 2 == 0
        AHEAD_X = 4
        for n in range(0, AHEAD_X, 2):
            s1_load(pair_of(n))
        for n in range(NT + 4):
            if n % 2 == 0 and n + AHEAD_X < NT:
                s1_load(pair_of(n + AHEAD_X))
            if 5 <= n < 5 + SLOT_GROUPS:
                slot_count(n - 5)
            if n == 5 + SLOT_GROUPS:
                slot_sums()
            if n == 8 + SLOT_GROUPS:
                slot_keys()
            for first_turn, step in ((16, slot_fetch), (19, slot_table), (20, slot_keep)):
                if first_turn <= n < first_turn + 2 * SLOT_GROUPS:
                    step(n - first_turn)
            if n < NT:
                s1_stats(n)
            if 2 <= n <= NT + 1:
                s1_norm(n - 2)
                s1_resid(n - 2)
                s1_turn(n - 2)
            if 3 <= n <= NT + 2:
                s1_product(n - 3)
            if 4 <= n:
                s1_keep(n - 4)
                if n % 2 or n - 4 == NT - 1:
                    s1_store(pair_of(n - 5 if n % 2 else n - 4))
        spare_zero = write_blanks()
        m = pe.do(lambda e: e.transpose(bank[6][:, 0:VECS], vec_rows[0:VECS, :], ident[0:VECS, 0:VECS]),
                  [d_vec.mark(), c_ident, tables["keys"][0]])
        vecs_turned = dve.do(lambda e: e.tensor_copy(vecs[:, :], bank[6][:, 0:VECS]), [m])
        table_written = d_t.mark()
        slots_ready = tables["kept", 2 * SLOT_GROUPS - 1]
        rows_ready = acc_copied[NT - 1]
        row_made = tables["keys"][0]

        ends_found = dve.do(lambda e: e.tensor_reduce(max_src[:, 0, :], acc[:, 0:NT, D:ROW].rearrange("p n h -> p h n"),
                                                      AX.X, ALU.max), [rows_ready[0]])
        m = dve.do(lambda e: e.tensor_reduce(max_src[:, 1, :], acc[:, 0:NT, D:ROW].rearrange("p n h -> p h n"),
                                             AX.X, ALU.min), [rows_ready[0]])
        m = dve.do(lambda e: e.tensor_single_scalar(max_src[:, 1, :], max_src[:, 1, :], -1.0, ALU.mult), [m])
        all_max = pool.do(lambda e: e.partition_all_reduce(
            max_all[:, :, :].rearrange("p a h -> p (a h)"), max_src[:, :, :].rearrange("p a h -> p (a h)"), P,
            bass.bass_isa.ReduceOp.max), [m, ends_found])
        shift_ap = pick[:, 0:NT, HEADS:PICK]
        a_dst_ap = pick[:, 0:NT, 0:HEADS]
        m = dve.do(lambda e: e.tensor_tensor(src_range[:, :], max_all[:, 0, :], max_all[:, 1, :], ALU.add), [all_max])
        k = dve.do(lambda e: e.tensor_tensor(own[:, :, :], a_dst_ap, max_all[:, 0:1, :].broadcast_to([P, NT, HEADS]),
                                             ALU.add), [all_max, rows_ready[1]])
        m = dve.do(lambda e: e.tensor_reduce(wide[:, 0:1], src_range[:, :], AX.X, ALU.max), [m])
        m = dve.do(lambda e: e.tensor_single_scalar(wide[:, 1:2], wide[:, 0:1], SAFE_RANGE, ALU.is_gt), [m])
        bound_made = dve.do(lambda e: e.scalar_tensor_tensor(shift_ap, own[:, :, :], NEG_SLOPE, own[:, :, :],
                                                             ALU.mult, ALU.max), [k])
        wide_known = dve.do(lambda e: e.tensor_copy(wide_flag[:, :], wide[:, 1:2]), [m])

        m_sems = {n: sem("max_" + n) for n in ("table", "free", "loads", "gathered", "turned", "scanned", "back", "ready",
                                               "scattered", "fetched", "passed")}
        M_LOADS = 5

        def general_path(body):
            def go(e):
                with e.register("wide_flag") as flag:
                    e.reg_load(flag, wide_flag[0:1, 0:1])
                    with e.If_ne(flag, 0):
                        body(e)
            return go

        def max_loads(e):
            e.dma_start(segment_max[0:NT * P, :].rearrange("(n p) h -> p n h", p=P),
                        acc[:, 0:NT, D:ROW]).then_inc(m_sems["table"], 16)
            e.wait_ge(m_sems["table"], 16)
            e.sem_inc(m_sems["free"], 1)
            flat = dst_pad.rearrange("t p -> (t p)")
            with e.Fori(0, ET) as i:
                e.wait_ge(m_sems["free"], i + 1)
                for to, of in ((m_col[:, 0:1], src_pad[bass.ds(i, 1), :].rearrange("a p -> p a")),
                               (m_col[:, 1:2], dst_pad[bass.ds(i, 1), :].rearrange("a p -> p a")),
                               (m_col[:, 2:3], flat[bass.ds(i * P + 1, P)].rearrange("(p a) -> p a", a=1)),
                               (m_row[0:HEADS, 0, :], dst_pad[bass.ds(i, 1), :].broadcast_to([HEADS, P])),
                               (m_row[0:HEADS, 1, :],
                                flat[bass.ds(i * P + 1, P)].rearrange("(a p) -> a p", a=1).broadcast_to([HEADS, P]))):
                    e.dma_start(to, of, allow_slow_non_contiguous=True).then_inc(m_sems["loads"], 16)
            e.wait_ge(m_sems["free"], ET + 1)
            e.dma_start(m_table[:, :, :], segment_max[0:NT * P, :].rearrange("(n p) h -> p n h", p=P)
                        ).then_inc(m_sems["fetched"], 16)
            e.wait_ge(m_sems["fetched"], 16)

        def max_moves(e):
            with e.Fori(0, ET) as i:
                e.wait_ge(m_sems["loads"], (i + 1) * 16 * M_LOADS)
                e.sem_inc(m_sems["passed"], 1)
                e.indirect_dma_start(out=m_rows[:, :], out_offset=None, in_=node_table,
                                     in_offset=bass.IndirectOffsetOnAxis(ap=m_col[:, 0:1], axis=0)
                                     ).then_inc(m_sems["gathered"], 16)
                e.wait_ge(m_sems["ready"], i + 1)
                e.sem_inc(m_sems["passed"], 1)
                e.indirect_dma_start(out=segment_max, out_offset=bass.IndirectOffsetOnAxis(ap=m_to[:, 0:1], axis=0),
                                     in_=m_out[:, :], in_offset=None).then_inc(m_sems["scattered"], 16)
                e.wait_ge(m_sems["scattered"], (i + 1) * 16)
                e.sem_inc(m_sems["free"], 1)

        def max_turns(e):
            with e.Fori(0, ET) as i:
                e.wait_ge(m_sems["gathered"], (i + 1) * 16)
                e.sem_inc(m_sems["passed"], 1)
                e.transpose(bank[5][0:HEADS, 0:P], m_rows[:, D:ROW], ident[:, :]).then_inc(m_sems["turned"], 1)
                e.wait_ge(m_sems["scanned"], i + 1)
                e.sem_inc(m_sems["passed"], 1)
                e.transpose(bank[6][:, 0:HEADS], m_scan[0:HEADS, :], ident[0:HEADS, 0:HEADS]
                            ).then_inc(m_sems["back"], 1)

        def max_scans(e):
            e.memset(m_carry[0:HEADS, :], FAR_BELOW).then_inc(m_sems["order"], 1)
            e.memset(m_reset[0:HEADS, P:P + 1], 0.0).then_inc(m_sems["order"], 1)
            e.tensor_single_scalar(spare_row[:, :], part[:, :], float(NT * P), ALU.add).then_inc(m_sems["order"], 1)
            START, STEPS = 3, 12
            e.wait_ge(m_sems["order"], START)
            with e.Fori(0, ET) as i:
                done = [0]

                def step(made):
                    made.then_inc(m_sems["order"], 1)
                    done[0] += 1
                    e.wait_ge(m_sems["order"], i * STEPS + START + done[0])

                e.wait_ge(m_sems["loads"], (i + 1) * 16 * M_LOADS)
                step(e.tensor_copy(m_reset[0:HEADS, 0:1], m_reset[0:HEADS, P:P + 1]))
                step(e.tensor_copy(m_row_f[0:HEADS, :, :], m_row[0:HEADS, :, :]))
                step(e.tensor_tensor(m_reset[0:HEADS, 1:1 + P], m_row_f[0:HEADS, 0, :], m_row_f[0:HEADS, 1, :],
                                     ALU.not_equal))
                step(e.tensor_single_scalar(m_scan[0:HEADS, :], m_reset[0:HEADS, 0:P], FAR_BELOW, ALU.mult))
                step(e.tensor_copy(m_to_f[:, 0:2], m_col[:, 1:3]))
                step(e.tensor_tensor(m_to_f[:, 2:3], m_to_f[:, 0:1], m_to_f[:, 1:2], ALU.not_equal))
                step(e.scalar_tensor_tensor(m_to_f[:, 3:4], m_to_f[:, 0:1], spare_row[:, 0:1], m_to_f[:, 2:3],
                                            ALU.subtract, ALU.mult))
                step(e.tensor_tensor(m_to_f[:, 3:4], m_to_f[:, 3:4], spare_row[:, :], ALU.add))
                step(e.tensor_copy(m_to[:, 0:1], m_to_f[:, 3:4]))
                e.wait_ge(m_sems["turned"], i + 1)
                step(e.tensor_tensor_scan(m_scan[0:HEADS, :], m_scan[0:HEADS, :], bank[5][0:HEADS, 0:P],
                                          m_carry[0:HEADS, 0:1], ALU.add, ALU.max))
                step(e.tensor_copy(m_carry[0:HEADS, :], m_scan[0:HEADS, P - 1:P]))
                e.sem_inc(m_sems["scanned"], 1)
                e.wait_ge(m_sems["back"], i + 1)
                step(e.tensor_copy(m_out[:, :], bank[6][:, 0:HEADS]))
                e.sem_inc(m_sems["ready"], 1)
                assert done[0] == STEPS
            at = ET * STEPS + START
            e.wait_ge(m_sems["fetched"], 16)
            for made in (lambda: e.tensor_tensor(own2[:, :, :], m_table[:, :, :], acc[:, 0:NT, D:ROW], ALU.max),
                         lambda: e.tensor_tensor(own[:, :, :], a_dst_ap, own2[:, :, :], ALU.add),
                         lambda: e.scalar_tensor_tensor(shift_ap, own[:, :, :], NEG_SLOPE, own[:, :, :], ALU.mult,
                                                        ALU.max)):
                made().then_inc(m_sems["order"], 1)
                at += 1
                e.wait_ge(m_sems["order"], at)

        general_ready = [wide_known, bound_made, table_written, rows_ready[0], rows_ready[1], row_made, slots_ready,
                         edges_padded, c_ident]
        m_sems["order"] = sem("max_order")
        for stream, body in ((sp, max_loads), (pool, max_moves), (pe, max_turns), (dve, max_scans)):
            stream.quiet(general_path(body), general_ready)

        m = dve.do(lambda e: e.tensor_tensor(own2[:, :, :], a_dst_ap, acc[:, 0:NT, D:ROW], ALU.add), [rows_ready[1]])
        m = dve.do(lambda e: e.scalar_tensor_tensor(own[:, :, :], own2[:, :, :], NEG_SLOPE, own2[:, :, :],
                                                    ALU.mult, ALU.max), [m, bound_made])
        m = shift_made = dve.do(lambda e: e.tensor_tensor(own[:, :, :], own[:, :, :], shift_ap, ALU.subtract), [m])
        own_weight = act.do(lambda e: e.activation(acc[:, 0:NT, D:ROW], own[:, :, :], ACT.Exp), [m, table_written])
        for g in range(GROUPS):
            acc_started = dve.do(lambda e, g=g: e.tensor_tensor(
                acc[:, g * NG:(g + 1) * NG, 0:D].rearrange("p n (h d) -> p n h d", d=DH),
                acc[:, g * NG:(g + 1) * NG, 0:D].rearrange("p n (h d) -> p n h d", d=DH),
                acc[:, g * NG:(g + 1) * NG, D:ROW].rearrange("p n (h a) -> p n h a", a=1)
                .broadcast_to([P, NG, HEADS, DH]), ALU.mult), [own_weight, table_written])

        TOP_EXP = 14
        SX, SW1, SH, SW2 = range(4)

        def powers(which, bound, after):
            c = slice(0, bound.shape[1])
            return powers_at(which, c, bound, after)

        def powers_at(which, c, bound, after):
            ex_, sc_, un_ = (t[:, which, c] for t in (exponent, scale, unscale))
            m = dve.do(lambda e: e.tensor_single_scalar(ex_.bitcast(F32), bound, 1e-30, ALU.max), after)
            m = dve.do(lambda e: e.tensor_single_scalar(ex_, ex_, 23, ALU.arith_shift_right), [m])
            k = dve.do(lambda e: e.tensor_scalar(sc_, ex_, -1, 254 + TOP_EXP, ALU.mult, ALU.add), [m])
            m = dve.do(lambda e: e.tensor_single_scalar(un_, ex_, -TOP_EXP, ALU.add), [m])
            k = dve.do(lambda e: e.tensor_single_scalar(sc_, sc_, 23, ALU.arith_shift_left), [k])
            return dve.do(lambda e: e.tensor_single_scalar(un_, un_, 23, ALU.arith_shift_left), [m, k])

        def scale_of(which, ee):
            return scale[:, which, ee:ee + 1].bitcast(F32)

        d_w1 = dma_marker("w1_loaded")
        w1_free = [acc_started, own_weight, all_max, edges_padded, resid_made[NT - 1],
                   slots_ready] + [r.mark() for r in d_r]
        w1_state = {}
        HALF = HID // 2

        def w1_steps(ee):
            w = w1_state
            w["loaded"] = sp.dma(d_w1, lambda e: e.dma_start(w1_stage[:, :, :], W1[ee].rearrange("(k p) h -> p k h", p=P)),
                                 w1_free + ([w["lo"], w["hi"]] if ee else []))
            yield
            for k in range(KD):
                if k:
                    yield
                w["max"] = dve.do(lambda e, k=k: e.tensor_reduce(piece_max[:, k:k + 1], w1_stage[:, k, :], AX.X, ALU.max,
                                                                 apply_absolute_value=True), [w["loaded"]])
            w["max"] = dve.do(lambda e: e.tensor_reduce(w_max[:, 0, ee:ee + 1], piece_max[:, 0:KD], AX.X, ALU.max),
                              [w["max"]])
            for _ in range(2):
                yield
            w["top"] = pool.do(lambda e: e.partition_all_reduce(w_top[:, 0, ee:ee + 1], w_max[:, 0, ee:ee + 1], P,
                                                                bass.bass_isa.ReduceOp.max), [w["max"]])
            w["scaled"] = powers_at(SW1, slice(ee, ee + 1), w_top[:, 0, ee:ee + 1], [w["top"]])
            for k in range(KD):
                for h in range(2):
                    hs = slice(h * HALF, (h + 1) * HALF)
                    w["hi"] = act.do(lambda e, k=k, hs=hs: e.activation(
                        w1_hi[:, k, ee, hs], w1_stage[:, k, hs], ACT.Copy, scale=scale_of(SW1, ee)), [w["scaled"]])
                    yield
                    w["lo"] = dve.do(lambda e, k=k, hs=hs: e.scalar_tensor_tensor(
                        w1_lo[:, k, ee, hs], w1_stage[:, k, hs], scale_of(SW1, ee), w1_hi[:, k, ee, hs], ALU.mult,
                        ALU.subtract), [w["hi"]])

        def vector_steps():
            for i, (at, n) in enumerate(((NE * KH, KD), (NE * (KH + KD), KD), (0, KH))):
                m = dve.do(lambda e, i=i, at=at, n=n: e.tensor_reduce(
                    vec_max[:, i, :], vecs[:, at:at + NE * n].rearrange("p (x c) -> p x c", c=n), AX.X, ALU.max,
                    apply_absolute_value=True), [vecs_turned])
            for _ in range(GB + 1):
                yield
            w1_state["vectors"] = pool.do(lambda e: e.partition_all_reduce(
                vec_top[:, :, :].rearrange("p i x -> p (i x)"), vec_max[:, :, :].rearrange("p i x -> p (i x)"), P,
                bass.bass_isa.ReduceOp.max), [m])
            yield

        def weight_steps():
            yield from vector_steps()
            for ee in range(NE):
                yield from w1_steps(ee)

        d_g = [[dma_marker(f"gathered{b}_{j}") for j in range(EB)] for b in range(GB)]
        OHT, AGG = (0, 1), (3, 4, 5, 6)
        PICKS = (2, 7)
        gat, oh, ohT, ohTc, pk, zz, wgt, msg, agg, added = ({} for _ in range(10))

        def e_gather(b):
            for j in range(EB):
                s = b * EB + j
                after = [slots_ready, table_written]
                if b >= GB:
                    after.append(agg[b - GB, EB - 1])
                else:
                    after.append(row_made)
                gat[b, j] = pool.dma(d_g[b % GB][j], lambda e, s=s, j=j: e.indirect_dma_start(
                    out=gather_ring[:, b % GB, j, :], out_offset=None, in_=node_table,
                    in_offset=bass.IndirectOffsetOnAxis(ap=src_slot[:, s:s + 1], axis=0)), after)

        def e_onehot(b, j):
            s = b * EB + j
            after = [slots_ready] + ([agg[b - OHB, EB - 1]] if b >= OHB else [])
            oh[b, j] = dve.do(lambda e: e.tensor_scalar(onehot[:, b % OHB, j, :], iota_free[:, :],
                                                        dst_slot[:, s:s + 1], None, ALU.is_equal), after)

        def e_turn(b):
            for h in range(2):
                after = [ohTc[b - 1, h]] if b >= 1 else list(acc_copied[NT - 1]) + [slots_ready]
                for j in range(4 * h, 4 * h + 4):
                    ohT[b, h] = pe.do(lambda e, j=j, h=h: e.transpose(
                        bank[OHT[h]][:, (j % 4) * P:(j % 4 + 1) * P], onehot[:, b % OHB, j, :], ident[:, :]),
                        after + [oh[b, j]])
                ohTc[b, h] = act.do(lambda e, h=h: e.activation(
                    onehotT[:, 0, 4 * h:4 * h + 4, :].rearrange("p j m -> p (j m)"), bank[OHT[h]][:, :], ACT.Copy),
                    [ohT[b, h]] + ([pk[b - 1]] if b >= 1 else []))

        reg = {}

        def load_tiles(stream, name, b):
            def go(e):
                _, values = nc.values_load_multi_w_load_instructions(
                    node_tile_row[0:1, b * EB:(b + 1) * EB], engines=[e.engine], min_val=0, max_val=NT,
                    skip_runtime_bounds_check_because=IN_RANGE)
                reg[name, b] = values
            stream.quiet(go, [row_made])

        def e_pick(b):
            load_tiles(pe, "pe", b)
            for j in range(EB):
                after = [ohTc[b, j // 4], shift_made] + ([zz[b - 2]] if b >= 2 else [])
                at = j * PICK
                pk[b] = pe.do(lambda e, j=j, at=at: e.matmul(
                    bank[PICKS[b % 2]][:, at:at + PICK], onehotT[:, 0, j, :],
                    pick[:, bass.ds(reg["pe", b][j], 1), :], start=True, stop=True), after)

        def picked(b, lo):
            return bank[PICKS[b % 2]][:, 0:EB * PICK].rearrange("p (j c) -> p j c", c=PICK)[:, :, lo:lo + HEADS]

        def e_z(b):
            return dve.do(lambda e: e.tensor_tensor(zbuf[:, 0, :, :], gather_ring[:, b % GB, :, D:ROW], picked(b, 0),
                                                    ALU.add), [gat[b, j] for j in range(EB)] + [pk[b]])

        def e_leaky(b, m):
            return dve.do(lambda e: e.scalar_tensor_tensor(zbuf[:, 1, :, :], zbuf[:, 0, :, :], NEG_SLOPE,
                                                           zbuf[:, 0, :, :], ALU.mult, ALU.max),
                          [m] + ([wgt[b - 1]] if b >= 1 else []))

        def e_shift(b, m):
            zz[b] = dve.do(lambda e: e.tensor_tensor(zbuf[:, 1, :, :], zbuf[:, 1, :, :], picked(b, HEADS),
                                                     ALU.subtract), [m])
            return zz[b]

        def e_bound(b, m):
            return dve.do(lambda e: e.tensor_single_scalar(zbuf[:, 1, :, :], zbuf[:, 1, :, :], 0.0, ALU.min), [m])

        def e_weight(b, m):
            wgt[b] = act.do(lambda e: e.activation(gather_ring[:, b % GB, :, D:ROW], zbuf[:, 1, :, :], ACT.Exp), [m])

        def e_message(b):
            v = lambda: gather_ring[:, b % GB, :, 0:D].rearrange("p j (h d) -> p j h d", d=DH)
            msg[b] = dve.do(lambda e: e.tensor_tensor(
                v(), v(), gather_ring[:, b % GB, :, D:ROW].rearrange("p j (h a) -> p j h a", a=1)
                .broadcast_to([P, EB, HEADS, DH]), ALU.mult), [wgt[b]])

        def e_sum(b):
            for j in range(EB):
                s = b * EB + j
                after = [msg[b], wgt[b], oh[b, j]]
                if s >= len(AGG):
                    after.append(lambda s=s: added[s - len(AGG)])
                agg[b, j] = pe.do(lambda e, s=s, j=j: e.matmul(
                    bank[AGG[s % len(AGG)]][:, 0:ROW], onehot[:, b % OHB, j, :], gather_ring[:, b % GB, j, :],
                    start=True, stop=True), after)

        def e_add(b, j):
            s = b * EB + j
            after = [agg[b, j], acc_started] + ([added[s - 1]] if s else [])

            def go(e):
                a = acc[:, bass.ds(reg["dve", b][j], 1), :]
                return e.tensor_tensor(a, a, bank[AGG[s % len(AGG)]][:, 0:ROW].rearrange("p (a c) -> p a c", a=1), ALU.add)
            added[s] = dve.do(go, after)

        for j in range(EB):
            e_onehot(0, j)
        e_turn(0)
        e_pick(0)
        weight_work = weight_steps()
        for b in range(BATCHES + 1):
            now, nxt = b < BATCHES, b + 1 < BATCHES
            next(weight_work, None)
            if b:
                load_tiles(dve, "dve", b - 1)
            if now:
                e_gather(b)
                m = e_z(b)
            for j in range(EB):
                if nxt:
                    e_onehot(b + 1, j)
                if now and j in (0, 1, 2):
                    m = (e_leaky, e_shift, e_bound)[j](b, m)
                    if j == 2:
                        e_weight(b, m)
                if b:
                    e_add(b - 1, j)
            if now:
                e_message(b)
            if nxt:
                e_turn(b + 1)
                e_pick(b + 1)
            if now:
                e_sum(b)
        edges_done = added[SLOTS - 1]
        for _ in weight_work:
            pass
        m = dve.do(lambda e: e.scalar_tensor_tensor(x_bound[:, :], vec_top[:, 0, :], float(np.sqrt(D)), vec_top[:, 1, :],
                                                    ALU.mult, ALU.add), [w1_state["vectors"]])
        k = dve.do(lambda e: e.scalar_tensor_tensor(h_bound[:, :], x_bound[:, :], float(D), w_top[:, 0, :], ALU.mult,
                                                    ALU.mult), [m, w1_state["top"]])
        k = dve.do(lambda e: e.tensor_tensor(h_bound[:, :], h_bound[:, :], vec_top[:, 2, :], ALU.add), [k])
        m = powers(SX, x_bound[:, :], [m])
        k = powers(SH, h_bound[:, :], [k])

        def across(ap, n):
            return ap.bitcast(F32).rearrange("p (x a) -> p x a", a=1).broadcast_to([P, NE, n])

        for at, col_, n in ((NE * KH, G_COL, KD), (NE * (KH + KD), LB_COL, KD)):
            m = dve.do(lambda e, at=at, col_=col_, n=n: e.tensor_tensor(
                expert_cols[:, :, col_:col_ + n], vecs[:, at:at + NE * n].rearrange("p (x c) -> p x c", c=n),
                across(scale[:, SX, :], n), ALU.mult), [m])
        m = dve.do(lambda e: e.tensor_copy(expert_cols[:, :, B1_COL:B1_COL + KH],
                                           vecs[:, 0:NE * KH].rearrange("p (x c) -> p x c", c=KH)), [m])
        m = dve.do(lambda e: e.tensor_tensor(expert_cols[:, :, PRE_COL:PRE_COL + 1], across(unscale[:, SX, :], 1),
                                             across(unscale[:, SW1, :], 1), ALU.mult), [m, w1_state["scaled"]])
        cols_made = dve.do(lambda e: e.tensor_copy(expert_cols[:, :, HS_COL:HS_COL + 1], across(scale[:, SH, :], 1)),
                           [m, k])

        ring_free = [edges_done, agg[BATCHES - 1, EB - 1], wgt[BATCHES - 1]]
        d_c = dma_marker("stage3_rows")
        for to, of in ((bias_row, bias), (gamma_row, gamma)):
            act.dma(d_c, lambda e, to=to, of=of: e.dma_start(to, of.rearrange("(a n) -> a n", a=1).broadcast_to([P, D])),
                    ring_free)
        act.dma(d_c, lambda e: e.dma_start(wr[:, :, :], Wr.rearrange("(k p) n -> p k n", p=P)), ring_free)
        act.dma(d_c, lambda e: e.dma_start(br_row[:, :], br.rearrange("(a n) -> a n", a=1).broadcast_to([P, NE])),
                ring_free)
        c_rows = d_c.mark()

        def tiles(g):
            return slice(g * NG, (g + 1) * NG)

        m = dve.do(lambda e: e.reciprocal(acc[:, 0:NT, D:ROW], acc[:, 0:NT, D:ROW]), [edges_done])
        summed = None
        for g in range(GROUPS):
            v = lambda g=g: acc[:, tiles(g), 0:D].rearrange("p n (h d) -> p n h d", d=DH)
            a = dve.do(lambda e, g=g, v=v: e.tensor_tensor(v(), v(), acc[:, tiles(g), D:ROW].rearrange(
                "p n (h a) -> p n h a", a=1).broadcast_to([P, NG, HEADS, DH]), ALU.mult), [m])
            for n in range(g * NG, (g + 1) * NG):
                r = rows_of(n)
                summed = pe.do(lambda e, n=n, r=r: e.matmul(bank[7][:, 0:D], ones[0:r, :], acc[0:r, n, 0:D],
                                                            start=(n == 0), stop=(n == NT - 1)), [a])
        m = dve.do(lambda e: e.scalar_tensor_tensor(mean_row, bank[7][:, 0:D], 1.0 / N, bias_row, ALU.mult, ALU.add),
                   [summed, c_rows])
        mean_made = dve.do(lambda e: e.tensor_tensor(mean_row, bias_row, mean_row, ALU.subtract), [m])
        sq, sq_used = {}, {}
        for g in range(GROUPS):
            a = dve.do(lambda e, g=g: e.tensor_tensor(
                acc[:, tiles(g), 0:D], acc[:, tiles(g), 0:D],
                mean_row.rearrange("p (a d) -> p a d", a=1).broadcast_to([P, NG, D]), ALU.add), [mean_made, summed])
            sq[g] = act.do(lambda e, g=g: e.activation(square[:, g % 2, :, :], acc[:, tiles(g), 0:D], ACT.Square),
                           [a] + ([sq_used[g - 2]] if g >= 2 else ring_free))
            for n in range(g * NG, (g + 1) * NG):
                r = rows_of(n)
                sq_used[g] = pe.do(lambda e, n=n, g=g, r=r: e.matmul(
                    bank[6][:, 0:D], ones[0:r, :], square[0:r, g % 2, n % NG, :],
                    start=(n == 0), stop=(n == NT - 1)), [sq[g]])
        centred = a
        m = act.do(lambda e: e.activation(sd_row, bank[6][:, 0:D], ACT.Sqrt, bias=eps[:, :], scale=1.0 / N),
                   [sq_used[GROUPS - 1]])
        m = dve.do(lambda e: e.reciprocal(scale_row, sd_row), [m])
        scale_made = dve.do(lambda e: e.tensor_tensor(scale_row, scale_row, gamma_row, ALU.mult), [m, c_rows])

        d_ri = [dma_marker(f"resid_loaded{i}") for i in range(2)]
        d_o = dma_marker("out_started")
        xf_made, xf_turned, xfT_made, lg_done, row_ready = {}, {}, {}, {}, {}
        r_loaded, x1_made, rs_done = {}, {}, {}

        def resid_load(g):
            r_loaded[g] = sp.dma(d_ri[g % 2], lambda e: e.dma_start(
                r_ring[:, g % 2, :, :], resid_rows[g * NG * P:(g + 1) * NG * P, :].rearrange("(n p) d -> p n d", p=P)),
                ring_free + [r.mark() for r in d_r] + ([x1_made[g - 2]] if g >= 2 else []))

        def x1_stage(g):
            t = tiles(g)
            a = dve.do(lambda e: e.tensor_tensor(acc[:, t, 0:D], acc[:, t, 0:D],
                                                 scale_row.rearrange("p (a d) -> p a d", a=1).broadcast_to([P, NG, D]),
                                                 ALU.mult), [scale_made, sq[GROUPS - 1]])
            yield
            a = x1_made[g] = dve.do(lambda e: e.tensor_tensor(acc[:, t, 0:D], acc[:, t, 0:D],
                                                              r_ring[:, g % 2, :, :], ALU.add), [a, r_loaded[g]])
            for n in range(g * NG, (g + 1) * NG):
                sp.dma(d_o, lambda e, n=n: e.dma_start(out[n * P:n * P + rows_of(n), :], acc[0:rows_of(n), n, 0:D]), [a])
            x1_stored[g] = d_o.mark()
            for i in range(NG):
                yield
                b = dve.do(lambda e, i=i: e.bn_stats(bn6[:, i, :], acc[:, g * NG + i, 0:D]), [a])
            for i in range(NG):
                yield
                b = dve.do(lambda e, i=i: e.bn_aggr(mv[:, g * NG + i, :], bn6[:, i, :]), [b])
            var = mv[:, t, 1:2].rearrange("p n a -> p (n a)")
            m = act.do(lambda e: e.activation(sd1[:, t], var, ACT.Sqrt, bias=eps[:, :]), [b])
            yield
            m = dve.do(lambda e: e.reciprocal(rs1[:, t], sd1[:, t]), [m])
            yield
            m = dve.do(lambda e: e.tensor_tensor(v2[:, t], var, rs1[:, t], ALU.mult), [m])
            yield
            m = dve.do(lambda e: e.tensor_tensor(v2[:, t], v2[:, t], rs1[:, t], ALU.mult), [m])
            m = act.do(lambda e: e.activation(sd2[:, t], v2[:, t], ACT.Sqrt, bias=eps[:, :]), [m])
            yield
            rs_done[g] = dve.do(lambda e: e.reciprocal(rs2[:, t], sd2[:, t]), [m])
            for n in range(g * NG, (g + 1) * NG + LATER):
                yield
                if n < (g + 1) * NG:
                    xf_stage(n)
                if n - LATER >= g * NG:
                    logits(n - LATER)

        def xf_stage(n):
            q, g = n % FR, n // NG
            after = [rs_done[g]] + ([xf_turned[n - FR], row_ready[n - FR]] if n >= FR else [])
            xf_made[n] = dve.do(lambda e: e.tensor_scalar(xf[:, q, :], acc[:, n, 0:D], mv[:, n, 0:1], rs1[:, n:n + 1],
                                                          ALU.subtract, ALU.mult), after)
            for k in range(KD):
                xf_turned[n] = pe.do(lambda e, k=k: e.transpose(bank[q][:, k * P:(k + 1) * P],
                                                                xf[:, q, k * P:(k + 1) * P], ident[:, :]),
                                     [xf_made[n]] + ([xfT_made[n - FR]] if n >= FR else []))
            xfT_made[n] = act.do(lambda e: e.activation(xfT[:, q, :, :].rearrange("p k m -> p (k m)"), bank[q][:, 0:D],
                                                        ACT.Copy), [xf_turned[n]] + ([lg_done[n - FR]] if n >= FR else []))
            row_ready[n] = act.do(lambda e: e.activation(acc[:, n, 0:D], xf[:, q, :], ACT.Copy, scale=rs2[:, n:n + 1]),
                                  [xf_made[n], x1_stored[g]])

        LATER = 2

        def logits(n):
            q, g = n % FR, n // NG
            for k in range(KD):
                lg_done[n] = pe.do(lambda e, k=k: e.matmul(
                    bank[LG[g % 2]][:, (n % NG) * NE:(n % NG + 1) * NE], xfT[:, q, k, :], wr[:, k, :],
                    start=(k == 0), stop=(k == KD - 1)),
                    [xfT_made[n], c_rows, scale_made] + ([lg_read[g - 2]] if g >= 2 else []))

        x1_stored, lg_read, rank_read, tot_read = {}, {}, {}, {}
        LG, RANK, TOT = (4, 5), 6, 7
        c_e = pool.do(lambda e: e.iota(iota_e[:, :, :], [[0, NT], [1, NE]], base=0, channel_multiplier=0,
                                       allow_small_or_imprecise_dtypes=True), ring_free)
        c_tok = pool.do(lambda e: e.iota(tok[:, :], [[P, NT]], base=0, channel_multiplier=1,
                                         allow_small_or_imprecise_dtypes=True), ring_free)
        c_ti = pool.do(lambda e: e.iota(tile_iota[:, :], [[P, FT]], base=0, channel_multiplier=0,
                                        allow_small_or_imprecise_dtypes=True), ring_free)
        c_re = pool.do(lambda e: e.iota(region_e[:, :], [[REGION, NE]], base=0, channel_multiplier=0,
                                        allow_small_or_imprecise_dtypes=True), ring_free)
        c_valid = dve.do(lambda e: e.tensor_single_scalar(valid[:, :], tok[:, :], float(N), ALU.is_lt), [c_tok])
        c_below = dve.do(lambda e: e.tensor_scalar(below[:, :], iota_free[:, :], part[:, 0:1], None, ALU.is_gt),
                         ring_free)
        c_or = dve.do(lambda e: e.memset(ones_row[:, :], 1.0), ring_free)

        def tt(o, a, b, op, after):
            return dve.do(lambda e: e.tensor_tensor(o, a, b, op), after)

        def reduce_e(o, a, op, after):
            return dve.do(lambda e: e.tensor_reduce(o, a, AX.X, op), after)

        d_s = dma_marker("dispatched")

        def route(g):
            t = tiles(g)

            def per_tile(ap):
                return ap.rearrange("p (n a) -> p n a", a=1).broadcast_to([P, NG, NE])

            def per_expert(ap):
                return ap.rearrange("p (a h) -> p a h", a=1).broadcast_to([P, NG, NE])

            L3, P3, Q3, C3, IE = (z[:, t, :] for z in (lg, prob, eq, chosen, iota_e))
            TP = [top[:, i, t] for i in range(6)]
            last = g * NG + NG - 1
            m = lg_read[g] = tt(L3, bank[LG[g % 2]][:, 0:NG * NE].rearrange("p (n a) -> p n a", a=NE),
                                per_expert(br_row[:, :]), ALU.add, [lg_done[last], c_rows])
            yield
            m = reduce_e(TP[0], L3, ALU.max, [m])
            yield
            m = tt(L3, L3, per_tile(TP[0]), ALU.subtract, [m])
            m = act.do(lambda e: e.activation(P3, L3, ACT.Exp), [m])
            yield
            m = reduce_e(TP[1], P3, ALU.add, [m])
            yield
            m = dve.do(lambda e: e.reciprocal(TP[1], TP[1]), [m])
            yield
            m = tt(P3, P3, per_tile(TP[1]), ALU.mult, [m])
            for c in range(TOP):
                F3 = first[:, c, t, :]
                yield
                m = reduce_e(TP[2 + c], P3, ALU.max, [m])
                yield
                m = tt(Q3, P3, per_tile(TP[2 + c]), ALU.is_equal, [m])
                yield
                m = dve.do(lambda e, F3=F3: e.scalar_tensor_tensor(F3, IE, float(NE), Q3, ALU.subtract, ALU.mult),
                           [m, c_e])
                yield
                m = reduce_e(TP[4], F3, ALU.min, [m])
                yield
                m = dve.do(lambda e: e.tensor_single_scalar(TP[4], TP[4], float(NE), ALU.add), [m])
                if c == 0:
                    yield
                    m = dve.do(lambda e: e.tensor_copy(acc[:, t, FIRST_COL:FIRST_COL + 1].rearrange("p n a -> p (n a)"),
                                                       TP[4]), [m])
                yield
                m = tt(F3, IE, per_tile(TP[4]), ALU.is_equal, [m])
                if c == 0:
                    yield
                    m = dve.do(lambda e, F3=F3: e.scalar_tensor_tensor(P3, F3, -2.0, P3, ALU.mult, ALU.add), [m])
            yield
            k = tt(C3, first[:, 0, t, :], first[:, 1, t, :], ALU.add, [m])
            yield
            k = tt(C3, C3, per_tile(valid[:, t]), ALU.mult, [k, c_valid])
            flat = chosen[:, t, :].rearrange("p n a -> p (n a)")
            rank_done = pe.do(lambda e: e.matmul(bank[RANK][:, 0:NG * NE], below[:, :], flat, start=True, stop=True),
                              [k, c_below, scale_made] + ([rank_read[g - 1]] if g else []))
            tot_done = pe.do(lambda e: e.matmul(bank[TOT][:, 0:NG * NE], ones[:, :], flat, start=True, stop=True),
                             [k] + ([tot_read[g - 1]] if g else []))
            yield
            m = tt(TP[5], TP[2], TP[3], ALU.add, [m])
            yield
            m = dve.do(lambda e: e.reciprocal(TP[5], TP[5]), [m])
            for c in range(TOP):
                yield
                w = tt(acc[:, t, W_COL + c:W_COL + c + 1].rearrange("p n a -> p (n a)"), TP[2 + c], TP[5], ALU.mult, [m])
            yield
            w = dve.do(lambda e: e.tensor_copy(acc[:, t, TOKEN_COL:TOKEN_COL + 1].rearrange("p n a -> p (n a)"),
                                               tok[:, t]), [w, c_tok])
            yield
            m = tot_read[g] = dve.do(lambda e: e.tensor_copy(totals[:, t, :].rearrange("p n a -> p (n a)"),
                                                             bank[TOT][:, 0:NG * NE]), [tot_done])
            for ee in range(NE):
                before = upto[:, g * NG - 1, ee:ee + 1] if g else 0.0
                if ee % 2 == 0:
                    yield
                mm = dve.do(lambda e, ee=ee, before=before: e.tensor_tensor_scan(
                    upto[:, t, ee:ee + 1].rearrange("p n a -> p (n a)"), ones_row[:, 0:NG],
                    totals[:, t, ee:ee + 1].rearrange("p n a -> p (n a)"), before, ALU.mult, ALU.add),
                    [m, c_or] + ([counted[g - 1]] if g else []))
            counted[g] = mm
            PL = place[:, t, :]
            yield
            m = tt(PL, upto[:, t, :], totals[:, t, :], ALU.subtract, [mm])
            yield
            m = rank_read[g] = tt(PL, PL, bank[RANK][:, 0:NG * NE].rearrange("p (n a) -> p n a", a=NE), ALU.add,
                                  [m, rank_done])
            yield
            m = tt(PL, PL, per_expert(region_e[:, :]), ALU.add, [m, c_re])
            for c in range(TOP):
                yield
                m = tt(Q3, PL, first[:, c, t, :], ALU.mult, [m])
                yield
                m = reduce_e(TP[c], Q3, ALU.add, [m])
                yield
                m = dve.do(lambda e, c=c: e.tensor_copy(row_of[:, c, t], TP[c]), [m])
                for n in range(g * NG, (g + 1) * NG):
                    r = rows_of(n)
                    pool.dma(d_s, lambda e, n=n, c=c, r=r: e.indirect_dma_start(
                        out=expert_rows, out_offset=bass.IndirectOffsetOnAxis(ap=row_of[0:r, c, n:n + 1], axis=0),
                        in_=acc[0:r, n, 0:XROW], in_offset=None), [m, w, row_ready[n]])

        counted = {}

        def alternate(*makers):
            live = list(makers)
            while live:
                for one in list(live):
                    if next(one, live) is live:
                        live.remove(one)

        d_w2 = [dma_marker(f"w2_loaded{i}") for i in range(4)]
        w2_loaded, w2_top, w2_scaled, w2_hi_made, w2_lo_made = ({} for _ in range(5))

        def w2_raw(ee):
            return (w2_stage_a, w2_stage_b)[ee % 4 // 2][:, ee % 2, :, :]

        def w2_load(ee, after):
            w2_loaded[ee] = sp.dma(d_w2[ee % 4], lambda e: e.dma_start(
                w2_raw(ee), W2[ee].rearrange("(c p) d -> p c d", p=P)),
                after + ([w2_lo_made[ee - 4], w2_hi_made[ee - 4]] if ee >= 4 else []))

        def w2_measure(ee):
            m = dve.do(lambda e: e.tensor_reduce(w_max[:, 1, ee:ee + 1], w2_raw(ee).rearrange("p c d -> p (c d)"), AX.X,
                                                 ALU.max, apply_absolute_value=True), [w2_loaded[ee]])
            w2_top[ee] = pool.do(lambda e: e.partition_all_reduce(w_top[:, 1, ee:ee + 1], w_max[:, 1, ee:ee + 1], P,
                                                                  bass.bass_isa.ReduceOp.max), [m])

        def w2_power(ee):
            w2_scaled[ee] = powers_at(SW2, slice(ee, ee + 1), w_top[:, 1, ee:ee + 1], [w2_top[ee]])

        def w2_split_hi(ee):
            w2_hi_made[ee] = act.do(lambda e: e.activation(
                w2_hi[:, ee, :, :], w2_raw(ee), ACT.Copy, scale=scale_of(SW2, ee)), [w2_scaled[ee], experts_known])

        def w2_split_lo(ee):
            w2_lo_made[ee] = dve.do(lambda e: e.scalar_tensor_tensor(
                w2_lo[:, ee, :, :], w2_raw(ee), scale_of(SW2, ee), w2_hi[:, ee, :, :], ALU.mult,
                ALU.subtract), [w2_hi_made[ee]])

        for g in range(GROUPS + 1):
            if g < GROUPS:
                resid_load(g)
            if g < 2:
                w2_load(g, ring_free)
            if g in (2, 3):
                w2_measure(g - 2)
            if g in (3, 4):
                w2_power(g - 3)
            alternate(*([x1_stage(g)] if g < GROUPS else []), *([route(g - 1)] if g else []))
        mm = counted[GROUPS - 1]

        count = upto[:, NT - 1, :]
        m = dve.do(lambda e: e.tensor_single_scalar(ex[:, 0, :], count, float(P - 1), ALU.add), [mm])
        m = dve.do(lambda e: e.tensor_copy(ex_i[:, 0, :], ex[:, 0, :]), [m])
        m = dve.do(lambda e: e.tensor_single_scalar(ex_i[:, 1, :], ex_i[:, 0, :], 7, ALU.arith_shift_right), [m])
        m = dve.do(lambda e: e.tensor_copy(ex[:, 1, :], ex_i[:, 1, :]), [m])
        blank_known = tt(blank_row[:, :], count, region_e[:, :], ALU.add, [mm, c_re])
        ends = dve.do(lambda e: e.tensor_tensor_scan(ex[:, 2, :], ones_row[:, 0:NE], ex[:, 1, :], 0.0, ALU.mult,
                                                     ALU.add), [m])
        m = dve.do(lambda e: e.tensor_scalar(ex[:, 3, :], ex[:, 1, :], -float(P), float(REGION), ALU.mult, ALU.add), [ends])
        m = dve.do(lambda e: e.tensor_single_scalar(ex[:, 2, :], ex[:, 2, :], float(P), ALU.mult), [m])
        m = tt(cmp_e[:, :, :], tile_iota[:, :].rearrange("p (s a) -> p s a", a=1).broadcast_to([P, FT, NE]),
               ex[:, 2, :].rearrange("p (a h) -> p a h", a=1).broadcast_to([P, FT, NE]), ALU.is_ge, [m, c_ti, xf_turned[NT - 1], row_ready[NT - 1]])
        k = reduce_e(tile_e[:, :], cmp_e[:, :, :], ALU.add, [m])
        k = dve.do(lambda e: e.tensor_single_scalar(expert_of_tile_f[:, :], tile_e[:, :], float(NE - 1), ALU.min), [k])
        k = dve.do(lambda e: e.tensor_copy(expert_of_tile[:, :], expert_of_tile_f[:, :]), [k])
        m = tt(cmp_e[:, :, :], cmp_e[:, :, :], ex[:, 3, :].rearrange("p (a h) -> p a h", a=1)
               .broadcast_to([P, FT, NE]), ALU.mult, [k])
        m = reduce_e(tile_e[:, :], cmp_e[:, :, :], ALU.add, [m])
        experts_known = tt(row_of_tile[:, :], tile_e[:, :], tile_iota[:, :], ALU.add, [m])
        d_tail = dma_marker("region_tails_blanked")
        for ee in range(NE):
            def load_blank(e, ee=ee):
                _, values = nc.values_load_multi_w_load_instructions(
                    blank_row[0:1, ee:ee + 1], engines=[e.engine], min_val=ee * REGION, max_val=ee * REGION + N,
                    skip_runtime_bounds_check_because=IN_RANGE)
                reg["blank", ee] = values[0]
            sp.quiet(load_blank, [blank_known])
            sp.dma(d_tail, lambda e, ee=ee: e.dma_start(expert_rows[bass.ds(reg["blank", ee], P), :], blank[:, :]),
                   [spare_zero])
        dispatched = [d_s.mark(), d_tail.mark(), d_blank.mark()]
        rank_done = rank_read[GROUPS - 1]

        d_b2 = dma_marker("b2_loaded")
        b2_ready = act.dma(d_b2, lambda e: e.dma_start(
            b2_all[:, :, :].rearrange("p e d -> p (e d)"),
            b2.rearrange("e d -> (e d)").rearrange("(a n) -> a n", a=1).broadcast_to([P, NE * D])), dispatched)

        w2_load(2, dispatched)
        w2_load(3, dispatched)
        w2_split_hi(0)
        w2_split_hi(1)
        for ee in range(NE):
            w2_split_lo(ee)
            if ee + 4 < NE:
                w2_load(ee + 4, [])
            if 0 < ee < NE - 1:
                w2_power(ee + 1)
                w2_split_hi(ee + 1)
            if ee + 2 < NE:
                w2_measure(ee + 2)
        w2_ready = w2_lo_made[NE - 1]
        cols_made = dve.do(lambda e: e.tensor_tensor(expert_cols[:, :, Y_COL:Y_COL + 1], across(unscale[:, SH, :], 1),
                                                     across(unscale[:, SW2, :], 1), ALU.mult),
                           [cols_made, w2_scaled[NE - 1]])

        d_xs = [dma_marker(f"expert_rows_loaded{i}") for i in range(XR)]
        d_y = dma_marker("out_added")
        XT, HB, YB = (0, 5), (1, 2, 3, 4), (6, 7)
        loaded, gone, gate_made, cols_now, turned, xe_made, xe_hi_made, xe_split = ({} for _ in range(8))
        h_done, h_act, h_hi_made, h_split, y_done, y_made, y_sent, ereg = ({} for _ in range(8))
        EL = 4

        def expert_regs(stream, name, s):
            if s % EL == 0:
                def go(e):
                    hi = min(s + EL, FT)
                    _, values = nc.values_load_multi_w_load_instructions(
                        expert_of_tile[0:1, s:hi], engines=[e.engine], min_val=0, max_val=NE - 1,
                        skip_runtime_bounds_check_because=IN_RANGE)
                    for i in range(s, hi):
                        ereg[name, i] = values[i - s]
                stream.quiet(go, [experts_known])

        def f_load(s):
            after = dispatched + ([y_made[s - XR], turned[s - XR]] if s >= XR else [])
            if s % EL == 0:
                def go(e):
                    hi = min(s + EL, FT)
                    _, values = nc.values_load_multi_w_load_instructions(
                        row_of_tile[0:1, s:hi], engines=[e.engine], min_val=0, max_val=NE * REGION + (SPARE_TILES - 1) * P,
                        skip_runtime_bounds_check_because=IN_RANGE)
                    for i in range(s, hi):
                        ereg["row", i] = values[i - s]
                sp.quiet(go, [experts_known])
            loaded[s] = sp.dma(d_xs[s % XR], lambda e: e.dma_start(
                xs[:, s % XR, :], expert_rows[bass.ds(ereg["row", s], P), :]), after)

        def col(s, c):
            return cols[:, s % CR, c:c + 1]

        def f_columns(s):
            expert_regs(dve, "dve", s)
            cols_now[s] = dve.do(lambda e: e.tensor_copy(
                cols[:, s % CR, :].rearrange("p (a c) -> p a c", a=1), expert_cols[:, bass.ds(ereg["dve", s], 1), :]),
                [cols_made] + dispatched + ([y_made[s - CR], h_act[s - CR, 1]] if s >= CR else []))
            gone[s] = dve.do(lambda e: e.tensor_copy(token_id[:, s % XR:s % XR + 1],
                                                     xs[:, s % XR, TOKEN_COL:TOKEN_COL + 1]),
                             [loaded[s]] + ([y_sent[s - XR]] if s >= XR else []))
            for c, op in enumerate((ALU.is_equal, ALU.not_equal)):
                made = dve.do(lambda e, c=c, op=op: e.tensor_scalar(
                    gate[:, s % XR, c:c + 1], xs[:, s % XR, FIRST_COL:FIRST_COL + 1], expert_of_tile_f[:, s:s + 1],
                    xs[:, s % XR, W_COL + c:W_COL + c + 1], op, ALU.mult),
                    [loaded[s], experts_known] + ([y_made[s - XR]] if s >= XR else []))
            gate_made[s] = dve.do(lambda e: e.tensor_tensor(gate[:, s % XR, 2:3], gate[:, s % XR, 0:1],
                                                            gate[:, s % XR, 1:2], ALU.add), [made])

        def f_turn(s):
            q = s % 2
            for k in range(KD):
                turned[s] = pe.do(lambda e, k=k: e.transpose(bank[XT[q]][:, k * P:(k + 1) * P],
                                                             xs[:, s % XR, k * P:(k + 1) * P], ident[:, :]),
                                  [loaded[s]] + ([xe_made[s - 2]] if s >= 2 else [rank_done, experts_known]))
            for k in range(KD):
                xe_made[s] = act.do(lambda e, k=k: e.activation(
                    xe[:, q, k, :], bank[XT[q]][:, k * P:(k + 1) * P], ACT.Identity, bias=col(s, LB_COL + k),
                    scale=col(s, G_COL + k)), [turned[s], cols_now[s]] + ([xe_split[s - 2]] if s >= 2 else []))

        def f_split_input(s):
            q = s % 2
            xe_hi_made[s] = dve.do(lambda e: e.tensor_copy(xe_hi[:, q, :, :], xe[:, q, :, :]),
                                   [xe_made[s]] + ([h_done[s - 2, 1]] if s >= 2 else []))
            xe_split[s] = dve.do(lambda e: e.tensor_tensor(xe_lo[:, q, :, :], xe[:, q, :, :], xe_hi[:, q, :, :],
                                                           ALU.subtract), [xe_hi_made[s]])

        def f_hidden(s):
            q = s % 2
            expert_regs(pe, "pe", s)
            for h in range(2):
                i = 2 * s + h
                bk = bank[HB[i % 4]]
                for c in range(KH // 2):
                    at = (h * KH // 2 + c) * P
                    parts = [(w, k, x_) for k in range(KD) for w, x_ in ((w1_hi, xe_hi), (w1_hi, xe_lo), (w1_lo, xe_hi))]
                    for n, (w, k, x_) in enumerate(parts):
                        h_done[s, h] = pe.do(lambda e, w=w, k=k, x_=x_, n=n, c=c, at=at, bk=bk: e.matmul(
                            bk[:, c * P:(c + 1) * P],
                            w[:, k, bass.ds(ereg["pe", s], 1), at:at + P].rearrange("p a m -> p (a m)"),
                            x_[:, q, k, :], start=(n == 0), stop=(n == len(parts) - 1)),
                            [xe_split[s], w1_ready] + ([h_act[(i - 4) // 2, h]] if i >= 4 else []))
                for c in range(KH // 2):
                    h_act[s, h] = act.do(lambda e, i=i, c=c, h=h, bk=bk: e.activation(
                        hid[:, i % HR, c, :], bk[:, c * P:(c + 1) * P], ACT.Gelu, bias=col(s, B1_COL + h * KH // 2 + c),
                        scale=col(s, PRE_COL)),
                        [h_done[s, h]] + ([h_split[(i - HR) // 2, (i - HR) % 2]] if i >= HR else []))

        def f_split_hidden(s, h):
            q, i = s % 2, 2 * s + h
            cs = slice(h * KH // 2, (h + 1) * KH // 2)
            h_hi_made[s, h] = dve.do(lambda e: e.tensor_scalar(hid_hi[:, q, cs, :], hid[:, i % HR, :, :], col(s, HS_COL),
                                                               None, ALU.mult),
                                     [h_act[s, h]] + ([y_done[s - 2]] if s >= 2 else []))
            h_split[s, h] = dve.do(lambda e: e.scalar_tensor_tensor(
                hid_lo[:, q, cs, :], hid[:, i % HR, :, :], col(s, HS_COL), hid_hi[:, q, cs, :], ALU.mult, ALU.subtract),
                [h_hi_made[s, h]])

        def f_output(s):
            q = s % 2
            parts = [(c, a, b) for c in range(KH) for a, b in ((hid_hi, w2_hi), (hid_hi, w2_lo), (hid_lo, w2_hi))]
            for n, (c, a, b) in enumerate(parts):
                y_done[s] = pe.do(lambda e, c=c, a=a, b=b, n=n: e.matmul(
                    bank[YB[q]][:, 0:D], a[:, q, c, :], b[:, bass.ds(ereg["pe", s], 1), c, :],
                    start=(n == 0), stop=(n == len(parts) - 1)),
                    [h_split[s, 2 * c // KH], w2_ready] + ([y_made[s - 2]] if s >= 2 else []))

        def f_finish(s):
            q = s % 2
            m = dve.do(lambda e: e.scalar_tensor_tensor(
                y[:, q, :].rearrange("p (a d) -> p a d", a=1),
                bank[YB[q]][:, 0:D].rearrange("p (a d) -> p a d", a=1), col(s, Y_COL),
                b2_all[:, bass.ds(ereg["dve", s], 1), :], ALU.mult, ALU.add),
                [y_done[s], b2_ready] + ([y_sent[s - 2]] if s >= 2 else []))
            y_made[s] = dve.do(lambda e: e.tensor_scalar(y[:, q, :], y[:, q, :], gate[:, s % XR, 2:3], None, ALU.mult),
                               [m, gate_made[s]])
            y_sent[s] = pool.dma(d_y, lambda e: e.indirect_dma_start(
                out=out, out_offset=bass.IndirectOffsetOnAxis(ap=token_id[:, s % XR:s % XR + 1], axis=0),
                in_=y[:, q, :], in_offset=None, compute_op=ALU.add),
                [y_made[s], gone[s], d_o.mark(), spare_zero] + ([y_sent[s - 1]] if s else []))

        w1_ready = w1_state["lo"]
        AHEAD = 3
        for s in range(AHEAD):
            f_load(s)
        for s in range(2):
            f_columns(s)
        f_turn(0)
        f_split_input(0)
        for s in range(FT + 1):
            if s + AHEAD < FT:
                f_load(s + AHEAD)
            if s + 1 < FT:
                f_turn(s + 1)
                f_split_input(s + 1)
            if s < FT:
                f_hidden(s)
                f_split_hidden(s, 0)
                f_split_hidden(s, 1)
            if s:
                f_output(s - 1)
                f_finish(s - 1)
            if s + 2 < FT:
                f_columns(s + 2)

        sp.quiet(lambda e: None, [m_.mark() for m_ in dmas if m_.count])

        block = ctx.enter_context(nc.Block())

        @block.sync
        def _(e):
            sp.play(e)

        @block.gpsimd
        def _(e):
            pool.play(e)

        @block.scalar
        def _(e):
            act.play(e)

        @block.vector
        def _(e):
            dve.play(e)

        @block.tensor
        def _(e):
            pe.play(e)


INPUTS = ["x", "src", "dst", "L0_gnn_W", "L0_gnn_att_src", "L0_gnn_att_dst", "L0_gnn_bias", "L0_gnn_gamma",
          "L0_gnn_beta", "L0_ffn_Wr", "L0_ffn_br", "L0_ffn_ln_g", "L0_ffn_ln_b", "L0_ffn_W1", "L0_ffn_b1",
          "L0_ffn_W2", "L0_ffn_b2"]


def kernel(**inputs):
    import numpy as _np
    import concourse.bacc as _bacc
    from concourse import mybir as _mybir
    from concourse.bass_utils import run_bass_kernel_spmd as _run

    nc = _bacc.Bacc("TRN2", target_bir_lowering=False, num_devices=1)
    arrays, args = {}, []
    for name in INPUTS:
        a = _np.ascontiguousarray(inputs[name])
        arrays[f"in_{name}"] = a
        args.append(nc.dram_tensor(f"in_{name}", a.shape, _mybir.dt.from_np(a.dtype), kind="ExternalInput").ap())
    n, d = inputs["x"].shape
    args.append(nc.dram_tensor("out_rows", (n + 128, d), _mybir.dt.float32, kind="ExternalOutput").ap())
    build_gnn_moe(nc, *args)
    r = _run(nc, [arrays], core_ids=[0])
    return r.results[0]["out_rows"][:n]
```
